# Optimizing a Trainium2 kernel written in Bass

```python
import numpy as np
import jax
import jax.numpy as jnp

def _softmax(x, axis=-1):
    return jax.nn.softmax(x, axis=axis)

def _gelu(x):
    return jax.nn.gelu(x, approximate=True)

def _silu(x):
    return jax.nn.silu(x)

def _sigmoid(x):
    return jax.nn.sigmoid(x)

def _layernorm(x, axis=-1, eps=1e-05):
    m = jnp.mean(x, axis=axis, keepdims=True)
    v = jnp.var(x, axis=axis, keepdims=True)
    return (x - m) / jnp.sqrt(v + eps)

def _scatter_add(tgt, idx, src, axis=0):
    return tgt.at[idx].add(src)

def _segment_sum(src, seg, n):
    return jax.ops.segment_sum(src, seg, n)
kernel_name = 'mk_xattn_ffn_d4_seqx_r4_ba49c8'

def setup_inputs(seed: int=0):
    np.random.seed(seed)
    _w = jnp.asarray

    def _rec_inputs():
        import jax
        import jax.numpy as jnp
        _rk = jax.random.key(seed)
        x = 0.002226 + 0.9996 * jax.random.normal(jax.random.fold_in(_rk, 1), (2, 1024, 256), jnp.float32)
        _lenS = 1024 - jax.random.randint(jax.random.fold_in(_rk, 7), (2,), 0, max(1, 1024 // 4) + 1, jnp.int32)
        _lenS2 = 77 - jax.random.randint(jax.random.fold_in(_rk, 8), (2,), 0, max(1, 77 // 4) + 1, jnp.int32)
        _ctx_1024P = jax.random.normal(jax.random.fold_in(_rk, 11), (2, 16, 256), jnp.float32)
        _ctx_1024c = jax.random.dirichlet(jax.random.fold_in(_rk, 511), 0.3 * jnp.ones((16,), jnp.float32), (2, 77))
        _ctx_1024t = jnp.einsum('bsk,bkd->bsd', _ctx_1024c, _ctx_1024P)
        _ctx_1024t = _ctx_1024t * jax.lax.rsqrt(jnp.mean(jnp.square(_ctx_1024t)) + 1e-12) * 0.953939
        ctx_1024 = -0.000125008 + 0.999885 * (_ctx_1024t + 0.3 * jax.random.normal(jax.random.fold_in(_rk, 611), (2, 77, 256), jnp.float32))
        return (x, ctx_1024)
    x, ctx_1024 = _rec_inputs()

    def _L0_xattn_setup():
        import jax, jax.numpy as jnp
        import numpy as np
        DIM = 256
        HEADS = 16
        DIM_HEAD = 64
        INNER = HEADS * DIM_HEAD
        EPS = 1e-05

        def _layernorm(x, w, b):
            m = jnp.mean(x, axis=-1, keepdims=True)
            v = jnp.mean(jnp.square(x - m), axis=-1, keepdims=True)
            return (x - m) * jax.lax.rsqrt(v + EPS) * w + b
        key = jax.random.key(seed)
        ks = jax.random.split(key, 9)
        B, N, L = (8, 1024, 64)
        x = jax.random.normal(ks[0], (B, N, DIM), dtype=jnp.float32)
        latents = jax.random.normal(ks[1], (B, L, DIM), dtype=jnp.float32)
        s = 1.0 / np.sqrt(DIM)
        Wq = jax.random.normal(ks[2], (DIM, INNER), dtype=jnp.float32) * s
        Wkv = jax.random.normal(ks[3], (DIM, 2 * INNER), dtype=jnp.float32) * s
        Wo = jax.random.normal(ks[4], (INNER, DIM), dtype=jnp.float32) * (1.0 / np.sqrt(INNER))
        ln1_w = jnp.ones((DIM,), jnp.float32)
        ln1_b = jnp.zeros((DIM,), jnp.float32)
        ln2_w = jnp.ones((DIM,), jnp.float32)
        ln2_b = jnp.zeros((DIM,), jnp.float32)
        return {'x': x, 'latents': latents, 'Wq': Wq, 'Wkv': Wkv, 'Wo': Wo, 'ln1_w': ln1_w, 'ln1_b': ln1_b, 'ln2_w': ln2_w, 'ln2_b': ln2_b}
    _L0_xattn_all = _L0_xattn_setup()
    _L0_xattn_in = {k: v for k, v in _L0_xattn_all.items() if k in ('Wq', 'Wkv', 'Wo', 'ln1_w', 'ln1_b', 'ln2_w', 'ln2_b')}
    del _L0_xattn_all

    def _L0_ffn_setup():
        import jax, jax.numpy as jnp
        import numpy as np
        H = 256
        I = 256
        E = 8
        key = jax.random.key(seed)
        ks = jax.random.split(key, 8)
        s = 0.02
        x = jax.random.normal(ks[0], (4, 512, H), dtype=jnp.float32)
        Wg = jax.random.normal(ks[1], (H, E), dtype=jnp.float32) * s
        bg = jnp.zeros((E,), dtype=jnp.float32)
        W1 = jax.random.normal(ks[2], (E, H, I), dtype=jnp.float32) * s
        b1 = jnp.zeros((E, I), dtype=jnp.float32)
        W2 = jax.random.normal(ks[3], (E, I, H), dtype=jnp.float32) * s
        b2 = jnp.zeros((E, H), dtype=jnp.float32)
        return {'x': x, 'Wg': Wg, 'bg': bg, 'W1': W1, 'b1': b1, 'W2': W2, 'b2': b2}
    _L0_ffn_all = _L0_ffn_setup()
    _L0_ffn_in = {k: v for k, v in _L0_ffn_all.items() if k in ('Wg', 'bg', 'W1', 'b1', 'W2', 'b2')}
    del _L0_ffn_all

    def _L1_xattn_setup():
        import jax, jax.numpy as jnp
        import numpy as np
        N_EMBD = 256
        N_HEAD = 16
        key = jax.random.key(seed)
        ks = jax.random.split(key, 8)
        C = N_EMBD
        s = 1.0 / np.sqrt(C)
        return {'x': jax.random.normal(ks[0], (8, 256, C), jnp.float32), 'encoder_output': jax.random.normal(ks[1], (8, 144, C), jnp.float32), 'Wq': jax.random.normal(ks[2], (C, C), jnp.float32) * s, 'bq': jnp.zeros((C,), jnp.float32), 'Wkv': jax.random.normal(ks[3], (2 * C, C), jnp.float32) * s, 'bkv': jnp.zeros((2 * C,), jnp.float32), 'Wo': jax.random.normal(ks[4], (C, C), jnp.float32) * s, 'bo': jnp.zeros((C,), jnp.float32)}
    _L1_xattn_all = _L1_xattn_setup()
    _L1_xattn_in = {k: v for k, v in _L1_xattn_all.items() if k in ('Wq', 'bq', 'Wkv', 'bkv', 'Wo', 'bo')}
    del _L1_xattn_all

    def _L1_ffn_setup():
        import jax, jax.numpy as jnp
        import numpy as np
        B, T, D, E, FF, K = (4, 256, 256, 8, 512, 2)
        SINKHORN_ITERS = 3

        def _sinkhorn(log_alpha, iters=SINKHORN_ITERS):
            for _ in range(iters):
                log_alpha = log_alpha - jax.nn.logsumexp(log_alpha, axis=-1, keepdims=True)
                log_alpha = log_alpha - jax.nn.logsumexp(log_alpha, axis=-2, keepdims=True)
            gates = jnp.exp(log_alpha)
            return gates / (jnp.sum(gates, axis=-1, keepdims=True) + 1e-08)
        key = jax.random.key(seed)
        ks = jax.random.split(key, 7)
        scale = 0.02
        return {'x': jax.random.normal(ks[0], (B, T, D), dtype=jnp.float32), 'router_w': jax.random.normal(ks[1], (E, D), dtype=jnp.float32) * scale, 'router_b': jnp.zeros((E,), dtype=jnp.float32), 'temperature': jnp.ones((1,), dtype=jnp.float32) * 0.5, 'wg': jax.random.normal(ks[2], (E, D, FF), dtype=jnp.float32) * scale, 'wp': jax.random.normal(ks[3], (E, D, FF), dtype=jnp.float32) * scale, 'wo': jax.random.normal(ks[4], (E, FF, D), dtype=jnp.float32) * scale}
    _L1_ffn_all = _L1_ffn_setup()
    _L1_ffn_in = {k: v for k, v in _L1_ffn_all.items() if k in ('router_w', 'router_b', 'temperature', 'wg', 'wp', 'wo')}
    del _L1_ffn_all

    def _L2_xattn_setup():
        import jax, jax.numpy as jnp
        import numpy as np
        D_MODEL = 256
        NHEAD = 16
        D_K = D_MODEL // NHEAD
        key = jax.random.key(seed)
        ks = jax.random.split(key, 11)
        B, S = (4, 512)
        s = 1.0 / np.sqrt(D_MODEL)
        return {'query': jax.random.normal(ks[0], (B, S, D_MODEL), jnp.float32), 'key': jax.random.normal(ks[1], (B, S, D_MODEL), jnp.float32), 'value': jax.random.normal(ks[2], (B, S, D_MODEL), jnp.float32), 'wq': jax.random.normal(ks[3], (D_MODEL, D_MODEL), jnp.float32) * s, 'bq': jnp.zeros((D_MODEL,), jnp.float32), 'wk': jax.random.normal(ks[4], (D_MODEL, D_MODEL), jnp.float32) * s, 'bk': jnp.zeros((D_MODEL,), jnp.float32), 'wv': jax.random.normal(ks[5], (D_MODEL, D_MODEL), jnp.float32) * s, 'bv': jnp.zeros((D_MODEL,), jnp.float32), 'wo': jax.random.normal(ks[6], (D_MODEL, D_MODEL), jnp.float32) * s, 'bo': jnp.zeros((D_MODEL,), jnp.float32)}
    _L2_xattn_all = _L2_xattn_setup()
    _L2_xattn_in = {k: v for k, v in _L2_xattn_all.items() if k in ('wq', 'bq', 'wk', 'bk', 'wv', 'bv', 'wo', 'bo')}
    del _L2_xattn_all

    def _L2_ffn_setup():
        import jax, jax.numpy as jnp
        import numpy as np
        EPS = 1e-05
        TOP_K = 2

        def _rmsnorm(x, w):
            xf = x.astype(jnp.float32)
            rms = jax.lax.rsqrt(jnp.mean(xf * xf, axis=-1, keepdims=True) + EPS)
            return (xf * rms).astype(x.dtype) * w

        def _attention(x, wq, wk, wv, wo, num_heads=16):
            B, S, H = x.shape
            D = H // num_heads
            q = (x @ wq.T).reshape(B, S, num_heads, D)
            k = (x @ wk.T).reshape(B, S, num_heads, D)
            v = (x @ wv.T).reshape(B, S, num_heads, D)
            scale = 1.0 / jnp.sqrt(jnp.float32(D)).astype(x.dtype)
            scores = jnp.einsum('bqhd,bkhd->bhqk', q, k) * scale
            probs = jax.nn.softmax(scores, axis=-1)
            out = jnp.einsum('bhqk,bkhd->bqhd', probs, v).reshape(B, S, H)
            return out @ wo.T

        def _moe(x, gate_w, w1, w2, w3):
            B, S, H = x.shape
            xf = x.reshape(-1, H)
            logits = xf @ gate_w.T
            rw, sel = jax.lax.top_k(logits, TOP_K)
            rw = jax.nn.softmax(rw.astype(jnp.float32), axis=-1).astype(x.dtype)
            E = gate_w.shape[0]
            out = jnp.zeros_like(xf)
            for e in range(E):
                we = jnp.sum(jnp.where(sel == e, rw, 0.0), axis=-1)
                h = jax.nn.silu(xf @ w1[e].T) * (xf @ w3[e].T)
                out = out + h @ w2[e].T * we[:, None]
            return out.reshape(B, S, H)
        key = jax.random.key(seed)
        ks = jax.random.split(key, 10)
        H, I, E, NH = (256, 512, 8, 16)
        B, S = (2, 512)
        s = 0.02
        return {'x': jax.random.normal(ks[0], (B, S, H), jnp.float32), 'ln1_w': jnp.ones((H,), jnp.float32), 'ln2_w': jnp.ones((H,), jnp.float32), 'wq': jax.random.normal(ks[1], (H, H), jnp.float32) * s, 'wk': jax.random.normal(ks[2], (H, H), jnp.float32) * s, 'wv': jax.random.normal(ks[3], (H, H), jnp.float32) * s, 'wo': jax.random.normal(ks[4], (H, H), jnp.float32) * s, 'gate_w': jax.random.normal(ks[5], (E, H), jnp.float32) * s, 'w1': jax.random.normal(ks[6], (E, I, H), jnp.float32) * s, 'w2': jax.random.normal(ks[7], (E, H, I), jnp.float32) * s, 'w3': jax.random.normal(ks[8], (E, I, H), jnp.float32) * s}
    _L2_ffn_all = _L2_ffn_setup()
    _L2_ffn_in = {k: v for k, v in _L2_ffn_all.items() if k in ('ln1_w', 'ln2_w', 'wq', 'wk', 'wv', 'wo', 'gate_w', 'w1', 'w2', 'w3')}
    del _L2_ffn_all

    def _L3_xattn_setup():
        import jax, jax.numpy as jnp
        import numpy as np
        from jax import lax
        BIG = jnp.float32(1e+30)

        def _pairwise_euclidean(a, b):
            aa = jnp.sum(a * a, axis=-1)[:, None]
            bb = jnp.sum(b * b, axis=-1)[None, :]
            ab = a @ b.T
            return jnp.sqrt(jnp.maximum(aa + bb - 2.0 * ab, 0.0))

        def _dtw_cost(D):
            row0 = jnp.cumsum(D[0])

            def row_step(prev_row, d_row):
                first = d_row[0] + prev_row[0]

                def col_step(left, inp):
                    d_ij, up, diag = inp
                    r = d_ij + jnp.minimum(jnp.minimum(up, left), diag)
                    return (r, r)
                _, rest = lax.scan(col_step, first, (d_row[1:], prev_row[1:], prev_row[:-1]))
                row = jnp.concatenate([first[None], rest])
                return (row, row)
            _, rows = lax.scan(row_step, row0, D[1:])
            return jnp.concatenate([row0[None], rows], axis=0)

        def _backtrack(R, T1, T2):
            L = T1 + T2 - 1

            def step(carry, _):
                i, j, done = carry
                valid = jnp.logical_not(done)
                cd = jnp.where((i > 0) & (j > 0), R[jnp.maximum(i - 1, 0), jnp.maximum(j - 1, 0)], BIG)
                cu = jnp.where(i > 0, R[jnp.maximum(i - 1, 0), j], BIG)
                cl = jnp.where(j > 0, R[i, jnp.maximum(j - 1, 0)], BIG)
                choice = jnp.argmin(jnp.stack([cd, cu, cl]))
                ni = jnp.where(choice <= 1, i - 1, i)
                nj = jnp.where((choice == 0) | (choice == 2), j - 1, j)
                at_origin = (i == 0) & (j == 0)
                ni = jnp.where(at_origin, 0, ni)
                nj = jnp.where(at_origin, 0, nj)
                return ((ni, nj, done | at_origin), (i, j, valid))
            init = (jnp.int32(T1 - 1), jnp.int32(T2 - 1), jnp.bool_(False))
            _, (i_idx, j_idx, valid) = lax.scan(step, init, None, length=L)
            return (i_idx, j_idx, valid)

        def _align_one(small, large):
            T_small, d = small.shape
            T_large = large.shape[0]
            D = _pairwise_euclidean(small, large)
            R = _dtw_cost(D)
            i_idx, j_idx, valid = _backtrack(R, T_small, T_large)
            contrib = small[i_idx] * valid[:, None].astype(small.dtype)
            expanded = jnp.zeros((T_large, d), dtype=small.dtype).at[j_idx].add(contrib)
            return expanded
        key = jax.random.key(seed)
        k1, k2 = jax.random.split(key)
        teacher = jax.random.normal(k1, (16, 100, 256), dtype=jnp.float32)
        student = jax.random.normal(k2, (16, 150, 256), dtype=jnp.float32)
        return {'teacher_features': teacher, 'student_features': student}
    _L3_xattn_all = _L3_xattn_setup()
    _L3_xattn_in = {k: v for k, v in _L3_xattn_all.items() if k in ()}
    del _L3_xattn_all

    def _L3_ffn_setup():
        import jax, jax.numpy as jnp
        import numpy as np
        B, M, D = (4, 512, 256)
        N, P = (64, 32)
        key = jax.random.key(seed)
        k1, k2, k3, k4 = jax.random.split(key, 4)
        x = jax.random.normal(k1, (B, M, D), dtype=jnp.float32)
        phi = jax.random.normal(k2, (D, N, P), dtype=jnp.float32) * (1.0 / np.sqrt(D))
        W = jax.random.normal(k3, (N, D, D), dtype=jnp.float32) * (1.0 / np.sqrt(D))
        b = jax.random.normal(k4, (N, D), dtype=jnp.float32) * 0.01
        return {'x': x, 'phi': phi, 'W': W, 'b': b}
    _L3_ffn_all = _L3_ffn_setup()
    _L3_ffn_in = {k: v for k, v in _L3_ffn_all.items() if k in ('phi', 'W', 'b')}
    del _L3_ffn_all
    return {'x': x, 'ctx_1024': ctx_1024, 'L0_xattn_Wq': _L0_xattn_in['Wq'], 'L0_xattn_Wkv': _L0_xattn_in['Wkv'], 'L0_xattn_Wo': _L0_xattn_in['Wo'], 'L0_xattn_ln1_w': _L0_xattn_in['ln1_w'], 'L0_xattn_ln1_b': _L0_xattn_in['ln1_b'], 'L0_xattn_ln2_w': _L0_xattn_in['ln2_w'], 'L0_xattn_ln2_b': _L0_xattn_in['ln2_b'], 'L0_ffn_Wg': _L0_ffn_in['Wg'], 'L0_ffn_bg': _L0_ffn_in['bg'], 'L0_ffn_W1': _L0_ffn_in['W1'], 'L0_ffn_b1': _L0_ffn_in['b1'], 'L0_ffn_W2': _L0_ffn_in['W2'], 'L0_ffn_b2': _L0_ffn_in['b2'], 'L1_xattn_Wq': _L1_xattn_in['Wq'], 'L1_xattn_bq': _L1_xattn_in['bq'], 'L1_xattn_Wkv': _L1_xattn_in['Wkv'], 'L1_xattn_bkv': _L1_xattn_in['bkv'], 'L1_xattn_Wo': _L1_xattn_in['Wo'], 'L1_xattn_bo': _L1_xattn_in['bo'], 'L1_ffn_router_w': _L1_ffn_in['router_w'], 'L1_ffn_router_b': _L1_ffn_in['router_b'], 'L1_ffn_temperature': _L1_ffn_in['temperature'], 'L1_ffn_wg': _L1_ffn_in['wg'], 'L1_ffn_wp': _L1_ffn_in['wp'], 'L1_ffn_wo': _L1_ffn_in['wo'], 'L2_xattn_wq': _L2_xattn_in['wq'], 'L2_xattn_bq': _L2_xattn_in['bq'], 'L2_xattn_wk': _L2_xattn_in['wk'], 'L2_xattn_bk': _L2_xattn_in['bk'], 'L2_xattn_wv': _L2_xattn_in['wv'], 'L2_xattn_bv': _L2_xattn_in['bv'], 'L2_xattn_wo': _L2_xattn_in['wo'], 'L2_xattn_bo': _L2_xattn_in['bo'], 'L2_ffn_ln1_w': _L2_ffn_in['ln1_w'], 'L2_ffn_ln2_w': _L2_ffn_in['ln2_w'], 'L2_ffn_wq': _L2_ffn_in['wq'], 'L2_ffn_wk': _L2_ffn_in['wk'], 'L2_ffn_wv': _L2_ffn_in['wv'], 'L2_ffn_wo': _L2_ffn_in['wo'], 'L2_ffn_gate_w': _L2_ffn_in['gate_w'], 'L2_ffn_w1': _L2_ffn_in['w1'], 'L2_ffn_w2': _L2_ffn_in['w2'], 'L2_ffn_w3': _L2_ffn_in['w3'], 'L3_ffn_phi': _L3_ffn_in['phi'], 'L3_ffn_W': _L3_ffn_in['W'], 'L3_ffn_b': _L3_ffn_in['b']}

def reference(x, ctx_1024, L0_xattn_Wq, L0_xattn_Wkv, L0_xattn_Wo, L0_xattn_ln1_w, L0_xattn_ln1_b, L0_xattn_ln2_w, L0_xattn_ln2_b, L0_ffn_Wg, L0_ffn_bg, L0_ffn_W1, L0_ffn_b1, L0_ffn_W2, L0_ffn_b2, L1_xattn_Wq, L1_xattn_bq, L1_xattn_Wkv, L1_xattn_bkv, L1_xattn_Wo, L1_xattn_bo, L1_ffn_router_w, L1_ffn_router_b, L1_ffn_temperature, L1_ffn_wg, L1_ffn_wp, L1_ffn_wo, L2_xattn_wq, L2_xattn_bq, L2_xattn_wk, L2_xattn_bk, L2_xattn_wv, L2_xattn_bv, L2_xattn_wo, L2_xattn_bo, L2_ffn_ln1_w, L2_ffn_ln2_w, L2_ffn_wq, L2_ffn_wk, L2_ffn_wv, L2_ffn_wo, L2_ffn_gate_w, L2_ffn_w1, L2_ffn_w2, L2_ffn_w3, L3_ffn_phi, L3_ffn_W, L3_ffn_b):
    import jax
    import jax.numpy as jnp

    def _L0_xattn_ref(x, latents, Wq, Wkv, Wo, ln1_w, ln1_b, ln2_w, ln2_b):
        import jax, jax.numpy as jnp
        import numpy as np
        DIM = 256
        HEADS = 16
        DIM_HEAD = 64
        INNER = HEADS * DIM_HEAD
        EPS = 1e-05

        def _layernorm(x, w, b):
            m = jnp.mean(x, axis=-1, keepdims=True)
            v = jnp.mean(jnp.square(x - m), axis=-1, keepdims=True)
            return (x - m) * jax.lax.rsqrt(v + EPS) * w + b
        B, L, _ = latents.shape
        xn = _layernorm(x, ln1_w, ln1_b)
        ln = _layernorm(latents, ln2_w, ln2_b)
        q = ln @ Wq
        kv_input = jnp.concatenate([xn, ln], axis=-2)
        kv = kv_input @ Wkv
        k, v = jnp.split(kv, 2, axis=-1)

        def heads(t):
            b, s, _ = t.shape
            return t.reshape(b, s, HEADS, DIM_HEAD).transpose(0, 2, 1, 3)
        q, k, v = (heads(q), heads(k), heads(v))
        scale = 1.0 / np.sqrt(np.sqrt(DIM_HEAD))
        logits = jnp.einsum('bhld,bhsd->bhls', q * scale, k * scale)
        w = jax.nn.softmax(logits.astype(jnp.float32), axis=-1).astype(logits.dtype)
        out = jnp.einsum('bhls,bhsd->bhld', w, v)
        out = out.transpose(0, 2, 1, 3).reshape(B, L, INNER)
        return out @ Wo

    def _L0_ffn_ref(x, Wg, bg, W1, b1, W2, b2):
        import jax, jax.numpy as jnp
        import numpy as np
        H = 256
        I = 256
        E = 8
        B, S, Hd = x.shape
        xf = x.reshape(-1, Hd)
        logits = xf @ Wg + bg
        gates = jax.nn.softmax(logits, axis=-1)
        idx = jnp.argmax(gates, axis=-1)
        h = jax.nn.gelu(jnp.einsum('th,ehi->tei', xf, W1) + b1, approximate=False)
        y = jnp.einsum('tei,eih->teh', h, W2) + b2
        out = jnp.take_along_axis(y, idx[:, None, None], axis=1)[:, 0, :]
        return out.reshape(B, S, Hd)

    def _L1_xattn_ref(x, encoder_output, Wq, bq, Wkv, bkv, Wo, bo):
        import jax, jax.numpy as jnp
        import numpy as np
        N_EMBD = 256
        N_HEAD = 16
        B, T, C = x.shape
        I = encoder_output.shape[1]
        H, D = (N_HEAD, C // N_HEAD)
        q = jnp.einsum('btc,oc->bto', x, Wq) + bq
        kv = jnp.einsum('bic,oc->bio', encoder_output, Wkv) + bkv
        k, v = (kv[..., :C], kv[..., C:])
        q = q.reshape(B, T, H, D).transpose(0, 2, 1, 3)
        k = k.reshape(B, I, H, D).transpose(0, 2, 1, 3)
        v = v.reshape(B, I, H, D).transpose(0, 2, 1, 3)
        att = jnp.einsum('bhtd,bhid->bhti', q, k) * (1.0 / np.sqrt(D))
        att = jax.nn.softmax(att, axis=-1)
        y = jnp.einsum('bhti,bhid->bhtd', att, v)
        y = y.transpose(0, 2, 1, 3).reshape(B, T, C)
        return jnp.einsum('btc,oc->bto', y, Wo) + bo

    def _L1_ffn_ref(x, router_w, router_b, temperature, wg, wp, wo):
        import jax, jax.numpy as jnp
        import numpy as np
        B, T, D, E, FF, K = (4, 256, 256, 8, 512, 2)
        SINKHORN_ITERS = 3

        def _sinkhorn(log_alpha, iters=SINKHORN_ITERS):
            for _ in range(iters):
                log_alpha = log_alpha - jax.nn.logsumexp(log_alpha, axis=-1, keepdims=True)
                log_alpha = log_alpha - jax.nn.logsumexp(log_alpha, axis=-2, keepdims=True)
            gates = jnp.exp(log_alpha)
            return gates / (jnp.sum(gates, axis=-1, keepdims=True) + 1e-08)
        temp = jnp.maximum(temperature, 0.1)
        scores = (jnp.einsum('btd,ed->bte', x, router_w) + router_b) / temp
        gates = _sinkhorn(scores)
        topk_vals, topk_idx = jax.lax.top_k(gates, K)
        topk_gates = topk_vals / (jnp.sum(topk_vals, axis=-1, keepdims=True) + 1e-08)
        g = jax.nn.relu(jnp.einsum('btd,edf->btef', x, wg))
        p = jnp.einsum('btd,edf->btef', x, wp)
        all_out = jnp.einsum('btef,efd->bted', g * p, wo)
        gathered = jnp.take_along_axis(all_out, topk_idx[..., None], axis=2)
        expert_out = jnp.sum(gathered * topk_gates[..., None], axis=2)
        return x + expert_out

    def _L2_xattn_ref(query, key, value, wq, bq, wk, bk, wv, bv, wo, bo):
        import jax, jax.numpy as jnp
        import numpy as np
        D_MODEL = 256
        NHEAD = 16
        D_K = D_MODEL // NHEAD
        B, Sq, _ = query.shape
        Sk = key.shape[1]
        scale = 1.0 / np.sqrt(D_K).astype(np.float32)
        Q = (query @ wq.T + bq).reshape(B, Sq, NHEAD, D_K).transpose(0, 2, 1, 3)
        K = (key @ wk.T + bk).reshape(B, Sk, NHEAD, D_K).transpose(0, 2, 1, 3)
        V = (value @ wv.T + bv).reshape(B, Sk, NHEAD, D_K).transpose(0, 2, 1, 3)
        scores = jnp.einsum('bhqd,bhkd->bhqk', Q, K) * scale
        attn = jax.nn.softmax(scores, axis=-1)
        ctx = jnp.einsum('bhqk,bhkd->bhqd', attn, V)
        ctx = ctx.transpose(0, 2, 1, 3).reshape(B, Sq, D_MODEL)
        return ctx @ wo.T + bo

    def _L2_ffn_ref(x, ln1_w, ln2_w, wq, wk, wv, wo, gate_w, w1, w2, w3):
        import jax, jax.numpy as jnp
        import numpy as np
        EPS = 1e-05
        TOP_K = 2

        def _rmsnorm(x, w):
            xf = x.astype(jnp.float32)
            rms = jax.lax.rsqrt(jnp.mean(xf * xf, axis=-1, keepdims=True) + EPS)
            return (xf * rms).astype(x.dtype) * w

        def _attention(x, wq, wk, wv, wo, num_heads=16):
            B, S, H = x.shape
            D = H // num_heads
            q = (x @ wq.T).reshape(B, S, num_heads, D)
            k = (x @ wk.T).reshape(B, S, num_heads, D)
            v = (x @ wv.T).reshape(B, S, num_heads, D)
            scale = 1.0 / jnp.sqrt(jnp.float32(D)).astype(x.dtype)
            scores = jnp.einsum('bqhd,bkhd->bhqk', q, k) * scale
            probs = jax.nn.softmax(scores, axis=-1)
            out = jnp.einsum('bhqk,bkhd->bqhd', probs, v).reshape(B, S, H)
            return out @ wo.T

        def _moe(x, gate_w, w1, w2, w3):
            B, S, H = x.shape
            xf = x.reshape(-1, H)
            logits = xf @ gate_w.T
            rw, sel = jax.lax.top_k(logits, TOP_K)
            rw = jax.nn.softmax(rw.astype(jnp.float32), axis=-1).astype(x.dtype)
            E = gate_w.shape[0]
            out = jnp.zeros_like(xf)
            for e in range(E):
                we = jnp.sum(jnp.where(sel == e, rw, 0.0), axis=-1)
                h = jax.nn.silu(xf @ w1[e].T) * (xf @ w3[e].T)
                out = out + h @ w2[e].T * we[:, None]
            return out.reshape(B, S, H)
        h = x + _attention(_rmsnorm(x, ln1_w), wq, wk, wv, wo)
        h = h + _moe(_rmsnorm(h, ln2_w), gate_w, w1, w2, w3)
        return h

    def _L3_xattn_ref(teacher_features, student_features):
        import jax, jax.numpy as jnp
        import numpy as np
        from jax import lax
        BIG = jnp.float32(1e+30)

        def _pairwise_euclidean(a, b):
            aa = jnp.sum(a * a, axis=-1)[:, None]
            bb = jnp.sum(b * b, axis=-1)[None, :]
            ab = a @ b.T
            return jnp.sqrt(jnp.maximum(aa + bb - 2.0 * ab, 0.0))

        def _dtw_cost(D):
            row0 = jnp.cumsum(D[0])

            def row_step(prev_row, d_row):
                first = d_row[0] + prev_row[0]

                def col_step(left, inp):
                    d_ij, up, diag = inp
                    r = d_ij + jnp.minimum(jnp.minimum(up, left), diag)
                    return (r, r)
                _, rest = lax.scan(col_step, first, (d_row[1:], prev_row[1:], prev_row[:-1]))
                row = jnp.concatenate([first[None], rest])
                return (row, row)
            _, rows = lax.scan(row_step, row0, D[1:])
            return jnp.concatenate([row0[None], rows], axis=0)

        def _backtrack(R, T1, T2):
            L = T1 + T2 - 1

            def step(carry, _):
                i, j, done = carry
                valid = jnp.logical_not(done)
                cd = jnp.where((i > 0) & (j > 0), R[jnp.maximum(i - 1, 0), jnp.maximum(j - 1, 0)], BIG)
                cu = jnp.where(i > 0, R[jnp.maximum(i - 1, 0), j], BIG)
                cl = jnp.where(j > 0, R[i, jnp.maximum(j - 1, 0)], BIG)
                choice = jnp.argmin(jnp.stack([cd, cu, cl]))
                ni = jnp.where(choice <= 1, i - 1, i)
                nj = jnp.where((choice == 0) | (choice == 2), j - 1, j)
                at_origin = (i == 0) & (j == 0)
                ni = jnp.where(at_origin, 0, ni)
                nj = jnp.where(at_origin, 0, nj)
                return ((ni, nj, done | at_origin), (i, j, valid))
            init = (jnp.int32(T1 - 1), jnp.int32(T2 - 1), jnp.bool_(False))
            _, (i_idx, j_idx, valid) = lax.scan(step, init, None, length=L)
            return (i_idx, j_idx, valid)

        def _align_one(small, large):
            T_small, d = small.shape
            T_large = large.shape[0]
            D = _pairwise_euclidean(small, large)
            R = _dtw_cost(D)
            i_idx, j_idx, valid = _backtrack(R, T_small, T_large)
            contrib = small[i_idx] * valid[:, None].astype(small.dtype)
            expanded = jnp.zeros((T_large, d), dtype=small.dtype).at[j_idx].add(contrib)
            return expanded
        return jax.vmap(_align_one)(teacher_features, student_features)

    def _L3_ffn_ref(x, phi, W, b):
        import jax, jax.numpy as jnp
        import numpy as np
        B, M, D = (4, 512, 256)
        N, P = (64, 32)
        logits = jnp.einsum('bmd,dnp->bmnp', x, phi)
        dispatch = jax.nn.softmax(logits, axis=0)
        bsz, m, n, p = logits.shape
        combine = jax.nn.softmax(logits.reshape(bsz, m, n * p), axis=-1).reshape(bsz, m, n, p)
        slots = jnp.einsum('bmd,bmnp->bnpd', x, dispatch)
        y = jnp.einsum('bnpd,nde->bnpe', slots, W) + b[None, :, None, :]
        out = jnp.einsum('bnpd,bmnp->bmd', y, combine)
        return out
    x = x + _L0_xattn_ref(ctx_1024, _layernorm(x, axis=-1), L0_xattn_Wq, L0_xattn_Wkv, L0_xattn_Wo, L0_xattn_ln1_w, L0_xattn_ln1_b, L0_xattn_ln2_w, L0_xattn_ln2_b)
    x = x + _L0_ffn_ref(_layernorm(x, axis=-1), L0_ffn_Wg, L0_ffn_bg, L0_ffn_W1, L0_ffn_b1, L0_ffn_W2, L0_ffn_b2)
    x = x + _L1_xattn_ref(_layernorm(x, axis=-1), ctx_1024, L1_xattn_Wq, L1_xattn_bq, L1_xattn_Wkv, L1_xattn_bkv, L1_xattn_Wo, L1_xattn_bo)
    x = x + _L1_ffn_ref(_layernorm(x, axis=-1), L1_ffn_router_w, L1_ffn_router_b, L1_ffn_temperature, L1_ffn_wg, L1_ffn_wp, L1_ffn_wo)
    x = x + _L2_xattn_ref(_layernorm(x, axis=-1), ctx_1024, ctx_1024, L2_xattn_wq, L2_xattn_bq, L2_xattn_wk, L2_xattn_bk, L2_xattn_wv, L2_xattn_bv, L2_xattn_wo, L2_xattn_bo)
    x = x + _L2_ffn_ref(_layernorm(x, axis=-1), L2_ffn_ln1_w, L2_ffn_ln2_w, L2_ffn_wq, L2_ffn_wk, L2_ffn_wv, L2_ffn_wo, L2_ffn_gate_w, L2_ffn_w1, L2_ffn_w2, L2_ffn_w3)
    x = x + _L3_xattn_ref(ctx_1024, _layernorm(x, axis=-1))
    x = x + _L3_ffn_ref(_layernorm(x, axis=-1), L3_ffn_phi, L3_ffn_W, L3_ffn_b)
    return x

_drawn_inputs = setup_inputs


def setup_inputs(seed=0):
    import zlib

    import numpy as np

    out = dict(_drawn_inputs(seed))
    spreads = {'L0_xattn_ln1_w': (1.0, 0.2),
     'L0_xattn_ln1_b': (0.0, 0.693),
     'L0_xattn_ln2_w': (1.0, 0.6),
     'L0_xattn_ln2_b': (0.0, 0.1),
     'L0_ffn_bg': (0.0, 0.269),
     'L0_ffn_b1': (0.0, 0.661),
     'L0_ffn_b2': (0.0, 0.1),
     'L1_xattn_bq': (0.0, 0.279),
     'L1_xattn_bkv': (0.0, 0.1),
     'L1_xattn_bo': (0.0, 0.1),
     'L1_ffn_router_b': (0.0, 0.8),
     'L2_xattn_bq': (0.0, 0.495),
     'L2_xattn_bk': (0.0, 0.8),
     'L2_xattn_bv': (0.0, 0.1),
     'L2_xattn_bo': (0.0, 0.1),
     'L2_ffn_ln1_w': (1.0, 0.6),
     'L2_ffn_ln2_w': (1.0, 0.6)}
    factors = {'L0_ffn_W1': 3.501,
     'L1_ffn_router_w': 8.0,
     'L1_ffn_wg': 8.0,
     'L1_ffn_wp': 8.0,
     'L1_ffn_wo': 8.0,
     'L2_ffn_wq': 8.0,
     'L2_ffn_wk': 8.0,
     'L2_ffn_gate_w': 8.0,
     'L2_ffn_w1': 8.0,
     'L2_ffn_w2': 8.0,
     'L2_ffn_w3': 8.0,
     'L3_ffn_b': 8.0}
    for name, (base, spread) in spreads.items():
        noise = np.random.default_rng([zlib.crc32(name.encode()), seed]).standard_normal(out[name].shape)
        drawn = base * np.exp(spread * noise) if base else spread * noise
        out[name] = jnp.asarray(drawn.astype(out[name].dtype))
    for name, factor in factors.items():
        out[name] = (out[name] * factor).astype(out[name].dtype)
    return out
```

```python
from contextlib import ExitStack

import concourse.bass as bass
from concourse import mybir

ALU = mybir.AluOpType
ACT = mybir.ActivationFunctionType
F32 = mybir.dt.float32
F32R = mybir.dt.float32r
F16 = mybir.dt.float16
AX = mybir.AxisListType

P = 128
B = 2
S = 1024
T = B * S
D = 256
C = D // P
CTX = 77
BLK = 512
NBLK = T // BLK
TILES = T // P
EPS = 1e-5
E = 8


class Scope:

    def __init__(self, nc, stack, stage):
        self.nc, self.stack, self.stage = nc, stack, stage
        self.semaphores = []
        stack.callback(self.clear)

    def clear(self):
        for s in self.semaphores:
            self.nc.gpsimd.sem_clear(s)

    def sb(self, name, shape, dt=F32):
        return self.stack.enter_context(self.nc.sbuf_tensor(f"{self.stage}_{name}", shape, dt))

    def psum(self, name="banks"):
        return self.stack.enter_context(self.nc.psum_tensor(f"{self.stage}_{name}", [P, 8, BLK], F32))

    def sem(self, name):
        self.semaphores.append(self.stack.enter_context(self.nc.semaphore(f"{self.stage}_{name}")))
        return self.semaphores[-1]


def load_stage(nc, stage, pairs):
    with ExitStack() as stack:
        loaded = Scope(nc, stack, stage).sem("loaded")
        with nc.Block() as block:
            @block.sync
            def _(sp):
                for dst, src in pairs:
                    sp.dma_start(dst, src).then_inc(loaded, 16)
                sp.wait_ge(loaded, 16 * len(pairs))


def norm_stage(nc, stage, consts, jobs):
    with ExitStack() as stack:
        sc = Scope(nc, stack, stage)
        centred = sc.sb("centred", [P, 2, C, BLK])
        squared = sc.sb("squared", [P, 2, C, BLK])
        logvar = sc.sb("logvar", [P, 2, BLK])
        rstd = sc.sb("rstd", [P, 2, BLK])
        ps = sc.psum()
        mean_ready, centred_ready, squared_ready = sc.sem("mean_ready"), sc.sem("centred_ready"), sc.sem("squared_ready")
        var_ready, log_ready, rstd_ready = sc.sem("var_ready"), sc.sem("log_ready"), sc.sem("rstd_ready")
        normed, scaled = sc.sem("normed"), sc.sem("scaled")
        affine = [n for n, job in enumerate(jobs) if job[5] is not None]
        with nc.Block() as block:
            @block.tensor
            def _(pe):
                def mean(n):
                    src, _, t0, w, rms, _, _ = jobs[n]
                    if n >= 2:
                        pe.wait_ge(centred_ready, n - 1)
                    if n < 2 or not rms:
                        pass
                    for c in range(C):
                        mm = pe.matmul(ps[:, n % 2, 0:w], consts["mean"][:, :], src[:, c, t0:t0 + w],
                                       start=c == 0, stop=c == C - 1)
                    mm.then_inc(mean_ready, 1)

                mean(0)
                for n, (_, _, _, w, _, _, _) in enumerate(jobs):
                    if n + 1 < len(jobs):
                        mean(n + 1)
                    pe.wait_ge(squared_ready, n + 1)
                    if n >= 2:
                        pe.wait_ge(log_ready, n - 1)
                    for c in range(C):
                        mm = pe.matmul(ps[:, 2 + n % 2, 0:w], consts["mean"][:, :], squared[:, n % 2, c, 0:w],
                                       start=c == 0, stop=c == C - 1)
                    mm.then_inc(var_ready, 1)

            @block.vector
            def _(dve):
                def centre(n):
                    src, _, t0, w, rms, _, _ = jobs[n]
                    if n >= 2:
                        dve.wait_ge(normed, n - 1)
                        dve.wait_ge(squared_ready, n - 1)
                    dve.wait_ge(mean_ready, n + 1)
                    if rms:
                        dve.tensor_copy(centred[:, n % 2, :, 0:w], src[:, :, t0:t0 + w]).then_inc(centred_ready, 1)
                    else:
                        dve.tensor_tensor(centred[:, n % 2, :, 0:w], src[:, :, t0:t0 + w],
                                          ps[:, n % 2, 0:w].unsqueeze(1).broadcast_to([P, C, w]),
                                          ALU.subtract).then_inc(centred_ready, 1)

                centre(0)
                for n, (_, dst, t0, w, _, scale, _) in enumerate(jobs):
                    if n + 1 < len(jobs):
                        centre(n + 1)
                    dve.wait_ge(rstd_ready, n + 1)
                    dve.wait_ge(centred_ready, n + 1)
                    dve.tensor_tensor(dst[:, :, t0:t0 + w], centred[:, n % 2, :, 0:w],
                                      rstd[:, n % 2, 0:w].unsqueeze(1).broadcast_to([P, C, w]),
                                      ALU.mult).then_inc(normed, 1)

            @block.scalar
            def _(act):
                def square(n):
                    w = jobs[n][3]
                    act.wait_ge(centred_ready, n + 1)
                    if n >= 2:
                        act.wait_ge(var_ready, n - 1)
                    act.activation(squared[:, n % 2, :, 0:w], centred[:, n % 2, :, 0:w],
                                   ACT.Square).then_inc(squared_ready, 1)

                square(0)
                for n, (_, _, _, w, _, _, _) in enumerate(jobs):
                    if n + 1 < len(jobs):
                        square(n + 1)
                    act.wait_ge(var_ready, n + 1)
                    if n >= 2:
                        act.wait_ge(normed, n - 1)
                    act.activation(logvar[:, n % 2, 0:w], ps[:, 2 + n % 2, 0:w], ACT.Ln,
                                   bias=consts["eps"][:, 0:1]).then_inc(log_ready, 1)
                    act.wait_ge(log_ready, n + 1)
                    act.activation(rstd[:, n % 2, 0:w], logvar[:, n % 2, 0:w], ACT.Exp,
                                   scale=-0.5).then_inc(rstd_ready, 1)

            if affine:
                @block.gpsimd
                def _(pool):
                    for n in affine:
                        _, dst, t0, w, _, scale, shift = jobs[n]
                        pool.wait_ge(normed, n + 1)
                        for c in range(C):
                            part = dst[:, c, t0:t0 + w]
                            if shift is None:
                                pool.tensor_scalar(part, part, scale[:, c:c + 1], None, ALU.mult).then_inc(scaled, 1)
                            else:
                                pool.tensor_scalar(part, part, scale[:, c:c + 1], shift[:, c:c + 1],
                                                   ALU.mult, ALU.add).then_inc(scaled, 1)
                    pool.wait_ge(scaled, C * len(affine))


def norm_jobs(src, dst, rms=False, scale=None, shift=None):
    return [(src, dst, n * BLK, BLK, rms, scale, shift) for n in range(NBLK)]


def latent_attention(nc, consts, x, a, ctx_n, w_qkv, w_o):
    HP = 8
    DH = 64
    KEYS = S + CTX
    PIECE = KEYS // 3
    KT = S // P + 1
    QT = S // P
    RING = 3
    assert PIECE * 3 == KEYS
    AUX = [DH, 0]
    with ExitStack() as stack:
        sc = Scope(nc, stack, "A")
        wqkv = sc.sb("wqkv", [P, 2, 3, C, P])
        wo = sc.sb("wo", [P, 2, D])
        q_pair = sc.sb("q_pair", [P, S], F32R)
        q_aug = sc.sb("q_aug", [P, 2, S])
        k_aug = sc.sb("k_aug", [P, 2, KEYS])
        k_max = sc.sb("k_max", [P, 2, KEYS + 1], F32R)
        v_feat = sc.sb("v_feat", [P, S])
        v_tok = sc.sb("v_tok", [P, KT, P])
        probs = sc.sb("probs", [P, 2, RING, S])
        psum_keys = sc.sb("psum_keys", [P, 2, S])
        nmax = sc.sb("nmax", [P, 2, QT])
        logden = sc.sb("logden", [P, S])
        rden = sc.sb("rden", [P, S])
        heads = sc.sb("heads", [P, S])
        ps = sc.psum()
        names = """zeroed q_ps k_ps v_ps ctx_ps q_rounded k_rounded q_copied k_copied v_copied v_turned_ps ctx_v_ready
                   v_ready max_ps max_ready row_ps row_ready score_ps exp_ready pv_ps summed den_ps logden_ready
                   rden_ready heads_ready y_ps x_added"""
        s = {n: sc.sem(n) for n in names.split()}
        w_loaded = [sc.sem(f"w_loaded{u}") for u in range(2)]

        def bank_pair(b):
            return ps[:, b:b + 2, :].rearrange("p b n -> p (b n)")

        block = stack.enter_context(nc.Block())

        def load_pair(sp, pair, u):
            sp.dma_start(wqkv[:, u], w_qkv[pair].rearrange("o p t c n -> p (o t) c n")).then_inc(w_loaded[u], 16)
            sp.dma_start(wo[:, u], w_o[pair].rearrange("o p n -> p (o n)")).then_inc(w_loaded[u], 16)

        @block.sync
        def _(sp):
            for u in range(2):
                load_pair(sp, slice(u, u + 1), u)
            for b in range(B):
                with sp.Fori(0 if b else 1, HP // 2) as g:
                    for u in range(2):
                        sp.wait_ge(s["y_ps"], b * HP + 2 * g + u - 1)
                        load_pair(sp, bass.ds(2 * g + u, 1), u)

        def pe_pair(pe, g, u, b):
            n = 2 * g + u
            tok = b * S
            pe.wait_ge(w_loaded[u], 32 * (g + 1))
            pe.wait_ge(s["x_added"], n + 1)
            for t, first, done in ((0, 0, "q_ps"), (1, 2, "k_ps"), (2, 6, "v_ps")):
                for blk in range(2):
                    for c in range(C):
                        mm = pe.matmul(ps[:, first + blk, :], wqkv[:, u, t, c, :],
                                       a[:, c, tok + blk * BLK:tok + (blk + 1) * BLK], start=c == 0, stop=c == C - 1)
                mm.then_inc(s[done], 1)
            for c in range(C):
                pe.matmul(ps[:, 5, 0:CTX], wqkv[:, u, 1, c, :], ctx_n[:, c, b * CTX:(b + 1) * CTX],
                          start=c == 0, stop=c == C - 1)
            for c in range(C):
                mm = pe.matmul(ps[0:CTX, 5, P:2 * P], ctx_n[:, c, b * CTX:(b + 1) * CTX], wqkv[:, u, 2, c, :],
                               start=c == 0, stop=c == C - 1)
            mm.then_inc(s["ctx_ps"], 1)
            pe.wait_ge(s["v_copied"], n + 1)
            for kt in range(S // P):
                mm = pe.transpose(bank_pair(6)[:, kt * P:(kt + 1) * P], v_feat[:, kt * P:(kt + 1) * P],
                                  consts["ident"][:, :])
            mm.then_inc(s["v_turned_ps"], 1)
            pe.wait_ge(s["q_copied"], 2 * n + 2)
            pe.wait_ge(s["q_rounded"], 2 * n + 2)
            pe.wait_ge(s["k_rounded"], 2 * n + 2)
            pe.wait_ge(s["ctx_v_ready"], n + 1)
            for m in range(2 * QT):
                j, qt = divmod(m, QT)
                if m >= 2:
                    pe.wait_ge(s["max_ready"], 2 * QT * n + (m - 1))
                for i in range(3):
                    w = PIECE + PIECE % 2
                    mm = pe.matmul(ps[:, 3 * (m % 2) + i, 0:w], q_pair[:, qt * P:(qt + 1) * P],
                                   k_max[:, j, i * PIECE:i * PIECE + w], start=True, stop=True)
                mm.then_inc(s["max_ps"], 1)
            pe.wait_ge(s["max_ready"], 2 * QT * (n + 1))
            pe.wait_ge(s["v_ready"], n + 1)
            for j in range(2):
                for qt in range(QT):
                    mm = pe.matmul(bank_pair(6)[AUX[j]:AUX[j] + 1, qt * P:(qt + 1) * P], nmax[:, j, qt:qt + 1],
                                   consts["ident"][:, :], start=True, stop=True)
            mm.then_inc(s["row_ps"], 1)
            pe.wait_ge(s["row_ready"], 2 * n + 2)

            def pv(kt):
                kw = P if kt < KT - 1 else CTX
                pe.wait_ge(s["exp_ready"], 2 * KT * n + 2 * kt + 2)
                for blk in range(2):
                    for j in range(2):
                        mm = pe.matmul(ps[DH * j:DH * j + DH, 4 + blk, :], v_tok[0:kw, kt, DH * j:DH * j + DH],
                                       probs[0:kw, j, kt % RING, blk * BLK:(blk + 1) * BLK],
                                       start=kt == 0, stop=kt == KT - 1)
                mm.then_inc(s["pv_ps"], 1)

            for kt in range(KT):
                kw = P if kt < KT - 1 else CTX
                for j in range(2):
                    if kt:
                        pe.wait_ge(s["exp_ready"], 2 * KT * n + 2 * (kt - 1) + j + 1)
                    for blk in range(2):
                        mm = pe.matmul(ps[0:kw, 2 * j + blk, :], k_aug[:, j, kt * P:kt * P + kw],
                                       q_aug[:, j, blk * BLK:(blk + 1) * BLK], start=True, stop=True)
                    mm.then_inc(s["score_ps"], 1)
                if kt:
                    pv(kt - 1)
            pv(KT - 1)
            pe.wait_ge(s["summed"], 2 * (KT - 1) * (n + 1))
            for blk in range(2):
                for j in range(2):
                    mm = pe.matmul(ps[DH * j:DH * j + DH, 6 + blk, :], consts["ones"][:, 0:DH],
                                   psum_keys[:, j, blk * BLK:(blk + 1) * BLK], start=True, stop=True)
            mm.then_inc(s["den_ps"], 1)
            pe.wait_ge(s["heads_ready"], n + 1)
            for c in range(C):
                for blk in range(2):
                    mm = pe.matmul(ps[:, 2 * c + blk, :], wo[:, u, c * P:(c + 1) * P],
                                   heads[:, blk * BLK:(blk + 1) * BLK], start=True, stop=True)
            mm.then_inc(s["y_ps"], 1)

        @block.tensor
        def _(pe):
            pe.wait_ge(s["zeroed"], 5)
            for b in range(B):
                with pe.Fori(0, HP // 2) as g:
                    for u in range(2):
                        pe_pair(pe, b * (HP // 2) + g, u, b)

        def act_pair(act, n, b):
            act.wait_ge(s["k_ps"], n + 1)
            for j in range(2):
                r = slice(DH * j, DH * j + DH)
                act.activation(k_aug[r, j, 0:S], bank_pair(2)[r], ACT.Copy).then_inc(s["k_copied"], 1)
            act.wait_ge(s["v_ps"], n + 1)
            act.activation(v_feat[:, :], bank_pair(6), ACT.Copy).then_inc(s["v_copied"], 1)
            act.wait_ge(s["ctx_ps"], n + 1)
            for j in range(2):
                r = slice(DH * j, DH * j + DH)
                act.activation(k_aug[r, j, S:KEYS], ps[r, 5, 0:CTX], ACT.Copy).then_inc(s["k_copied"], 1)
            act.activation(v_tok[0:CTX, KT - 1, :], ps[0:CTX, 5, P:2 * P], ACT.Copy).then_inc(s["ctx_v_ready"], 1)
            for kt in range(KT):
                kw = P if kt < KT - 1 else CTX
                for j in range(2):
                    act.wait_ge(s["score_ps"], 2 * KT * n + 2 * kt + j + 1)
                    if kt >= RING:
                        act.wait_ge(s["pv_ps"], KT * n + kt - RING + 1)
                        act.wait_ge(s["summed"], 2 * (KT - 1) * n + 2 * max(kt - RING, 1))
                    act.activation(probs[0:kw, j, kt % RING, :], bank_pair(2 * j)[0:kw], ACT.Exp,
                                   scale=1.0 / 8.0).then_inc(s["exp_ready"], 1)
            act.wait_ge(s["den_ps"], n + 1)
            act.activation(logden[:, :], bank_pair(6), ACT.Ln).then_inc(s["logden_ready"], 1)
            act.wait_ge(s["logden_ready"], n + 1)
            act.activation(rden[:, :], logden[:, :], ACT.Exp, scale=-1.0).then_inc(s["rden_ready"], 1)

        @block.scalar
        def _(act):
            act.wait_ge(s["zeroed"], 5)
            for b in range(B):
                with act.Fori(0, HP // 2) as g:
                    for u in range(2):
                        act_pair(act, b * HP + u + 2 * g, b)

        def dve_pair(dve, n, b):
            dve.wait_ge(s["q_ps"], n + 1)
            for j in range(2):
                r = slice(DH * j, DH * j + DH)
                dve.tensor_copy(q_aug[r, j, :], bank_pair(0)[r]).then_inc(s["q_copied"], 1)
            dve.wait_ge(s["q_copied"], 2 * n + 2)
            for j in range(2):
                r = slice(DH * j, DH * j + DH)
                dve.tensor_copy(q_pair[r, :], q_aug[r, j, :]).then_inc(s["q_rounded"], 1)
            dve.wait_ge(s["k_copied"], 4 * n + 4)
            for j in range(2):
                r = slice(DH * j, DH * j + DH)
                dve.tensor_copy(k_max[r, j, 0:KEYS], k_aug[r, j, :]).then_inc(s["k_rounded"], 1)
            dve.wait_ge(s["v_turned_ps"], n + 1)
            dve.tensor_copy(v_tok[:, 0:KT - 1, :], ps[:, 6:8, :].rearrange("p b (t n) -> p (b t) n", n=P)).then_inc(s["v_ready"], 1)
            for m in range(2 * QT):
                j, qt = divmod(m, QT)
                dve.wait_ge(s["max_ps"], 2 * QT * n + m + 1)
                dve.tensor_reduce(nmax[:, j, qt:qt + 1], ps[:, 3 * (m % 2):3 * (m % 2) + 3, 0:PIECE], AX.XY,
                                  ALU.max, negate=True).then_inc(s["max_ready"], 1)
            dve.wait_ge(s["row_ps"], n + 1)
            for j in range(2):
                r = slice(AUX[j], AUX[j] + 1)
                dve.tensor_copy(q_aug[r, j, :], bank_pair(6)[r]).then_inc(s["row_ready"], 1)
            dve.wait_ge(s["rden_ready"], n + 1)
            dve.wait_ge(s["pv_ps"], KT * (n + 1))
            dve.tensor_tensor(heads[:, :], bank_pair(4), rden[:, :], ALU.mult).then_inc(s["heads_ready"], 1)
            dve.wait_ge(s["y_ps"], n + 1)
            part = x[:, :, b * S:(b + 1) * S]
            dve.tensor_tensor(part, part, ps[:, 0:4, :].rearrange("p (c b) n -> p c (b n)", c=C), ALU.add)\
               .then_inc(s["x_added"], 1)
            dve.wait_ge(s["x_added"], n + 2)

        @block.vector
        def _(dve):
            dve.sem_inc(s["x_added"], 1)
            for buf in (q_aug, k_aug):
                dve.memset(buf[:, :, :], 0.0).then_inc(s["zeroed"], 1)
            dve.memset(k_max[:, :, :].bitcast(F32), 0.0).then_inc(s["zeroed"], 1)
            dve.wait_ge(s["zeroed"], 3)
            for j in range(2):
                dve.memset(k_aug[AUX[j]:AUX[j] + 1, j, :], 1.0).then_inc(s["zeroed"], 1)
            for b in range(B):
                with dve.Fori(0, HP // 2) as g:
                    for u in range(2):
                        dve_pair(dve, b * HP + u + 2 * g, b)

        def pool_pair(pool, n):
            for kt in range(1, KT):
                kw = P if kt < KT - 1 else CTX
                for j in range(2):
                    pool.wait_ge(s["exp_ready"], 2 * KT * n + 2 * kt + j + 1)
                    if kt == 1:
                        first = probs[:, j, 0, :]
                    else:
                        first = psum_keys[0:kw, j, :]
                        pool.wait_ge(s["summed"], 2 * (KT - 1) * n + 2 * (kt - 2) + j + 1)
                    pool.tensor_tensor(psum_keys[0:kw, j, :], first, probs[0:kw, j, kt % RING, :],
                                       ALU.add).then_inc(s["summed"], 1)

        @block.gpsimd
        def _(pool):
            for b in range(B):
                with pool.Fori(0, HP // 2) as g:
                    for u in range(2):
                        pool_pair(pool, b * HP + u + 2 * g)


def chain(engine, sem):
    count = [0]

    def step(instruction):
        count[0] += 1
        instruction.then_inc(sem, 1)
        engine.wait_ge(sem, count[0])
    return step


def top_experts(dve, step, order, score, left, index, keep, first, onehots, tops):
    wide = [P, TILES, E]
    for k, hot in enumerate(onehots):
        src = left if k else score
        step(dve.tensor_reduce(tops[k], src[:, :, :], AX.X, ALU.max))
        step(dve.tensor_tensor(index[:, :, :], src[:, :, :], tops[k].unsqueeze(2).broadcast_to(wide), ALU.is_equal))
        step(dve.tensor_tensor(index[:, :, :], index[:, :, :], order[:, :].unsqueeze(1).broadcast_to(wide), ALU.mult))
        step(dve.tensor_reduce(first, index[:, :, :], AX.X, ALU.max))
        step(dve.tensor_tensor(hot[:, :, :], index[:, :, :], first.unsqueeze(2).broadcast_to(wide), ALU.is_equal))
        if k + 1 < len(onehots):
            step(dve.tensor_scalar(keep[:, :, :], hot[:, :, :], -1.0, 1.0, ALU.mult, ALU.add))
            step(dve.tensor_tensor(index[:, :, :], score[:, :, :], keep[:, :, :], ALU.mult))
            step(dve.tensor_scalar(keep[:, :, :], hot[:, :, :], -3.0e38, None, ALU.mult))
            step(dve.tensor_tensor(left[:, :, :], index[:, :, :], keep[:, :, :], ALU.add))


def router_stage(nc, stage, kind, consts, y, router_w, bias, small, order, temperature, gates_t, gates_dram, weights):
    G = B * E
    wide = [P, TILES, E]
    with ExitStack() as stack:
        sc = Scope(nc, stack, stage)
        score, left, index, keep, gates, expd = (sc.sb(n, wide) for n in ("score", "left", "index", "keep", "gates", "expd"))
        hot = [sc.sb(f"hot{k}", wide) for k in range(1 if kind == "top1" else 2)]
        rowv = sc.sb("rowv", [P, 8, TILES])
        colv = sc.sb("colv", [P, 5, G])
        temp = sc.sb("temp", [P, 2])
        ps = sc.psum()
        small_loaded, logits_ps, dve_step = sc.sem("small_loaded"), sc.sem("logits_ps"), sc.sem("dve_step")
        act_asked, act_done = sc.sem("act_asked"), sc.sem("act_done")
        maxima_ready, maxima_all = sc.sem("maxima_ready"), sc.sem("maxima_all")
        sums_ready, sums_all = sc.sem("sums_ready"), sc.sem("sums_all")
        gates_ready, turned_ps, gates_copied, stored = (sc.sem(n) for n in ("gates_ready", "turned_ps", "gates_copied", "stored"))
        rounds = 3 if kind == "sinkhorn" else 0
        block = stack.enter_context(nc.Block())

        @block.sync
        def _(sp):
            for dst, src in small:
                sp.dma_start(dst, src).then_inc(small_loaded, 16)
            for dst, src, loaded in weights:
                sp.dma_start(dst, src).then_inc(loaded, 16)
            sp.wait_ge(gates_copied, 1)
            sp.dma_start(gates_dram, gates_t[:, :]).then_inc(stored, 16)
            sp.wait_ge(stored, 16)

        @block.tensor
        def _(pe):
            pe.wait_ge(small_loaded, 16 * len(small))
            for t in range(TILES):
                for c in range(C):
                    mm = pe.matmul(ps[:, 0, t * E:(t + 1) * E], y[:, c, t * P:(t + 1) * P], router_w[:, c, :],
                                   start=c == 0, stop=c == C - 1)
            mm.then_inc(logits_ps, 1)
            for r in range(rounds):
                pe.wait_ge(sums_ready, r + 1)
                pe.matmul(ps[:, 1, 0:G], consts["ones"][:, :], colv[:, 3, :], start=True, stop=True).then_inc(sums_all, 1)
            pe.wait_ge(gates_ready, 1)
            for t in range(TILES):
                mm = pe.transpose(ps[0:E, 4 + t // 4, (t % 4) * P:(t % 4 + 1) * P], gates[:, t, :], consts["ident"][:, :])
            mm.then_inc(turned_ps, 1)

        @block.vector
        def _(dve):
            step = chain(dve, dve_step)
            asked = [0]

            def act_does():
                asked[0] += 1
                dve.sem_inc(act_asked, 1)
                dve.wait_ge(act_done, asked[0])

            def per_token(v):
                return v.unsqueeze(2).broadcast_to(wide)

            def by_expert(v):
                return v.rearrange("p (b t) e -> p b e t", b=B)

            def per_expert(v):
                return v.rearrange("p (b e) -> p b e", b=B).unsqueeze(3).broadcast_to([P, B, E, TILES // B])

            def grouped(v):
                return v.rearrange("p (b e) -> p b e", b=B)

            dve.wait_ge(small_loaded, 16 * len(small))
            dve.wait_ge(logits_ps, 1)
            logits = ps[:, 0, 0:TILES * E].rearrange("p (t e) -> p t e", e=E)
            if bias is not None:
                step(dve.tensor_tensor(score[:, :, :], logits, bias.unsqueeze(1).broadcast_to(wide), ALU.add))
            else:
                step(dve.tensor_copy(score[:, :, :], logits))
            if kind == "sinkhorn":
                s4 = by_expert(score[:, :, :])
                step(dve.tensor_scalar(temp[:, 0:1], temperature, 0.1, None, ALU.max))
                step(dve.reciprocal(temp[:, 1:2], temp[:, 0:1]))
                step(dve.tensor_scalar(score[:, :, :], score[:, :, :], temp[:, 1:2], None, ALU.mult))
                for r in range(rounds):
                    step(dve.tensor_reduce(rowv[:, 0, :], score[:, :, :], AX.X, ALU.max))
                    step(dve.tensor_tensor(score[:, :, :], score[:, :, :], per_token(rowv[:, 0, :]), ALU.subtract))
                    act_does()
                    step(dve.tensor_reduce(rowv[:, 1, :], expd[:, :, :], AX.X, ALU.add))
                    act_does()
                    step(dve.tensor_tensor(score[:, :, :], score[:, :, :], per_token(rowv[:, 2, :]), ALU.subtract))
                    step(dve.tensor_reduce(grouped(colv[:, 0, :]), s4, AX.X, ALU.max))
                    dve.sem_inc(maxima_ready, 1)
                    dve.wait_ge(maxima_all, r + 1)
                    step(dve.tensor_tensor(s4, s4, per_expert(colv[:, 1, :]), ALU.subtract))
                    act_does()
                    step(dve.tensor_reduce(grouped(colv[:, 3, :]), by_expert(expd[:, :, :]), AX.X, ALU.add))
                    dve.sem_inc(sums_ready, 1)
                    dve.wait_ge(sums_all, r + 1)
                    act_does()
                    step(dve.tensor_tensor(s4, s4, per_expert(colv[:, 4, :]), ALU.subtract))
                act_does()
                step(dve.tensor_reduce(rowv[:, 3, :], expd[:, :, :], AX.X, ALU.add))
                step(dve.tensor_scalar(rowv[:, 3, :], rowv[:, 3, :], 1e-8, None, ALU.add))
                step(dve.reciprocal(rowv[:, 4, :], rowv[:, 3, :]))
                step(dve.tensor_tensor(score[:, :, :], expd[:, :, :], per_token(rowv[:, 4, :]), ALU.mult))
            tops = [rowv[:, 5, :], rowv[:, 6, :]]
            top_experts(dve, step, order, score, left, index, keep, rowv[:, 7, :], hot, tops)
            if kind == "top1":
                dve.tensor_copy(gates[:, :, :], hot[0][:, :, :]).then_inc(gates_ready, 1)
                return
            if kind == "top2":
                step(dve.tensor_tensor(rowv[:, 0, :], tops[1], tops[0], ALU.subtract))
                act_does()
                step(dve.tensor_scalar(rowv[:, 2, :], rowv[:, 1, :], 1.0, None, ALU.add))
                step(dve.reciprocal(rowv[:, 3, :], rowv[:, 2, :]))
                step(dve.tensor_tensor(rowv[:, 4, :], rowv[:, 1, :], rowv[:, 3, :], ALU.mult))
            else:
                step(dve.tensor_tensor(rowv[:, 0, :], tops[1], tops[0], ALU.add))
                step(dve.tensor_scalar(rowv[:, 1, :], rowv[:, 0, :], 1e-8, None, ALU.add))
                step(dve.reciprocal(rowv[:, 2, :], rowv[:, 1, :]))
                step(dve.tensor_tensor(rowv[:, 3, :], tops[0], rowv[:, 2, :], ALU.mult))
                step(dve.tensor_tensor(rowv[:, 4, :], tops[1], rowv[:, 2, :], ALU.mult))
            for k in range(2):
                step(dve.tensor_tensor(hot[k][:, :, :], hot[k][:, :, :], per_token(rowv[:, 3 + k, :]), ALU.mult))
            dve.tensor_tensor(gates[:, :, :], hot[0][:, :, :], hot[1][:, :, :], ALU.add).then_inc(gates_ready, 1)

        @block.scalar
        def _(act):
            def answer(n, out, in_, func):
                act.wait_ge(act_asked, n)
                act.activation(out, in_, func).then_inc(act_done, 1)

            for r in range(rounds):
                answer(4 * r + 1, expd[:, :, :], score[:, :, :], ACT.Exp)
                answer(4 * r + 2, rowv[:, 2, :], rowv[:, 1, :], ACT.Ln)
                answer(4 * r + 3, expd[:, :, :], score[:, :, :], ACT.Exp)
                answer(4 * r + 4, colv[:, 4, :], ps[:, 1, 0:G], ACT.Ln)
            if kind == "sinkhorn":
                answer(4 * rounds + 1, expd[:, :, :], score[:, :, :], ACT.Exp)
            if kind == "top2":
                answer(1, rowv[:, 1, :], rowv[:, 0, :], ACT.Exp)
            act.wait_ge(turned_ps, 1)
            act.activation(gates_t[:, :], ps[0:E, 4:8, :].rearrange("p b n -> p (b n)"), ACT.Copy).then_inc(gates_copied, 1)

        if rounds:
            @block.gpsimd
            def _(pool):
                for r in range(rounds):
                    pool.wait_ge(maxima_ready, r + 1)
                    pool.partition_all_reduce(colv[:, 1, :], colv[:, 0, :], P, bass.bass_isa.ReduceOp.max).then_inc(maxima_all, 1)


def experts_stage(nc, stage, func, x, y, hidden, w_in, b_in, w_out, b_out, gates_t, gates_dram, loaded, plus):
    MC = hidden // P
    pairs = w_in[0].shape[1]
    STEPS = E * MC
    LAG = 2
    NB = 3
    NH = 4
    with ExitStack() as stack:
        sc = Scope(nc, stack, stage)
        gate = sc.sb("gate", [P, E, BLK])
        active = sc.sb("active", [P, NB, BLK])
        product = sc.sb("product", [P, NH, BLK]) if pairs == 2 else None
        gated = sc.sb("gated", [P, NH, BLK])
        ps = sc.psum()
        gate_loaded = [sc.sem(f"gate_loaded{e}") for e in range(E)]
        hidden_ps, active_ready, product_ready, gated_ready, out_ps, bias_ps, x_added, plus_added = (
            sc.sem(n) for n in ("hidden_ps", "active_ready", "product_ready", "gated_ready", "out_ps", "bias_ps",
                                "x_added", "plus_added"))
        read_done = product_ready if pairs == 2 else active_ready
        ONE = 1
        block = stack.enter_context(nc.Block())

        def gate_load(sp, e, tokens):
            sp.dma_start(gate[:, e, :], gates_dram[e:e + 1, tokens].broadcast_to([P, BLK])).then_inc(gate_loaded[e], 16)

        @block.sync
        def _(sp):
            for e in range(E):
                gate_load(sp, e, slice(0, BLK))
            with sp.Fori(0, NBLK - 1) as t:
                for e in range(E):
                    sp.wait_ge(gated_ready, ONE + STEPS * t + MC * (e + 1))
                    gate_load(sp, e, bass.ds(t * BLK + BLK, BLK))

        @block.tensor
        def _(pe):
            pe.sem_inc(out_ps, ONE)
            for e in range(E):
                pe.wait_ge(loaded[e], 32)

            def out(t, q):
                e, m = divmod(q, MC)
                pe.wait_ge(gated_ready, ONE + STEPS * t + q + 1)
                if q == 0:
                    pe.wait_ge(x_added, ONE + t)
                for c in range(C):
                    mm = pe.matmul(ps[:, 6 + c, :], w_out[e][:, m, c * P:(c + 1) * P], gated[:, q % NH, :],
                                   start=q == 0, stop=q == STEPS - 1 and b_out is None)
                mm.then_inc(out_ps, 1)

            with pe.Fori(0, NBLK) as t:
                for q in range(STEPS):
                    e, m = divmod(q, MC)
                    pe.wait_ge(read_done, ONE + STEPS * t + max(q - NB + 1, 0))
                    for i in range(pairs):
                        for c in range(C):
                            mm = pe.matmul(ps[:, pairs * (q % NB) + i, :], w_in[e][:, i, c, m * P:(m + 1) * P],
                                           y[:, c, bass.ts(t, BLK)], start=c == 0, stop=c == C - 1)
                    mm.then_inc(hidden_ps, 1)
                    if q >= LAG:
                        out(t, q - LAG)
                for q in range(STEPS - LAG, STEPS):
                    out(t, q)
                if b_out is not None:
                    for c in range(C):
                        mm = pe.matmul(ps[:, 6 + c, :], b_out[:, c * P:(c + 1) * P], gates_t[:, bass.ts(t, BLK)],
                                       start=False, stop=True)
                    mm.then_inc(bias_ps, 1)

        @block.scalar
        def _(act):
            act.sem_inc(active_ready, ONE)
            with act.Fori(0, NBLK) as t:
                for q in range(STEPS):
                    e, m = divmod(q, MC)
                    act.wait_ge(hidden_ps, STEPS * t + q + 1)
                    act.wait_ge(product_ready if pairs == 2 else gated_ready, ONE + STEPS * t + max(q - NB + 1, 0))
                    bias = b_in[:, e, m:m + 1] if b_in is not None else 0.0
                    act.activation(active[:, q % NB, :], ps[:, pairs * (q % NB), :], func, bias=bias).then_inc(active_ready, 1)

        def gating(engine, t, q, src, src_ready):
            e, m = divmod(q, MC)
            engine.wait_ge(src_ready, ONE + STEPS * t + q + 1)
            if m == 0:
                engine.wait_ge(gate_loaded[e], 16 * t + 16)
            engine.wait_ge(out_ps, ONE + STEPS * t + max(q - NH + 1, 0))
            engine.tensor_tensor(gated[:, q % NH, :], src, gate[:, e, :], ALU.mult).then_inc(gated_ready, 1)

        @block.vector
        def _(dve):
            dve.sem_inc(x_added, ONE)
            dve.sem_inc(product_ready if pairs == 2 else gated_ready, ONE)
            with dve.Fori(0, NBLK) as t:
                for q in range(STEPS):
                    if pairs == 2:
                        dve.wait_ge(active_ready, ONE + STEPS * t + q + 1)
                        dve.wait_ge(gated_ready, ONE + STEPS * t + max(q - NH + 1, 0))
                        dve.tensor_tensor(product[:, q % NH, :], active[:, q % NB, :], ps[:, 2 * (q % NB) + 1, :],
                                          ALU.mult).then_inc(product_ready, 1)
                    else:
                        gating(dve, t, q, active[:, q % NB, :], active_ready)
                part = x[:, :, bass.ts(t, BLK)]
                for i, more in enumerate(plus):
                    dve.tensor_tensor(part, part, more[:, :, bass.ts(t, BLK)], ALU.add).then_inc(plus_added, 1)
                    dve.wait_ge(plus_added, len(plus) * t + i + 1)
                if b_out is not None:
                    dve.wait_ge(bias_ps, t + 1)
                else:
                    dve.wait_ge(out_ps, ONE + STEPS * (t + 1))
                dve.tensor_tensor(part, part, ps[:, 6:8, :], ALU.add).then_inc(x_added, 1)

        if pairs == 2:
            @block.gpsimd
            def _(pool):
                pool.sem_inc(gated_ready, ONE)
                with pool.Fori(0, NBLK) as t:
                    for q in range(STEPS):
                        gating(pool, t, q, product[:, q % NH, :], product_ready)


def moe(nc, name, kind, func, hidden, consts, x, y, t, plus):
    with ExitStack() as stack:
        sc = Scope(nc, stack, name)
        pairs = t[f"{name}_w_in"].shape[2]
        w_in = [sc.sb(f"w_in{e}", [P, pairs, C, hidden]) for e in range(E)]
        w_out = [sc.sb(f"w_out{e}", [P, hidden // P, D]) for e in range(E)]
        loaded = [sc.sem(f"loaded{e}") for e in range(E)]
        weights = []
        for e in range(E):
            weights += [(w_in[e][:, :, :, :], t[f"{name}_w_in"][e], loaded[e]),
                        (w_out[e][:, :, :], t[f"{name}_w_out"][e], loaded[e])]
        router_w = sc.sb("router_w", [P, C, E])
        order = sc.sb("order", [P, E])
        small = [(router_w[:, :, :], t[f"{name}_router_w"]), (order[:, :], t["c_order"])]
        bias = temperature = b_in = b_out = None
        if f"{name}_router_b" in t:
            bias_t = sc.sb("router_b", [P, E])
            small.append((bias_t[:, :], t[f"{name}_router_b"]))
            bias = bias_t[:, :]
        if kind == "sinkhorn":
            temp_t = sc.sb("temperature", [P, 1])
            small.append((temp_t[:, :], t[f"{name}_temperature"]))
            temperature = temp_t[:, 0:1]
        if f"{name}_b_in" in t:
            b_in = sc.sb("b_in", [P, E, hidden // P])
            b_out = sc.sb("b_out", [E, D])
            small += [(b_in[:, :, :], t[f"{name}_b_in"]), (b_out[:, :], t[f"{name}_b_out"])]
        gates_t = sc.sb("gates_t", [E, T])
        gates_dram = t["scratch_gates_" + name]
        router_stage(nc, name + "r", kind, consts, y, router_w, bias, small, order, temperature, gates_t, gates_dram, weights)
        experts_stage(nc, name + "e", func, x, y, hidden, w_in, b_in, w_out, b_out, gates_t, gates_dram, loaded, plus)


def context_attention(nc, name, consts, x, y, ctx, t):
    HG, DH = 8, 16
    GK = HG * CTX
    HALF = GK // 2
    CH = [(k * P, min(P, GK - k * P)) for k in range(-(-GK // P))]
    FULL = len(CH) - 1
    SHORT = CH[-1][1]
    TB = BLK // P

    def slot(g, i):
        return g * FULL + i if i < FULL else C * FULL + g

    with ExitStack() as stack:
        sc = Scope(nc, stack, name)
        w = {k: sc.sb(k, [P, C, D]) for k in ("wq", "wk", "wv", "wo")}
        bias = {k: sc.sb(k, [P, C]) for k in ("bq", "bk", "bv", "bo")}
        mask = sc.sb("mask", [P, HG])
        q = sc.sb("q", [P, C, T])
        k_feat, v_feat = sc.sb("k_feat", [P, C, B * CTX]), sc.sb("v_feat", [P, C, B * CTX])
        k_spread, v_spread = sc.sb("k_spread", [P, B, C, GK]), sc.sb("v_spread", [P, B, C, GK])
        v_rows = sc.sb("v_rows", [P, B, C, len(CH), P])
        with ExitStack() as setup:
            ss = Scope(nc, setup, name + "s")
            ps = ss.psum()
            loaded, kv_ps, kv_ready, spread_ready, turned_ps, turned, q_ps, q_ready = (
                ss.sem(n) for n in "loaded kv_ps kv_ready spread_ready turned_ps turned q_ps q_ready".split())
            loads = [(v[:, :, :], t[f"{name}_{k}"]) for k, v in w.items()] + \
                    [(v[:, :], t[f"{name}_{k}"]) for k, v in bias.items()] + [(mask[:, :], t["c_head_mask"])]
            block = setup.enter_context(nc.Block())

            @block.sync
            def _(sp):
                for dst, src in loads:
                    sp.dma_start(dst, src).then_inc(loaded, 16)
                sp.wait_ge(loaded, 16 * len(loads))

            @block.tensor
            def _(pe):
                pe.wait_ge(loaded, 16 * len(loads))
                for i, m in enumerate(("wk", "wv")):
                    for g in range(C):
                        for c in range(C):
                            mm = pe.matmul(ps[:, i, g * B * CTX:(g + 1) * B * CTX], w[m][:, c, g * P:(g + 1) * P],
                                           ctx[:, c, :], start=c == 0, stop=c == C - 1)
                    mm.then_inc(kv_ps, 1)
                for n in range(NBLK * C):
                    blk, g = divmod(n, C)
                    if n >= 4:
                        pe.wait_ge(q_ready, n - 3)
                    for c in range(C):
                        mm = pe.matmul(ps[:, 2 + n % 4, :], w["wq"][:, c, g * P:(g + 1) * P],
                                       y[:, c, blk * BLK:(blk + 1) * BLK], start=c == 0, stop=c == C - 1)
                    mm.then_inc(q_ps, 1)
                for n in range(B * C):
                    b, g = divmod(n, C)
                    pe.wait_ge(spread_ready, 2 * n + 2)
                    if n:
                        pe.wait_ge(turned, 2 * n)
                    for k, (r0, rows) in enumerate(CH):
                        mm = pe.transpose(ps[0:rows, 6 + k // 4, (k % 4) * P:(k % 4 + 1) * P],
                                          v_spread[:, b, g, r0:r0 + rows], consts["ident"][:, :])
                    mm.then_inc(turned_ps, 1)

            @block.scalar
            def _(act):
                for i, (dst, bv) in enumerate(((k_feat, "bk"), (v_feat, "bv"))):
                    act.wait_ge(kv_ps, i + 1)
                    for g in range(C):
                        act.activation(dst[:, g, :], ps[:, i, g * B * CTX:(g + 1) * B * CTX], ACT.Identity,
                                       bias=bias[bv][:, g:g + 1]).then_inc(kv_ready, 1)
                for n in range(NBLK * C):
                    blk, g = divmod(n, C)
                    act.wait_ge(q_ps, n + 1)
                    act.activation(q[:, g, blk * BLK:(blk + 1) * BLK], ps[:, 2 + n % 4, :], ACT.Identity,
                                   bias=bias["bq"][:, g:g + 1]).then_inc(q_ready, 1)

            @block.vector
            def _(dve):
                dve.wait_ge(kv_ready, 4)
                for b in range(B):
                    for g in range(C):
                        for dst, src in ((k_spread, k_feat), (v_spread, v_feat)):
                            dve.tensor_tensor(dst[:, b, g, :].rearrange("p (h k) -> p h k", h=HG),
                                              src[:, g, b * CTX:(b + 1) * CTX].unsqueeze(1).broadcast_to([P, HG, CTX]),
                                              mask[:, :].unsqueeze(2).broadcast_to([P, HG, CTX]),
                                              ALU.mult).then_inc(spread_ready, 1)
                for n in range(B * C):
                    b, g = divmod(n, C)
                    dve.wait_ge(turned_ps, n + 1)
                    dve.tensor_copy(v_rows[:, b, g, 0:4, :], ps[:, 6, :].rearrange("p (k n) -> p k n", n=P)).then_inc(turned, 1)
                    rows = CH[4][1]
                    dve.tensor_copy(v_rows[0:rows, b, g, 4, :], ps[0:rows, 7, 0:P]).then_inc(turned, 1)

        with ExitStack() as main:
            ms = Scope(nc, main, name + "m")
            NK = C * len(CH)
            diff = ms.sb("diff", [P, 2, C, GK])
            expd = ms.sb("expd", [P, 2, C, GK])
            probs = ms.sb("probs", [P, 2, C, GK])
            probs_t = ms.sb("probs_t", [P, 2, NK, BLK])
            attended = ms.sb("attended", [P, 2, C, BLK])
            top, total, share = (ms.sb(n, [P, 2, 2 * C, HG // 2]) for n in ("top", "total", "share"))
            ps = ms.psum()
            names = """score_ps top_ready diff_ready exp_ready sum_ready share_ready probs_ready turned_ps turned
                       out_ps out_ready y_ps x_added"""
            s = {n: ms.sem(n) for n in names.split()}
            block = main.enter_context(nc.Block())
            by_head = [P, 2 * C, HG // 2, CTX]

            def heads_of(buf, n):
                return buf[:, n % 2].rearrange("p g (a h k) -> p (g a) h k", a=2, h=HG // 2)

            @block.tensor
            def _(pe):
                def scores(n):
                    if n:
                        pe.wait_ge(s["diff_ready"], n)
                    for i in range(2 * C):
                        mm = pe.matmul(ps[:, i, 0:HALF], q[:, i // 2, n * P:(n + 1) * P],
                                       k_spread[:, n * P // S, i // 2, (i % 2) * HALF:(i % 2 + 1) * HALF],
                                       start=True, stop=True)
                    mm.then_inc(s["score_ps"], 1)

                scores(0)
                for n in range(TILES):
                    if n + 1 < TILES:
                        scores(n + 1)
                    pe.wait_ge(s["probs_ready"], n + 1)
                    if n:
                        pe.wait_ge(s["turned"], 2 * n)
                    for k in range(NK):
                        g, i = divmod(k, len(CH))
                        r0, rows = CH[i]
                        k = slot(g, i)
                        mm = pe.transpose(ps[0:rows, 4 + k // 4, (k % 4) * P:(k % 4 + 1) * P],
                                          probs[:, n % 2, g, r0:r0 + rows], consts["ident"][:, :])
                    mm.then_inc(s["turned_ps"], 1)
                    if n % TB != TB - 1:
                        continue
                    blk = n // TB
                    pe.wait_ge(s["turned"], 2 * n + 2)
                    for g in range(C):
                        if g:
                            pe.wait_ge(s["out_ready"], C * blk + g)
                        elif blk:
                            pe.wait_ge(s["x_added"], C * blk)
                        for i, (r0, rows) in enumerate(CH):
                            mm = pe.matmul(ps[:, 7, :], v_rows[0:rows, n * P // S, g, i, :],
                                           probs_t[0:rows, blk % 2, slot(g, i), :], start=i == 0, stop=i == len(CH) - 1)
                        mm.then_inc(s["out_ps"], 1)
                    pe.wait_ge(s["out_ready"], C * blk + C)
                    for c in range(C):
                        if c:
                            pe.wait_ge(s["x_added"], C * blk + c)
                        for g in range(C):
                            mm = pe.matmul(ps[:, 7, :], w["wo"][:, g, c * P:(c + 1) * P], attended[:, blk % 2, g, :],
                                           start=g == 0, stop=g == C - 1)
                        mm.then_inc(s["y_ps"], 1)

            @block.vector
            def _(dve):
                def before_exp(n):
                    dve.wait_ge(s["score_ps"], n + 1)
                    banks = ps[:, 0:2 * C, 0:HALF].rearrange("p a (h k) -> p a h k", k=CTX)
                    if n >= 2:
                        dve.wait_ge(s["exp_ready"], n - 1)
                    dve.tensor_reduce(top[:, n % 2], banks, AX.X, ALU.max).then_inc(s["top_ready"], 1)
                    dve.wait_ge(s["top_ready"], n + 1)
                    dve.tensor_tensor(heads_of(diff, n), banks, top[:, n % 2].unsqueeze(3).broadcast_to(by_head),
                                      ALU.subtract).then_inc(s["diff_ready"], 1)

                before_exp(0)
                for n in range(TILES):
                    if n + 1 < TILES:
                        before_exp(n + 1)
                    dve.wait_ge(s["exp_ready"], n + 1)
                    dve.tensor_reduce(total[:, n % 2], heads_of(expd, n), AX.X, ALU.add).then_inc(s["sum_ready"], 1)
                    dve.wait_ge(s["sum_ready"], n + 1)
                    if n >= 2:
                        dve.wait_ge(s["probs_ready"], n - 1)
                    dve.reciprocal(share[:, n % 2], total[:, n % 2]).then_inc(s["share_ready"], 1)
                    if n % TB == TB - 1:
                        blk = n // TB
                        for c in range(C):
                            dve.wait_ge(s["y_ps"], C * blk + c + 1)
                            part = x[:, c, blk * BLK:(blk + 1) * BLK]
                            dve.scalar_tensor_tensor(out=part, in0=ps[:, 7, :], scalar=bias["bo"][:, c:c + 1], in1=part,
                                                     op0=ALU.add, op1=ALU.add).then_inc(s["x_added"], 1)

            @block.scalar
            def _(act):
                def exp(n):
                    act.wait_ge(s["diff_ready"], n + 1)
                    if n >= 2:
                        act.wait_ge(s["probs_ready"], n - 1)
                        act.wait_ge(s["sum_ready"], n - 1)
                    act.activation(expd[:, n % 2].rearrange("p g k -> p (g k)"), diff[:, n % 2].rearrange("p g k -> p (g k)"),
                                   ACT.Exp, scale=DH ** -0.5).then_inc(s["exp_ready"], 1)

                exp(0)
                for n in range(TILES):
                    if n + 1 < TILES:
                        exp(n + 1)
                    blk, i = divmod(n, TB)
                    act.wait_ge(s["turned_ps"], n + 1)
                    if blk >= 2:
                        act.wait_ge(s["out_ps"], C * (blk - 1))
                    banks = ps[:, 4:7, :].rearrange("p b (k n) -> p (b k) n", n=P)
                    for rows, k0, k1 in ((P, 0, C * FULL), (SHORT, C * FULL, NK)):
                        act.activation(probs_t[0:rows, blk % 2, k0:k1, i * P:(i + 1) * P], banks[0:rows, k0:k1],
                                       ACT.Copy).then_inc(s["turned"], 1)
                    if i == TB - 1:
                        for g in range(C):
                            act.wait_ge(s["out_ps"], C * blk + g + 1)
                            if blk >= 2:
                                act.wait_ge(s["y_ps"], C * (blk - 1))
                            act.activation(attended[:, blk % 2, g, :], ps[:, 7, :], ACT.Copy).then_inc(s["out_ready"], 1)

            @block.gpsimd
            def _(pool):
                for n in range(TILES):
                    pool.wait_ge(s["share_ready"], n + 1)
                    if n >= 2:
                        pool.wait_ge(s["turned_ps"], n - 1)
                    pool.tensor_tensor(heads_of(probs, n), heads_of(expd, n),
                                       share[:, n % 2].unsqueeze(3).broadcast_to(by_head), ALU.mult).then_inc(s["probs_ready"], 1)


def self_attention(nc, consts, h, r, t):
    GROUPS, NH, DH = 4, 4, 16
    HR = P // 2
    KT = S // P
    RING = 3
    AUX = 32
    V0 = 32
    with ExitStack() as stack:
        sc = Scope(nc, stack, "F1")
        w_in = sc.sb("w_in", [P, 2, 5, C, P])
        w_out = sc.sb("w_out", [P, 2, D])
        cols = sc.sb("cols", [P, 5])
        ones_at = sc.sb("ones_at", [P, P])
        den_to = sc.sb("den_to", [P, P])
        rounded = sc.sb("rounded", [P, 4, S], F32R)
        q_split = sc.sb("q_split", [P, 2, S], F32R)
        k_split = sc.sb("k_split", [P, NH, S], F32R)
        v_feat = sc.sb("v_feat", [P, S])
        v_tok = sc.sb("v_tok", [P, KT, P])
        probs = sc.sb("probs", [P, 2, RING, 2, BLK])
        nmax = sc.sb("nmax", [P, NH, KT])
        raw = sc.sb("raw", [P, S])
        logden = sc.sb("logden", [P, S])
        rden = sc.sb("rden", [P, S])
        heads = sc.sb("heads", [P, S])
        ps = sc.psum()
        names = """setup zeroed proj_ps rounded_ready q_ready k_ready v_ps v_copied v_turned_ps v_ready max_ps max_ready
                   row_ps row_ready score_ps exp_ready pv_ps raw_ready den_ps logden_ready rden_ready heads_ready
                   y_ps h_added"""
        s = {n: sc.sem(n) for n in names.split()}
        w_loaded = [sc.sem(f"w_loaded{u}") for u in range(2)]

        def pair(b):
            return ps[:, b:b + 2, :].rearrange("p b n -> p (b n)")

        MAX_BANKS = [4, 6, 0]
        ROW_BANKS = [2, 4]
        block = stack.enter_context(nc.Block())

        def load_group(sp, g, u):
            sp.dma_start(w_in[:, u], t["F1_w_in"][g].rearrange("o p t c n -> p (o t) c n")).then_inc(w_loaded[u], 16)
            sp.dma_start(w_out[:, u], t["F1_w_out"][g].rearrange("o p n -> p (o n)")).then_inc(w_loaded[u], 16)

        @block.sync
        def _(sp):
            for dst, src in ((cols[:, :], t["F1_cols"]), (ones_at[:, :], t["F1_ones_at"]), (den_to[:, :], t["F1_den_to"])):
                sp.dma_start(dst, src).then_inc(s["setup"], 16)
            for u in range(2):
                load_group(sp, slice(u, u + 1), u)
            for b in range(B):
                with sp.Fori(0 if b else 1, GROUPS // 2) as g:
                    for u in range(2):
                        sp.wait_ge(s["y_ps"], b * GROUPS + 2 * g + u - 1)
                        load_group(sp, bass.ds(2 * g + u, 1), u)

        def pe_group(pe, g, u, b):
            n = 2 * g + u
            pe.wait_ge(w_loaded[u], 32 * (g + 1))
            pe.wait_ge(s["h_added"], n + 1)

            def project(i, first):
                for blk in range(2):
                    for c in range(C):
                        mm = pe.matmul(ps[:, first + blk, :], w_in[:, u, i, c, :],
                                       r[:, c, b * S + blk * BLK:b * S + (blk + 1) * BLK], start=c == 0, stop=c == C - 1)
                return mm

            for i in range(4):
                project(i, 2 * i).then_inc(s["proj_ps"], 1)
            pe.wait_ge(s["q_ready"], 2 * n + 1)
            project(4, 0).then_inc(s["v_ps"], 1)
            pe.wait_ge(s["q_ready"], 2 * n + 2)
            pe.wait_ge(s["v_copied"], n + 1)
            for kt in range(KT):
                mm = pe.transpose(pair(2)[:, kt * P:(kt + 1) * P], v_feat[:, kt * P:(kt + 1) * P], consts["ident"][:, :])
            mm.then_inc(s["v_turned_ps"], 1)
            for m in range(NH * KT):
                hd, qt = divmod(m, KT)
                if m < 2:
                    pe.wait_ge(s["k_ready"], NH * n + 2 * m + 2)
                if m >= 3:
                    pe.wait_ge(s["max_ready"], NH * KT * n + m - 2)
                for i in range(2):
                    mm = pe.matmul(ps[:, MAX_BANKS[m % 3] + i, :], q_split[:, hd // 2, qt * P:(qt + 1) * P],
                                   k_split[:, hd, i * BLK:(i + 1) * BLK], start=True, stop=True)
                mm.then_inc(s["max_ps"], 1)
            pe.wait_ge(s["max_ready"], NH * KT * (n + 1))
            pe.wait_ge(s["v_ready"], n + 1)
            for hd in range(NH):
                row = AUX + HR * (hd % 2)
                for qt in range(KT):
                    mm = pe.matmul(pair(ROW_BANKS[hd // 2])[row:row + 1, qt * P:(qt + 1) * P], nmax[:, hd, qt:qt + 1],
                                   consts["ident"][:, :], start=True, stop=True)
            mm.then_inc(s["row_ps"], 1)
            pe.wait_ge(s["row_ready"], NH * (n + 1))
            steps = 2 * KT

            def pv(i):
                blk, kt = divmod(i, KT)
                pe.wait_ge(s["exp_ready"], 2 * steps * n + 2 * i + 2)
                for hd in range(NH):
                    mm = pe.matmul(ps[V0 * hd:V0 * hd + V0, 6 + blk, :], v_tok[:, kt, V0 * hd:V0 * hd + V0],
                                   probs[:, hd // 2, i % RING, hd % 2, :], start=kt == 0, stop=kt == KT - 1)
                mm.then_inc(s["pv_ps"], 1)

            for i in range(steps):
                blk, kt = divmod(i, KT)
                for hp in range(2):
                    if i:
                        pe.wait_ge(s["exp_ready"], 2 * steps * n + 2 * (i - 1) + hp + 1)
                    for j in range(2):
                        mm = pe.matmul(ps[:, 2 * hp + j, :], k_split[:, 2 * hp + j, kt * P:(kt + 1) * P],
                                       q_split[:, hp, blk * BLK:(blk + 1) * BLK], start=True, stop=True)
                    mm.then_inc(s["score_ps"], 1)
                if i:
                    pv(i - 1)
            pv(steps - 1)
            pe.wait_ge(s["raw_ready"], n + 1)
            for blk in range(2):
                mm = pe.matmul(ps[:, 4 + blk, :], den_to[:, :], raw[:, blk * BLK:(blk + 1) * BLK], start=True, stop=True)
            mm.then_inc(s["den_ps"], 1)
            pe.wait_ge(s["heads_ready"], n + 1)
            for c in range(C):
                for blk in range(2):
                    mm = pe.matmul(ps[:, 2 * c + blk, :], w_out[:, u, c * P:(c + 1) * P], heads[:, blk * BLK:(blk + 1) * BLK],
                                   start=True, stop=True)
            mm.then_inc(s["y_ps"], 1)

        @block.tensor
        def _(pe):
            pe.wait_ge(s["setup"], 48)
            for b in range(B):
                with pe.Fori(0, GROUPS // 2) as g:
                    for u in range(2):
                        pe_group(pe, b * (GROUPS // 2) + g, u, b)

        def act_group(act, n):
            steps = 2 * KT
            for i in range(4):
                act.wait_ge(s["proj_ps"], 4 * n + i + 1)
                if i < 2:
                    act.activation(rounded[:, i, :], pair(2 * i), ACT.Copy, scale=cols[:, 0:1]).then_inc(s["rounded_ready"], 1)
                else:
                    act.activation(rounded[:, i, :], pair(2 * i), ACT.Identity, scale=cols[:, 2:3],
                                   bias=cols[:, 4:5]).then_inc(s["rounded_ready"], 1)
            act.wait_ge(s["v_ps"], n + 1)
            act.activation(v_feat[:, :], pair(0), ACT.Copy).then_inc(s["v_copied"], 1)
            for i in range(steps):
                for hp in range(2):
                    act.wait_ge(s["score_ps"], 2 * steps * n + 2 * i + hp + 1)
                    if i >= RING:
                        act.wait_ge(s["pv_ps"], steps * n + i - RING + 1)
                    act.activation(probs[:, hp, i % RING].rearrange("p j n -> p (j n)"), pair(2 * hp), ACT.Exp,
                                   scale=DH ** -0.5).then_inc(s["exp_ready"], 1)
            act.wait_ge(s["den_ps"], n + 1)
            act.activation(logden[:, :], pair(4), ACT.Ln).then_inc(s["logden_ready"], 1)
            act.wait_ge(s["logden_ready"], n + 1)
            act.activation(rden[:, :], logden[:, :], ACT.Exp, scale=-1.0).then_inc(s["rden_ready"], 1)

        @block.scalar
        def _(act):
            act.wait_ge(s["setup"], 48)
            for b in range(B):
                with act.Fori(0, GROUPS // 2) as g:
                    for u in range(2):
                        act_group(act, b * GROUPS + 2 * g + u)

        def dve_group(dve, n, b):
            for i in range(2):
                dve.wait_ge(s["rounded_ready"], 4 * n + i + 1)
                dve.scalar_tensor_tensor(out=q_split[:, i, :], in0=pair(2 * i), scalar=cols[:, 1:2],
                                         in1=rounded[:, i, :].bitcast(F32), op0=ALU.mult, op1=ALU.add).then_inc(s["q_ready"], 1)
            for hd in range(NH):
                i = 2 + hd // 2
                rr = slice(HR * (hd % 2), HR * (hd % 2) + HR)
                dve.wait_ge(s["rounded_ready"], 4 * n + i + 1)
                dve.scalar_tensor_tensor(out=k_split[rr, hd, :], in0=pair(2 * i)[rr], scalar=cols[rr, 3:4],
                                         in1=rounded[rr, i, :].bitcast(F32), op0=ALU.mult, op1=ALU.add).then_inc(s["k_ready"], 1)
            dve.wait_ge(s["v_turned_ps"], n + 1)
            dve.tensor_tensor(v_tok[:, :, :], ps[:, 2:4, :].rearrange("p b (t n) -> p (b t) n", n=P),
                              ones_at[:, :].unsqueeze(1).broadcast_to([P, KT, P]), ALU.add).then_inc(s["v_ready"], 1)
            for m in range(NH * KT):
                hd, qt = divmod(m, KT)
                dve.wait_ge(s["max_ps"], NH * KT * n + m + 1)
                dve.tensor_reduce(nmax[:, hd, qt:qt + 1], pair(MAX_BANKS[m % 3]), AX.X, ALU.max,
                                  negate=True).then_inc(s["max_ready"], 1)
            dve.wait_ge(s["row_ps"], n + 1)
            for hd in range(NH):
                row = AUX + HR * (hd % 2)
                dve.tensor_copy(q_split[row:row + 1, hd // 2, :], pair(ROW_BANKS[hd // 2])[row:row + 1]).then_inc(s["row_ready"], 1)
            dve.wait_ge(s["pv_ps"], 2 * KT * (n + 1))
            dve.tensor_copy(raw[:, :], pair(6)).then_inc(s["raw_ready"], 1)
            dve.wait_ge(s["rden_ready"], n + 1)
            dve.tensor_tensor(heads[:, :], raw[:, :], rden[:, :], ALU.mult).then_inc(s["heads_ready"], 1)
            dve.wait_ge(s["y_ps"], n + 1)
            part = h[:, :, b * S:(b + 1) * S]
            dve.tensor_tensor(part, part, ps[:, 0:4, :].rearrange("p (c b) n -> p c (b n)", c=C), ALU.add)\
               .then_inc(s["h_added"], 1)
            dve.wait_ge(s["h_added"], n + 2)

        @block.vector
        def _(dve):
            dve.sem_inc(s["h_added"], 1)
            dve.memset(k_split[:, :, :].bitcast(F32), 0.0).then_inc(s["zeroed"], 1)
            dve.wait_ge(s["zeroed"], 1)
            dve.wait_ge(s["setup"], 48)
            for b in range(B):
                with dve.Fori(0, GROUPS // 2) as g:
                    for u in range(2):
                        dve_group(dve, b * GROUPS + 2 * g + u, b)


def align_stage(nc, consts, x, y, ctx, t):
    CK = 16
    W = S // CK
    SLOTS = CTX + CK - 1
    PAD = CK - 1
    ROWS = CTX + 2 * PAD
    LANES = 32 * B
    BIG = 1.0e30

    def dram(name):
        return nc.dram_tensor(f"align_{name}", [B, ROWS, S], F32).ap()

    def skewed(a, b):
        return bass.AP(a.tensor, b * ROWS * S + PAD * W, [[S - W, CK], [S, SLOTS], [1, W]])

    def straight(a, first=0):
        return a[:, PAD + first:PAD + first + CTX, :].rearrange("b r n -> r b n")

    cost_dram, total_dram, path_dram = dram("cost"), dram("total"), dram("path")
    move_dram = [dram(f"move{n}") for n in range(3)]

    def pads(a):
        return [a[:, r:r + PAD, :].rearrange("b r n -> r b n") for r in (0, PAD + CTX)]

    with ExitStack() as stack:
        sc = Scope(nc, stack, "G1")
        fill = sc.sb("fill", [PAD, 2, B, S])
        ctx_sq, y_sq = sc.sb("ctx_sq", [P, C, B * CTX]), sc.sb("y_sq", [P, C, T])
        norm = sc.sb("norm", [CTX, B])
        sums, dist2, dist = (sc.sb(n, [CTX, 2, BLK]) for n in ("sums", "dist2", "dist"))
        cost = sc.sb("cost", [CTX, T])
        ps = sc.psum()
        names = "filled ctx_squared y_squared norm_ps norm_ready prod_ps sums_ready dist2_ready dist_ready cost_ready stored"
        s = {n: sc.sem(n) for n in names.split()}
        block = stack.enter_context(nc.Block())

        @block.gpsimd
        def _(pool):
            pool.memset(fill[:, 0], BIG).then_inc(s["filled"], 1)
            pool.memset(fill[:, 1], 0.0).then_inc(s["filled"], 1)
            for c in range(C):
                pool.tensor_tensor(ctx_sq[:, c, :], ctx[:, c, :], ctx[:, c, :], ALU.mult).then_inc(s["ctx_squared"], 1)

        @block.scalar
        def _(act):
            for n in range(NBLK):
                act.activation(y_sq[:, :, n * BLK:(n + 1) * BLK], y[:, :, n * BLK:(n + 1) * BLK], ACT.Square)\
                   .then_inc(s["y_squared"], 1)
            for n in range(NBLK):
                act.wait_ge(s["dist_ready"], n + 1)
                act.activation(cost[:, n * BLK:(n + 1) * BLK], dist[:, n % 2, :], ACT.Sqrt).then_inc(s["cost_ready"], 1)

        @block.tensor
        def _(pe):
            pe.wait_ge(s["ctx_squared"], C)
            for b in range(B):
                for c in range(C):
                    mm = pe.matmul(ps[0:CTX, 0, b:b + 1], ctx_sq[:, c, b * CTX:(b + 1) * CTX], consts["ones"][:, 0:1],
                                   start=c == 0, stop=c == C - 1)
            mm.then_inc(s["norm_ps"], 1)
            for n in range(NBLK):
                b = n * BLK // S
                if n >= 2:
                    pe.wait_ge(s["dist2_ready"], n - 1)
                pe.wait_ge(s["y_squared"], n + 1)
                for c in range(C):
                    pe.matmul(ps[0:CTX, 2 + n % 2, :], consts["ones"][:, 0:CTX], y_sq[:, c, n * BLK:(n + 1) * BLK],
                              start=c == 0, stop=c == C - 1)
                for c in range(C):
                    mm = pe.matmul(ps[0:CTX, 4 + n % 2, :], ctx[:, c, b * CTX:(b + 1) * CTX], y[:, c, n * BLK:(n + 1) * BLK],
                                   start=c == 0, stop=c == C - 1)
                mm.then_inc(s["prod_ps"], 1)

        @block.vector
        def _(dve):
            dve.wait_ge(s["norm_ps"], 1)
            dve.tensor_copy(norm[:, :], ps[0:CTX, 0, 0:B]).then_inc(s["norm_ready"], 1)
            dve.wait_ge(s["norm_ready"], 1)
            for n in range(NBLK):
                b = n * BLK // S
                dve.wait_ge(s["prod_ps"], n + 1)
                if n >= 2:
                    dve.wait_ge(s["cost_ready"], n - 1)
                dve.tensor_scalar(sums[:, n % 2, :], ps[0:CTX, 2 + n % 2, :], norm[:, b:b + 1], None, ALU.add)\
                   .then_inc(s["sums_ready"], 1)
                dve.wait_ge(s["sums_ready"], n + 1)
                dve.scalar_tensor_tensor(out=dist2[:, n % 2, :], in0=ps[0:CTX, 4 + n % 2, :], scalar=-2.0,
                                         in1=sums[:, n % 2, :], op0=ALU.mult, op1=ALU.add).then_inc(s["dist2_ready"], 1)
                dve.wait_ge(s["dist2_ready"], n + 1)
                dve.tensor_scalar(dist[:, n % 2, :], dist2[:, n % 2, :], 0.0, None, ALU.max).then_inc(s["dist_ready"], 1)

        @block.sync
        def _(sp):
            sp.wait_ge(s["filled"], 2)
            count = 0
            for n, arrays in enumerate(([cost_dram], move_dram)):
                for a in arrays:
                    for dst in pads(a):
                        sp.dma_start(dst, fill[:, n]).then_inc(s["stored"], 16)
                        count += 16
            sp.wait_ge(s["cost_ready"], NBLK)
            sp.dma_start(straight(cost_dram), cost[:, :].rearrange("r (b n) -> r b n", b=B)).then_inc(s["stored"], 16)
            sp.wait_ge(s["stored"], count + 16)

    with ExitStack() as stack:
        sc = Scope(nc, stack, "G2")
        cost = sc.sb("cost", [LANES, SLOTS, W])
        total = sc.sb("total", [LANES, SLOTS + 1, 1 + W])
        start = sc.sb("start", [LANES, 1 + W])
        above = sc.sb("above", [LANES, W])
        filled, loaded, edge_ready, above_ready, row_ready, stored = (
            sc.sem(n) for n in "filled loaded edge_ready above_ready row_ready stored".split())
        from_left = [min(q + 1, CK) for q in range(CK)] + list(range(CK, 32))
        block = stack.enter_context(nc.Block())

        @block.gpsimd
        def _(pool):
            pool.memset(cost[:, :, :], BIG).then_inc(filled, 1)
            pool.memset(total[:, :, :], BIG).then_inc(filled, 1)

        @block.sync
        def _(sp):
            sp.wait_ge(filled, 2)
            for b in range(B):
                sp.dma_start(cost[32 * b:32 * b + CK], skewed(cost_dram, b)).then_inc(loaded, 16)
            sp.dma_start(total[:, 0, :], t["G_start"]).then_inc(loaded, 16)
            sp.wait_ge(row_ready, SLOTS)
            for b in range(B):
                sp.dma_start(skewed(total_dram, b), total[32 * b:32 * b + CK, 1:, 1:]).then_inc(stored, 16)
            sp.wait_ge(stored, 32)

        @block.vector
        def _(dve):
            dve.wait_ge(loaded, 48)
            for n in range(SLOTS):
                if n:
                    dve.wait_ge(row_ready, n)
                dve.stream_shuffle(total[:, n + 1, 0:1], total[:, n, W:W + 1], from_left).then_inc(edge_ready, 1)
                dve.tensor_tensor(above[:, :], total[:, n, 1:], total[:, n, 0:W], ALU.min).then_inc(above_ready, 1)
                dve.wait_ge(edge_ready, n + 1)
                dve.wait_ge(above_ready, n + 1)
                dve.tensor_tensor_scan(total[:, n + 1, 1:], above[:, :], cost[:, n, :], initial=total[:, n + 1, 0:1],
                                       op0=ALU.min, op1=ALU.add).then_inc(row_ready, 1)

    with ExitStack() as stack:
        sc = Scope(nc, stack, "G3")
        here, over = sc.sb("here", [CTX, B, 1 + S]), sc.sb("over", [CTX, B, 1 + S])
        least, not_diag = sc.sb("least", [CTX, B, S]), sc.sb("not_diag", [CTX, B, S])
        up, diag, left = (sc.sb(n, [CTX, B, S + 1]) for n in ("up", "diag", "left"))
        filled, loaded, dve_step, stored = (sc.sem(n) for n in "filled loaded dve_step stored".split())
        block = stack.enter_context(nc.Block())

        @block.gpsimd
        def _(pool):
            for a in (here, over):
                pool.memset(a[:, :, 0:1], BIG).then_inc(filled, 1)
            pool.memset(over[0:1, :, 1:], BIG).then_inc(filled, 1)
            for a in (diag, left):
                pool.memset(a[:, :, S:S + 1], 0.0).then_inc(filled, 1)

        @block.sync
        def _(sp):
            sp.dma_start(here[:, :, 1:], straight(total_dram)).then_inc(loaded, 16)
            sp.dma_start(over[1:, :, 1:], straight(total_dram)[0:CTX - 1]).then_inc(loaded, 16)
            sp.wait_ge(dve_step, 6)
            for a, dst in ((up[:, :, 0:S], 0), (diag[:, :, 1:], 1), (left[:, :, 1:], 2)):
                sp.dma_start(straight(move_dram[dst]), a).then_inc(stored, 16)
            sp.wait_ge(stored, 48)

        @block.vector
        def _(dve):
            step = chain(dve, dve_step)
            dve.wait_ge(filled, 5)
            dve.wait_ge(loaded, 32)
            c_up, c_diag, c_left = over[:, :, 1:], over[:, :, 0:S], here[:, :, 0:S]
            step(dve.tensor_tensor(least[:, :, :], c_up, c_left, ALU.min))
            step(dve.tensor_tensor(diag[:, :, 0:S], c_diag, least[:, :, :], ALU.is_le))
            step(dve.tensor_tensor(least[:, :, :], c_up, c_left, ALU.is_le))
            step(dve.tensor_scalar(not_diag[:, :, :], diag[:, :, 0:S], -1.0, 1.0, ALU.mult, ALU.add))
            step(dve.tensor_tensor(up[:, :, 0:S], least[:, :, :], not_diag[:, :, :], ALU.mult))
            step(dve.tensor_tensor(left[:, :, 0:S], not_diag[:, :, :], up[:, :, 0:S], ALU.subtract))

    with ExitStack() as stack:
        sc = Scope(nc, stack, "G4")
        move = [sc.sb(f"move{n}", [LANES, SLOTS + 1, W]) for n in range(2)]
        left = sc.sb("left", [LANES, SLOTS, W])
        path = sc.sb("path", [LANES, SLOTS + 1, W + 1])
        below = sc.sb("below", [LANES, 2, W])
        enter = sc.sb("enter", [LANES, W])
        filled, loaded, edge_ready, below_ready, enter_ready, row_ready, stored = (
            sc.sem(n) for n in "filled loaded edge_ready below_ready enter_ready row_ready stored".split())
        from_right = [CK] + list(range(CK - 1)) + list(range(CK, 32))
        block = stack.enter_context(nc.Block())

        @block.gpsimd
        def _(pool):
            for a in (*move, left, path):
                pool.memset(a[:, :, :], 0.0).then_inc(filled, 1)
            pool.wait_ge(filled, 4)
            pool.memset(move[0][:, SLOTS, :], 1.0).then_inc(filled, 1)

        @block.sync
        def _(sp):
            sp.wait_ge(filled, 5)
            for b in range(B):
                for a, src in zip((*move, left), move_dram):
                    sp.dma_start(a[32 * b:32 * b + CK, 0:SLOTS], skewed(src, b)).then_inc(loaded, 16)
            sp.dma_start(path[:, SLOTS, :], t["G_end"]).then_inc(loaded, 16)
            sp.wait_ge(row_ready, SLOTS)
            for b in range(B):
                sp.dma_start(skewed(path_dram, b), path[32 * b:32 * b + CK, 0:SLOTS, 0:W]).then_inc(stored, 16)
            sp.wait_ge(stored, 32)

        @block.vector
        def _(dve):
            dve.wait_ge(loaded, 16 * (3 * B + 1))
            for i, n in enumerate(reversed(range(SLOTS))):
                if i:
                    dve.wait_ge(row_ready, i)
                dve.stream_shuffle(path[:, n, W:W + 1], path[:, n + 1, 0:1], from_right).then_inc(edge_ready, 1)
                for m in range(2):
                    dve.tensor_tensor(below[:, m, :], path[:, n + 1, m:m + W], move[m][:, n + 1, :], ALU.mult)\
                       .then_inc(below_ready, 1)
                dve.wait_ge(below_ready, 2 * i + 2)
                dve.tensor_tensor(enter[:, :], below[:, 0, :], below[:, 1, :], ALU.add).then_inc(enter_ready, 1)
                dve.wait_ge(edge_ready, i + 1)
                dve.wait_ge(enter_ready, i + 1)
                dve.tensor_tensor_scan(path[:, n, W - 1::-1], left[:, n, ::-1], enter[:, ::-1],
                                       initial=path[:, n, W:W + 1], op0=ALU.mult, op1=ALU.add).then_inc(row_ready, 1)

    with ExitStack() as stack:
        sc = Scope(nc, stack, "G5")
        path = sc.sb("path", [CTX, B, S])
        ctx_rows = sc.sb("ctx_rows", [CTX, B, D])
        ps = sc.psum()
        loaded, out_ps, x_added = (sc.sem(n) for n in "loaded out_ps x_added".split())
        block = stack.enter_context(nc.Block())

        @block.sync
        def _(sp):
            sp.dma_start(path[:, :, :], straight(path_dram)).then_inc(loaded, 16)
            sp.dma_start(ctx_rows[:, :, :], t["G_ctx_rows"]).then_inc(loaded, 16)

        @block.tensor
        def _(pe):
            pe.wait_ge(loaded, 32)
            for n in range(NBLK):
                b, blk = divmod(n, S // BLK)
                for c in range(C):
                    mm = pe.matmul(ps[:, C * n + c, :], ctx_rows[:, b, c * P:(c + 1) * P], path[:, b, blk * BLK:(blk + 1) * BLK],
                                   start=True, stop=True)
                mm.then_inc(out_ps, 1)

        @block.vector
        def _(dve):
            for n in range(NBLK):
                dve.wait_ge(out_ps, n + 1)
                part = x[:, :, n * BLK:(n + 1) * BLK]
                dve.tensor_tensor(part, part, ps[:, C * n:C * n + C, :], ALU.add).then_inc(x_added, 1)
            dve.wait_ge(x_added, NBLK)


def slots_stage(nc, consts, x, y, t):
    N, PS = 64, 32
    SL = N * PS
    Q = SL // BLK
    TB = S // P
    G = SL // P
    GE = P // PS
    slots_dram = nc.dram_tensor("slots", [B, P, C, SL], F32).ap()
    made_dram = nc.dram_tensor("made", [B, P, G, D], F32).ap()
    with ExitStack() as outer:
        oc = Scope(nc, outer, "H")
        y_tok = oc.sb("y_tok", [P, TILES, D])
        logits = oc.sb("logits", [P, TILES, SL])

        with ExitStack() as stack:
            sc = Scope(nc, stack, "H0")
            ps = sc.psum()
            turned_ps, turned = sc.sem("turned_ps"), sc.sem("turned")
            with nc.Block() as block:
                @block.tensor
                def _(pe):
                    for n in range(TILES // 2):
                        for k in range(2):
                            for c in range(C):
                                tile = 2 * n + k
                                mm = pe.transpose(ps[:, n, k * D + c * P:k * D + (c + 1) * P],
                                                  y[:, c, tile * P:(tile + 1) * P], consts["ident"][:, :])
                        mm.then_inc(turned_ps, 1)

                @block.vector
                def _(dve):
                    for n in range(TILES // 2):
                        dve.wait_ge(turned_ps, n + 1)
                        dve.tensor_copy(y_tok[:, 2 * n:2 * n + 2, :], ps[:, n, :].rearrange("p (k d) -> p k d", k=2))\
                           .then_inc(turned, 1)

        with ExitStack() as stack:
            sc = Scope(nc, stack, "H1")
            phi = sc.sb("phi", [P, 2, C, BLK])
            diff = sc.sb("diff", [P, 2, BLK])
            dispatch = sc.sb("dispatch", [P, 2, B, BLK])
            staged = sc.sb("staged", [P, B, C, BLK])
            ps = sc.psum()
            names = "logits_ps kept0 kept1 diff_ready dispatch_ready slots_ps staged_ready stored"
            s = {n: sc.sem(n) for n in names.split()}
            phi_loaded = [sc.sem(f"phi_loaded{n}") for n in range(2)]
            LAG = 1
            steps = [(q, m) for q in range(Q) for m in range(TB)]
            block = stack.enter_context(nc.Block())

            @block.sync
            def _(sp):
                for q in range(Q):
                    if q >= 2:
                        sp.wait_ge(s["logits_ps"], TB * (q - 1))
                    sp.dma_start(phi[:, q % 2], t["H_phi"][q]).then_inc(phi_loaded[q % 2], 16)
                    if q >= 1:
                        sp.wait_ge(s["staged_ready"], B * q)
                        for b in range(B):
                            sp.dma_start(slots_dram[b][:, :, (q - 1) * BLK:q * BLK], staged[:, b]).then_inc(s["stored"], 16)
                sp.wait_ge(s["staged_ready"], B * Q)
                for b in range(B):
                    sp.dma_start(slots_dram[b][:, :, (Q - 1) * BLK:Q * BLK], staged[:, b]).then_inc(s["stored"], 16)
                sp.wait_ge(s["stored"], 16 * B * Q)

            @block.tensor
            def _(pe):
                def gather(n):
                    q, m = steps[n]
                    pe.wait_ge(s["dispatch_ready"], B * n + B)
                    if m == 0 and q:
                        pe.wait_ge(s["staged_ready"], B * q)
                    for b in range(B):
                        for c in range(C):
                            mm = pe.matmul(ps[:, 4 + C * b + c, :], y_tok[:, b * TB + m, c * P:(c + 1) * P],
                                           dispatch[:, n % 2, b, :], start=m == 0, stop=m == TB - 1)
                    mm.then_inc(s["slots_ps"], 1)

                for n, (q, m) in enumerate(steps):
                    if m == 0:
                        pe.wait_ge(phi_loaded[q % 2], 16 * (q // 2 + 1))
                    if n >= 2:
                        pe.wait_ge(s["kept0"], n - 1)
                        pe.wait_ge(s["kept1"], n - 1)
                    for b in range(B):
                        for c in range(C):
                            mm = pe.matmul(ps[:, 2 * (n % 2) + b, :], y[:, c, (b * TB + m) * P:(b * TB + m + 1) * P],
                                           phi[:, q % 2, c, :], start=c == 0, stop=c == C - 1)
                    mm.then_inc(s["logits_ps"], 1)
                    if n >= LAG:
                        gather(n - LAG)
                gather(len(steps) - 1)

            @block.scalar
            def _(act):
                for n, (q, m) in enumerate(steps):
                    act.wait_ge(s["logits_ps"], n + 1)
                    act.activation(logits[:, m, q * BLK:(q + 1) * BLK], ps[:, 2 * (n % 2), :], ACT.Copy).then_inc(s["kept0"], 1)
                    act.wait_ge(s["diff_ready"], n + 1)
                    if n >= 2:
                        act.wait_ge(s["slots_ps"], n - 1)
                    for b in range(B):
                        act.activation(dispatch[:, n % 2, b, :], diff[:, n % 2, :], ACT.Sigmoid,
                                       scale=1.0 - 2.0 * b).then_inc(s["dispatch_ready"], 1)

            def stage_out(dve, q, b):
                dve.wait_ge(s["slots_ps"], TB * (q + 1))
                if q:
                    dve.wait_ge(s["stored"], 16 * B * q)
                dve.tensor_copy(staged[:, b], ps[:, 4 + C * b:4 + C * b + C, :]).then_inc(s["staged_ready"], 1)

            @block.vector
            def _(dve):
                for n, (q, m) in enumerate(steps):
                    dve.wait_ge(s["logits_ps"], n + 1)
                    dve.tensor_copy(logits[:, TB + m, q * BLK:(q + 1) * BLK], ps[:, 2 * (n % 2) + 1, :]).then_inc(s["kept1"], 1)
                    if m == 0 and q:
                        for b in range(B):
                            stage_out(dve, q - 1, b)
                for b in range(B):
                    stage_out(dve, Q - 1, b)

            @block.gpsimd
            def _(pool):
                for n, (q, m) in enumerate(steps):
                    pool.wait_ge(s["kept0"], n + 1)
                    pool.wait_ge(s["kept1"], n + 1)
                    if n >= 2:
                        pool.wait_ge(s["dispatch_ready"], B * (n - 1))
                    cols = slice(q * BLK, (q + 1) * BLK)
                    pool.tensor_tensor(diff[:, n % 2, :], logits[:, m, cols], logits[:, TB + m, cols],
                                       ALU.subtract).then_inc(s["diff_ready"], 1)

        slots = [y[:, :, :], y_tok[:, :, :].rearrange("p t d -> p (t d)").rearrange("p (c n) -> p c n", c=C)]
        with ExitStack() as stack:
            sc = Scope(nc, stack, "H2")
            RING = 3
            w = sc.sb("w", [P, RING, C, D])
            bias = sc.sb("bias", [P, 2, D])
            made = sc.sb("made", [P, 2, B, D])
            ps = sc.psum()
            names = "slots_loaded expert_ps group_ps made_ready"
            s = {n: sc.sem(n) for n in names.split()}
            w_loaded = [sc.sem(f"w_loaded{n}") for n in range(RING)]
            bias_loaded = [sc.sem(f"bias_loaded{n}") for n in range(2)]
            stored = [sc.sem(f"stored{n}") for n in range(2)]
            block = stack.enter_context(nc.Block())

            @block.sync
            def _(sp):
                for b in range(B):
                    sp.dma_start(slots[b], slots_dram[b]).then_inc(s["slots_loaded"], 16)
                for n in range(N):
                    if n >= RING:
                        sp.wait_ge(s["expert_ps"], n - RING + 1)
                    sp.dma_start(w[:, n % RING], t["H_w"][n]).then_inc(w_loaded[n % RING], 16)

            def store(pool, g):
                pool.wait_ge(s["made_ready"], g + 1)
                pool.dma_start(made_dram[:, :, g, :].rearrange("b p d -> p b d"), made[:, g % 2]).then_inc(stored[g % 2], 16)

            @block.gpsimd
            def _(pool):
                for g in range(G):
                    if g >= 2:
                        pool.wait_ge(s["made_ready"], g - 1)
                    pool.dma_start(bias[:, g % 2, :], t["H_b"][g]).then_inc(bias_loaded[g % 2], 16)
                    if g:
                        store(pool, g - 1)
                store(pool, G - 1)
                for n in range(2):
                    pool.wait_ge(stored[n], 16 * G // 2)

            @block.tensor
            def _(pe):
                pe.wait_ge(s["slots_loaded"], 16 * B)
                for n in range(N):
                    g, i = divmod(n, GE)
                    pe.wait_ge(w_loaded[n % RING], 16 * (n // RING + 1))
                    if i == 0 and g >= 2:
                        pe.wait_ge(s["made_ready"], g - 1)
                    for b in range(B):
                        for c in range(C):
                            mm = pe.matmul(ps[PS * i:PS * i + PS, 2 * (g % 2) + b, 0:D], slots[b][:, c, n * PS:(n + 1) * PS],
                                           w[:, n % RING, c, :], start=c == 0, stop=c == C - 1)
                    mm.then_inc(s["expert_ps"], 1)

            @block.vector
            def _(dve):
                for g in range(G):
                    dve.wait_ge(s["expert_ps"], GE * (g + 1))
                    dve.wait_ge(bias_loaded[g % 2], 16 * (g // 2 + 1))
                    if g >= 2:
                        dve.wait_ge(stored[g % 2], 16 * (g // 2))
                    dve.tensor_tensor(made[:, g % 2], ps[:, 2 * (g % 2):2 * (g % 2) + 2, 0:D],
                                      bias[:, g % 2, :].unsqueeze(1).broadcast_to([P, B, D]), ALU.add).then_inc(s["made_ready"], 1)

        outs = [y[:, :, :].rearrange("p c n -> p (c n)").rearrange("p (g d) -> p g d", d=D), y_tok[:, :, :]]
        with ExitStack() as stack:
            sc = Scope(nc, stack, "H3")
            nmax, total, share = (sc.sb(n, [P, TILES]) for n in ("nmax", "total", "share"))
            ps = sc.psum()
            names = "made_loaded max_ready exp_ready share_ready combine_ready turned_ps turned_a turned_b out_ps x_added"
            s = {n: sc.sem(n) for n in names.split()}
            BT = BLK // P
            block = stack.enter_context(nc.Block())

            @block.sync
            def _(sp):
                for b in range(B):
                    sp.dma_start(outs[b], made_dram[b]).then_inc(s["made_loaded"], 16)

            @block.tensor
            def _(pe):
                def out(blk):
                    if blk == 0:
                        pe.wait_ge(s["made_loaded"], 16 * B)
                    pe.wait_ge(s["turned_a"], BT * (blk + 1))
                    pe.wait_ge(s["turned_b"], BT * (blk + 1))
                    if blk >= 2:
                        pe.wait_ge(s["x_added"], blk - 1)
                    b = blk * BLK // S
                    for c in range(C):
                        for g in range(G):
                            mm = pe.matmul(ps[:, 4 + 2 * (blk % 2) + c, :], outs[b][:, g, c * P:(c + 1) * P],
                                           logits[:, BT * blk:BT * blk + BT, g * P:(g + 1) * P], start=g == 0, stop=g == G - 1)
                    mm.then_inc(s["out_ps"], 1)

                for n in range(TILES):
                    pe.wait_ge(s["combine_ready"], n + 1)
                    if n:
                        pe.wait_ge(s["turned_a"], n)
                        pe.wait_ge(s["turned_b"], n)
                    for g in range(G):
                        mm = pe.transpose(ps[:, g // 4, (g % 4) * P:(g % 4 + 1) * P], logits[:, n, g * P:(g + 1) * P],
                                          consts["ident"][:, :])
                    mm.then_inc(s["turned_ps"], 1)
                    if n % BT == 1 and n > BT:
                        out(n // BT - 1)
                out(TILES // BT - 1)

            def add(dve, blk):
                dve.wait_ge(s["out_ps"], blk + 1)
                part = x[:, :, blk * BLK:(blk + 1) * BLK]
                dve.tensor_tensor(part, part, ps[:, 4 + 2 * (blk % 2):6 + 2 * (blk % 2), :], ALU.add).then_inc(s["x_added"], 1)

            @block.vector
            def _(dve):
                def maximum(n):
                    dve.tensor_reduce(nmax[:, n:n + 1], logits[:, n, :], AX.X, ALU.max, negate=True).then_inc(s["max_ready"], 1)

                maximum(0)
                for n in range(TILES):
                    if n + 1 < TILES:
                        maximum(n + 1)
                    dve.wait_ge(s["exp_ready"], n + 1)
                    dve.reciprocal(share[:, n:n + 1], total[:, n:n + 1]).then_inc(s["share_ready"], 1)
                    dve.wait_ge(s["share_ready"], n + 1)
                    dve.tensor_scalar(logits[:, n, :], logits[:, n, :], share[:, n:n + 1], None, ALU.mult)\
                       .then_inc(s["combine_ready"], 1)
                    dve.wait_ge(s["turned_ps"], n + 1)
                    dve.tensor_copy(logits[:, n, SL // 2:], ps[:, 2:4, :].rearrange("p b n -> p (b n)")).then_inc(s["turned_b"], 1)
                    if n % BT == 2 and n > BT:
                        add(dve, n // BT - 1)
                add(dve, TILES // BT - 1)
                dve.wait_ge(s["x_added"], NBLK)

            @block.scalar
            def _(act):
                def exp(n):
                    act.wait_ge(s["max_ready"], n + 1)
                    act.activation(logits[:, n, :], logits[:, n, :], ACT.Exp, bias=nmax[:, n:n + 1],
                                   accum_out=total[:, n:n + 1]).then_inc(s["exp_ready"], 1)

                exp(0)
                for n in range(TILES):
                    if n + 1 < TILES:
                        exp(n + 1)
                    act.wait_ge(s["turned_ps"], n + 1)
                    act.activation(logits[:, n, 0:SL // 2], ps[:, 0:2, :].rearrange("p b n -> p (b n)"), ACT.Copy)\
                       .then_inc(s["turned_a"], 1)


def program(nc, t, out, stop=99, only=None):
    on = lambda k: stop >= k if only is None else k == only
    t = dict(t)
    for name in "BDF":
        t["scratch_gates_" + name] = nc.dram_tensor(f"gates_{name}", [E, T], F32).ap()
    with ExitStack() as stack:
        sc = Scope(nc, stack, "g")
        x = sc.sb("x", [P, C, T])
        y = sc.sb("y", [P, C, T])
        ctx = sc.sb("ctx", [P, C, B * CTX])
        names = ["mean", "ident", "ones"]
        consts = {n: sc.sb(n, [P, P]) for n in names}
        consts["eps"] = sc.sb("eps", [P, 1])
        load_stage(nc, "load", [(x[:, :, :], t["x"]), (ctx[:, :, :], t["ctx"]), (consts["eps"][:, :], t["c_eps"])]
                   + [(consts[n][:, :], t["c_" + n]) for n in names])
        if on(1):
            with ExitStack() as layer:
                ls = Scope(nc, layer, "A0")
                ctx_n = ls.sb("ctx_n", [P, C, B * CTX])
                lnw = {k: ls.sb(k, [P, C]) for k in ("ln1_w", "ln1_b", "ln2_w", "ln2_b")}
                load_stage(nc, "loadA", [(v[:, :], t["L0_xattn_" + k]) for k, v in lnw.items()])
                norm_stage(nc, "nA1", consts, norm_jobs(x, y))
                norm_stage(nc, "nA2", consts, norm_jobs(y, y, scale=lnw["ln2_w"], shift=lnw["ln2_b"])
                           + [(ctx, ctx_n, 0, B * CTX, False, lnw["ln1_w"], lnw["ln1_b"])])
                latent_attention(nc, consts, x, y, ctx_n, t["A_wqkv"], t["A_wo"])
        if on(2):
            norm_stage(nc, "nB", consts, norm_jobs(x, y))
            moe(nc, "B", "top1", ACT.Gelu, D, consts, x, y, t, [])
        if on(3):
            norm_stage(nc, "nC", consts, norm_jobs(x, y))
            context_attention(nc, "C", consts, x, y, ctx, t)
        if on(4):
            norm_stage(nc, "nD", consts, norm_jobs(x, y))
            moe(nc, "D", "sinkhorn", ACT.Relu, 2 * D, consts, x, y, t, [y])
        if on(5):
            norm_stage(nc, "nE", consts, norm_jobs(x, y))
            context_attention(nc, "E", consts, x, y, ctx, t)
        if on(6):
            norm_stage(nc, "nF", consts, norm_jobs(x, y))
            with ExitStack() as layer:
                ls = Scope(nc, layer, "F0")
                r = ls.sb("r", [P, C, T])
                lnw = {k: ls.sb(k, [P, C]) for k in ("ln1_w", "ln2_w")}
                load_stage(nc, "loadF", [(v[:, :], t["F_" + k]) for k, v in lnw.items()])
                norm_stage(nc, "nF1", consts, norm_jobs(y, r, rms=True, scale=lnw["ln1_w"]))
                self_attention(nc, consts, y, r, t)
                norm_stage(nc, "nF2", consts, norm_jobs(y, r, rms=True, scale=lnw["ln2_w"]))
                moe(nc, "F", "top2", ACT.Silu, 2 * D, consts, x, r, t, [y])
        if on(7):
            norm_stage(nc, "nG", consts, norm_jobs(x, y))
            align_stage(nc, consts, x, y, ctx, t)
        if on(8):
            norm_stage(nc, "nH", consts, norm_jobs(x, y))
            slots_stage(nc, consts, x, y, t)
        with ExitStack() as last:
            stored = Scope(nc, last, "out").sem("stored")
            with nc.Block() as block:
                @block.sync
                def _(sp):
                    sp.dma_start(out, x[:, :, :]).then_inc(stored, 16)
                    sp.wait_ge(stored, 16)


def lay_out(np, i):
    def feat(a):
        return a.T.reshape(-1, P, a.shape[0]).transpose(1, 0, 2)

    def rows(w):
        return w.reshape(-1, P, w.shape[-1]).transpose(1, 0, 2)

    def column(v):
        return v.reshape(-1, P).T

    def everywhere(v):
        return np.broadcast_to(v, (P,) + v.shape)

    def experts(name, w_in, w_out):
        w = np.stack(w_in, axis=1)
        t[name + "_w_in"] = w.reshape(E, len(w_in), C, P, -1).transpose(0, 3, 1, 2, 4)
        t[name + "_w_out"] = w_out.reshape(E, -1, P, D).transpose(0, 2, 1, 3)

    t = {"x": feat(i["x"].reshape(T, D)), "ctx": feat(i["ctx_1024"].reshape(B * CTX, D)),
         "c_mean": np.full((P, P), 1.0 / D, np.float32), "c_ident": np.eye(P, dtype=np.float32),
         "c_ones": np.ones((P, P), np.float32), "c_eps": np.full((P, 1), EPS, np.float32),
         "c_order": everywhere(np.arange(E, 0, -1, dtype=np.float32))}
    for k in ("ln1_w", "ln1_b", "ln2_w", "ln2_b"):
        t["L0_xattn_" + k] = column(i["L0_xattn_" + k])
    wq, wkv = i["L0_xattn_Wq"], i["L0_xattn_Wkv"]
    stacked = np.stack([wq, wkv[:, :1024], wkv[:, 1024:]])
    t["A_wqkv"] = stacked.reshape(3, C, P, 8, P).transpose(3, 2, 0, 1, 4)
    t["A_wo"] = i["L0_xattn_Wo"].reshape(8, P, D)
    experts("B", [i["L0_ffn_W1"]], i["L0_ffn_W2"])
    t["B_router_w"], t["B_router_b"] = rows(i["L0_ffn_Wg"]), everywhere(i["L0_ffn_bg"])
    t["B_b_in"] = i["L0_ffn_b1"].reshape(E, C, P).transpose(2, 0, 1)
    t["B_b_out"] = i["L0_ffn_b2"]
    experts("D", [i["L1_ffn_wg"], i["L1_ffn_wp"]], i["L1_ffn_wo"])
    t["D_router_w"], t["D_router_b"] = rows(i["L1_ffn_router_w"].T), everywhere(i["L1_ffn_router_b"])
    t["D_temperature"] = everywhere(i["L1_ffn_temperature"])
    t["F_ln1_w"], t["F_ln2_w"] = column(i["L2_ffn_ln1_w"]), column(i["L2_ffn_ln2_w"])
    experts("F", [i["L2_ffn_w1"].transpose(0, 2, 1), i["L2_ffn_w3"].transpose(0, 2, 1)], i["L2_ffn_w2"].transpose(0, 2, 1))
    t["F_router_w"] = rows(i["L2_ffn_gate_w"].T)
    t["c_head_mask"] = np.repeat(np.eye(8, dtype=np.float32), 16, axis=0)
    wkv, bkv = i["L1_xattn_Wkv"], i["L1_xattn_bkv"]
    for name, ws in (("C", (i["L1_xattn_Wq"], wkv[:D], wkv[D:], i["L1_xattn_Wo"])),
                     ("E", [i["L2_xattn_" + k] for k in ("wq", "wk", "wv", "wo")])):
        for k, w in zip(("wq", "wk", "wv", "wo"), ws):
            t[f"{name}_{k}"] = rows(w.T)
    for name, bs in (("C", (i["L1_xattn_bq"], bkv[:D], bkv[D:], i["L1_xattn_bo"])),
                     ("E", [i["L2_xattn_" + k] for k in ("bq", "bk", "bv", "bo")])):
        for k, b in zip(("bq", "bk", "bv", "bo"), bs):
            t[f"{name}_{k}"] = column(b)
    hi_hi, lo_hi, hi_lo, aux = 0, 16, 48, 32

    def qk_rows(w):
        w = w.reshape(4, 2, 2, 16, D)
        out = np.zeros((4, 2, 2, 64, D), w.dtype)
        for at in (hi_hi, lo_hi, hi_lo):
            out[:, :, :, at:at + 16] = w
        return out.reshape(4, 2, P, D).transpose(0, 1, 3, 2)

    v = np.zeros((4, 4, 32, D), np.float32)
    v[:, :, :16] = i["L2_ffn_wv"].reshape(4, 4, 16, D)
    wo = np.zeros((4, 4, 32, D), np.float32)
    wo[:, :, :16] = i["L2_ffn_wo"].T.reshape(4, 4, 16, D)
    w_in = np.concatenate([qk_rows(i["L2_ffn_wq"]), qk_rows(i["L2_ffn_wk"]), v.reshape(4, 1, P, D).transpose(0, 1, 3, 2)], 1)
    t["F1_w_in"] = w_in.reshape(4, 5, C, P, P).transpose(0, 3, 1, 2, 4)
    t["F1_w_out"] = wo.reshape(4, P, D)
    cols = np.zeros((2, 64, 5), np.float32)
    cols[:, :, 0] = cols[:, :, 2] = 1
    cols[:, hi_lo:hi_lo + 16, 0], cols[:, hi_lo:hi_lo + 16, 1] = -1, 1
    cols[:, lo_hi:lo_hi + 16, 2], cols[:, lo_hi:lo_hi + 16, 3] = -1, 1
    cols[:, aux, 4] = 1
    t["F1_cols"] = cols.reshape(P, 5)
    t["F1_ones_at"] = everywhere(np.tile(np.repeat(np.array([0, 1], np.float32), 16), 4))
    den = np.zeros((4, 32, 4, 32), np.float32)
    for hd in range(4):
        den[hd, 16, hd, :] = 1
    t["F1_den_to"] = den.reshape(P, P)
    start = np.full((2, 32, 65), 1.0e30, np.float32)
    start[:, 15, 0] = 0
    end = np.zeros((2, 32, 65), np.float32)
    end[:, 0, 63] = 1
    t["G_start"], t["G_end"] = start.reshape(64, 65), end.reshape(64, 65)
    t["G_ctx_rows"] = i["ctx_1024"].transpose(1, 0, 2)
    t["H_phi"] = rows(i["L3_ffn_phi"].reshape(D, 2048)).reshape(P, C, 4, BLK).transpose(2, 0, 1, 3)
    t["H_w"] = i["L3_ffn_W"].reshape(64, C, P, D).transpose(0, 2, 1, 3)
    t["H_b"] = np.repeat(i["L3_ffn_b"], 32, axis=0).reshape(16, P, D)
    return {k: np.ascontiguousarray(v) for k, v in t.items()}


def kernel(**inputs):
    import numpy as np
    import concourse.bacc as bacc
    from concourse.bass_utils import run_bass_kernel_spmd as run

    nc = bacc.Bacc("TRN2", target_bir_lowering=False, num_devices=1)
    arrays = lay_out(np, {k: np.asarray(v) for k, v in inputs.items()})
    aps = {k: nc.dram_tensor(f"in_{k}", v.shape, mybir.dt.from_np(v.dtype), kind="ExternalInput").ap()
           for k, v in arrays.items()}
    out = nc.dram_tensor("out", [P, C, T], F32, kind="ExternalOutput").ap()
    program(nc, aps, out)
    got = run(nc, [{f"in_{k}": v for k, v in arrays.items()}], core_ids=[0]).results[0]["out"]
    return got.transpose(1, 0, 2).reshape(D, T).T.reshape(B, S, D)
```

```python
from contextlib import ExitStack

import concourse.bass as bass
from concourse import mybir

ALU = mybir.AluOpType
ACT = mybir.ActivationFunctionType
F32 = mybir.dt.float32
F32R = mybir.dt.float32r
F16 = mybir.dt.float16
AX = mybir.AxisListType

P = 128
B = 2
S = 1024
T = B * S
D = 256
C = D // P
CTX = 77
BLK = 512
NBLK = T // BLK
TILES = T // P
EPS = 1e-5
E = 8


class Scope:

    def __init__(self, nc, stack, stage):
        self.nc, self.stack, self.stage = nc, stack, stage
        self.semaphores = []
        stack.callback(self.clear)

    def clear(self):
        for s in self.semaphores:
            self.nc.gpsimd.sem_clear(s)

    def sb(self, name, shape, dt=F32):
        return self.stack.enter_context(self.nc.sbuf_tensor(f"{self.stage}_{name}", shape, dt))

    def psum(self, name="banks"):
        return self.stack.enter_context(self.nc.psum_tensor(f"{self.stage}_{name}", [P, 8, BLK], F32))

    def sem(self, name):
        self.semaphores.append(self.stack.enter_context(self.nc.semaphore(f"{self.stage}_{name}")))
        return self.semaphores[-1]


def load_stage(nc, stage, pairs):
    with ExitStack() as stack:
        loaded = Scope(nc, stack, stage).sem("loaded")
        with nc.Block() as block:
            @block.sync
            def _(sp):
                for dst, src in pairs:
                    sp.dma_start(dst, src).then_inc(loaded, 16)
                sp.wait_ge(loaded, 16 * len(pairs))


def norm_stage(nc, stage, consts, jobs):
    with ExitStack() as stack:
        sc = Scope(nc, stack, stage)
        centred = sc.sb("centred", [P, 2, C, BLK])
        squared = sc.sb("squared", [P, 2, C, BLK])
        logvar = sc.sb("logvar", [P, 2, BLK])
        rstd = sc.sb("rstd", [P, 2, BLK])
        ps = sc.psum()
        mean_ready, centred_ready, squared_ready = sc.sem("mean_ready"), sc.sem("centred_ready"), sc.sem("squared_ready")
        var_ready, log_ready, rstd_ready = sc.sem("var_ready"), sc.sem("log_ready"), sc.sem("rstd_ready")
        normed, scaled = sc.sem("normed"), sc.sem("scaled")
        affine = [n for n, job in enumerate(jobs) if job[5] is not None]
        with nc.Block() as block:
            @block.tensor
            def _(pe):
                def mean(n):
                    src, _, t0, w, rms, _, _ = jobs[n]
                    if n >= 2:
                        pe.wait_ge(centred_ready, n - 1)
                    if n < 2 or not rms:
                        pass
                    for c in range(C):
                        mm = pe.matmul(ps[:, n % 2, 0:w], consts["mean"][:, :], src[:, c, t0:t0 + w],
                                       start=c == 0, stop=c == C - 1)
                    mm.then_inc(mean_ready, 1)

                mean(0)
                for n, (_, _, _, w, _, _, _) in enumerate(jobs):
                    if n + 1 < len(jobs):
                        mean(n + 1)
                    pe.wait_ge(squared_ready, n + 1)
                    if n >= 2:
                        pe.wait_ge(log_ready, n - 1)
                    for c in range(C):
                        mm = pe.matmul(ps[:, 2 + n % 2, 0:w], consts["mean"][:, :], squared[:, n % 2, c, 0:w],
                                       start=c == 0, stop=c == C - 1)
                    mm.then_inc(var_ready, 1)

            @block.vector
            def _(dve):
                def centre(n):
                    src, _, t0, w, rms, _, _ = jobs[n]
                    if n >= 2:
                        dve.wait_ge(normed, n - 1)
                        dve.wait_ge(squared_ready, n - 1)
                    dve.wait_ge(mean_ready, n + 1)
                    if rms:
                        dve.tensor_copy(centred[:, n % 2, :, 0:w], src[:, :, t0:t0 + w]).then_inc(centred_ready, 1)
                    else:
                        dve.tensor_tensor(centred[:, n % 2, :, 0:w], src[:, :, t0:t0 + w],
                                          ps[:, n % 2, 0:w].unsqueeze(1).broadcast_to([P, C, w]),
                                          ALU.subtract).then_inc(centred_ready, 1)

                centre(0)
                for n, (_, dst, t0, w, _, scale, _) in enumerate(jobs):
                    if n + 1 < len(jobs):
                        centre(n + 1)
                    dve.wait_ge(rstd_ready, n + 1)
                    dve.wait_ge(centred_ready, n + 1)
                    dve.tensor_tensor(dst[:, :, t0:t0 + w], centred[:, n % 2, :, 0:w],
                                      rstd[:, n % 2, 0:w].unsqueeze(1).broadcast_to([P, C, w]),
                                      ALU.mult).then_inc(normed, 1)

            @block.scalar
            def _(act):
                def square(n):
                    w = jobs[n][3]
                    act.wait_ge(centred_ready, n + 1)
                    if n >= 2:
                        act.wait_ge(var_ready, n - 1)
                    act.activation(squared[:, n % 2, :, 0:w], centred[:, n % 2, :, 0:w],
                                   ACT.Square).then_inc(squared_ready, 1)

                square(0)
                for n, (_, _, _, w, _, _, _) in enumerate(jobs):
                    if n + 1 < len(jobs):
                        square(n + 1)
                    act.wait_ge(var_ready, n + 1)
                    if n >= 2:
                        act.wait_ge(normed, n - 1)
                    act.activation(logvar[:, n % 2, 0:w], ps[:, 2 + n % 2, 0:w], ACT.Ln,
                                   bias=consts["eps"][:, 0:1]).then_inc(log_ready, 1)
                    act.wait_ge(log_ready, n + 1)
                    act.activation(rstd[:, n % 2, 0:w], logvar[:, n % 2, 0:w], ACT.Exp,
                                   scale=-0.5).then_inc(rstd_ready, 1)

            if affine:
                @block.gpsimd
                def _(pool):
                    for n in affine:
                        _, dst, t0, w, _, scale, shift = jobs[n]
                        pool.wait_ge(normed, n + 1)
                        for c in range(C):
                            part = dst[:, c, t0:t0 + w]
                            if shift is None:
                                pool.tensor_scalar(part, part, scale[:, c:c + 1], None, ALU.mult).then_inc(scaled, 1)
                            else:
                                pool.tensor_scalar(part, part, scale[:, c:c + 1], shift[:, c:c + 1],
                                                   ALU.mult, ALU.add).then_inc(scaled, 1)
                    pool.wait_ge(scaled, C * len(affine))


def norm_jobs(src, dst, rms=False, scale=None, shift=None):
    return [(src, dst, n * BLK, BLK, rms, scale, shift) for n in range(NBLK)]


def wait(engine, semaphore, value):
    if not isinstance(value, int) or value > 0:
        engine.wait_ge(semaphore, value)


def latent_attention(nc, consts, x, a, ctx_n, w_qkv, w_o):
    HP = 8
    DH = 64
    KEYS = S + CTX
    PIECE = KEYS // 3
    PW = PIECE + 1
    KT = S // P + 1
    QT = S // P
    UNITS = 2 * QT
    RING = 3
    assert PIECE * 3 == KEYS and PIECE % 2
    OWN = [slice(0, DH), slice(DH, P)]
    OTHER = [slice(DH, P), slice(0, DH)]
    AUX = [DH, 0]
    MAX_BANKS = (3, 6, 7)
    DEN_BANKS = (3, 6)
    PIECES = 3 * UNITS
    with ExitStack() as stack:
        sc = Scope(nc, stack, "A")
        wqkv = sc.sb("wqkv", [P, 3, C, P])
        wo = sc.sb("wo", [P, D])
        q_one = sc.sb("q_one", [P, 2, 2, S], F32R)
        q_two = sc.sb("q_two", [P, 2, 2, S], F32R)
        k_one = sc.sb("k_one", [P, 2, 2, KEYS + 1], F32R)
        k_two = sc.sb("k_two", [P, 2, 2, KEYS + 1], F32R)
        v_tok = sc.sb("v_tok", [P, 2, KT, P])
        probs = sc.sb("probs", [P, 2, RING, S])
        key_sums = sc.sb("key_sums", [P, 2, S])
        part_max = sc.sb("part_max", [P, UNITS, 3])
        nmax = sc.sb("nmax", [P, UNITS])
        nmax_rows = sc.sb("nmax_rows", [UNITS, P], F32R)
        logden = sc.sb("logden", [P, S])
        rden = sc.sb("rden", [P, S])
        heads = sc.sb("heads", [P, S])
        ps = sc.psum()
        names = """zeroed in_loaded out_loaded q_ps q_hi q_dup q_lo k_ps k_hi k_lo v_ps v_ready ctx_ps ctx_hi ctx_lo ctx_v
                   k_second piece_ps piece_max nmax_ready rows_ps rows_ready row_ready score_ps exp_ready
                   pv_ps summed den_ps logden_ready rden_ready heads_ready y_ps x_added"""
        s = {n: sc.sem(n) for n in names.split()}

        def bank_pair(b):
            return ps[:, b:b + 2, :].rearrange("p b n -> p (b n)")

        block = stack.enter_context(nc.Block())

        def units(engine, body, prologue=None):
            if prologue:
                prologue(0, 0)
            for b in range(B):
                body(b, b, b == 0, False)
            with engine.Fori(1, HP - 1) as hp:
                for b in range(B):
                    body(2 * hp + b, b, False, False)
            for b in range(B):
                body(2 * (HP - 1) + b, b, False, b == B - 1)

        @block.sync
        def _(sp):
            def load_in(pair):
                sp.dma_start(wqkv[:, :, :, :], w_qkv[pair].rearrange("o p t c n -> p (o t) c n")).then_inc(s["in_loaded"], 16)

            def load_out(pair):
                sp.dma_start(wo[:, :], w_o[pair].rearrange("o p n -> p (o n)")).then_inc(s["out_loaded"], 16)

            load_in(slice(0, 1))
            load_out(slice(0, 1))

            def reload(hp, pair):
                sp.wait_ge(s["v_ps"], 2 * hp)
                load_in(pair)
                sp.wait_ge(s["y_ps"], 4 * hp)
                load_out(pair)

            with sp.Fori(1, HP) as hp:
                reload(hp, bass.ds(hp, 1))

        @block.tensor
        def _(pe):
            def project(operand, b):
                for blk in range(2):
                    for c in range(C):
                        mm = pe.matmul(ps[:, 6 + blk, :], wqkv[:, operand, c, :],
                                       a[:, c, b * S + blk * BLK:b * S + (blk + 1) * BLK], start=c == 0, stop=c == C - 1)
                return mm

            def project_q(m, b):
                if b == 0:
                    pe.wait_ge(s["in_loaded"], 8 * m + 16)
                wait(pe, s["logden_ready"], 2 * m - 2)
                project(0, b).then_inc(s["q_ps"], 1)

            def project_k(m, b):
                if isinstance(m, int) and m < 2:
                    pe.wait_ge(s["q_lo"], 2 * m + 2)
                else:
                    pe.wait_ge(s["x_added"], 2 * m - 2)
                project(1, b).then_inc(s["k_ps"], 1)

            def project_ctx(m, b):
                for c in range(C):
                    pe.matmul(ps[:, 3, 0:CTX], wqkv[:, 1, c, :], ctx_n[:, c, b * CTX:(b + 1) * CTX],
                              start=c == 0, stop=c == C - 1)
                for c in range(C):
                    mm = pe.matmul(ps[0:CTX, 3, P:2 * P], ctx_n[:, c, b * CTX:(b + 1) * CTX], wqkv[:, 2, c, :],
                                   start=c == 0, stop=c == C - 1)
                mm.then_inc(s["ctx_ps"], 1)

            def project_v(m, b):
                pe.wait_ge(s["k_lo"], 2 * m + 2)
                for kt in range(KT - 1):
                    for c in range(C):
                        mm = pe.matmul(bank_pair(6)[:, kt * P:(kt + 1) * P], a[:, c, b * S + kt * P:b * S + (kt + 1) * P],
                                       wqkv[:, 2, c, :], start=c == 0, stop=c == C - 1)
                mm.then_inc(s["v_ps"], 1)

            def maxima(m, b, first, count):
                for i in range(first, min(first + count, PIECES)):
                    j, qt = divmod(i // 3, QT)
                    if i == 0:
                        pe.wait_ge(s["k_second"], 2 * m + 2)
                    elif i < 3:
                        pe.wait_ge(s["v_ready"], m + 1)
                    else:
                        pe.wait_ge(s["piece_max"], PIECES * m + i - 2)
                    pe.matmul(ps[:, MAX_BANKS[i % 3], 0:PW], q_one[:, b, j, qt * P:(qt + 1) * P],
                              k_one[:, b, j, (i % 3) * PIECE:(i % 3) * PIECE + PW], start=True, stop=True)\
                      .then_inc(s["piece_ps"], 1)

            def rows(m):
                pe.wait_ge(s["nmax_ready"], m + 1)
                pe.transpose(ps[0:UNITS, 7, 0:P], nmax[:, :], consts["ident"][:, :]).then_inc(s["rows_ps"], 1)

            def leave(n, c, q_after=None):
                if c == 0:
                    pe.wait_ge(s["heads_ready"], n + 1)
                    if q_after is not None:
                        pe.wait_ge(s["q_lo"], 2 * q_after + 2)
                else:
                    pe.wait_ge(s["x_added"], 2 * n + 1)
                for blk in range(2):
                    mm = pe.matmul(ps[:, 6 + blk, :], wo[:, c * P:(c + 1) * P], heads[:, blk * BLK:(blk + 1) * BLK],
                                   start=True, stop=True)
                mm.then_inc(s["y_ps"], 1)

            def values(n, b, kt, after=None):
                pe.wait_ge(s["exp_ready"], 4 * KT * n + 4 * kt + 4)
                if kt == 0:
                    wait(pe, s["heads_ready"], n)
                for blk in range(2):
                    for j in range(2):
                        mm = pe.matmul(ps[DH * j:DH * j + DH, 4 + blk, :], v_tok[:, b, kt, DH * j:DH * j + DH],
                                       probs[:, j, kt % RING, blk * BLK:(blk + 1) * BLK],
                                       start=kt == 0, stop=kt == KT - 1)
                        if (blk, j) == (1, 1):
                            mm.then_inc(s["pv_ps"], 1)
                        if after:
                            after()

            def denominators(n):
                pe.wait_ge(s["summed"], 2 * (KT - 1) * n + 2 * (KT - 1))
                pe.wait_ge(s["exp_ready"], 4 * KT * n + 4 * KT)
                for blk in range(2):
                    for j in range(2):
                        mm = pe.matmul(ps[DH * j:DH * j + DH, DEN_BANKS[blk], :], consts["ones"][:, 0:DH],
                                       key_sums[:, j, blk * BLK:(blk + 1) * BLK], start=True, stop=True)
                mm.then_inc(s["den_ps"], 1)

            def prologue(m, b):
                project_q(m, b)
                project_k(m, b)
                project_ctx(m, b)
                project_v(m, b)
                maxima(m, b, 0, PIECES)
                rows(m)

            def body(n, b, first, last):
                m, mb = n + 1, 1 - b
                if b == 1:
                    pe.wait_ge(s["out_loaded"], 8 * n + 8)
                pe.wait_ge(s["row_ready"], 32 * n + 32)
                pe.wait_ge(s["k_second"], 2 * n + 2)
                done = 0

                def more():
                    nonlocal done
                    if not last and kt >= 3 and done < PIECES:
                        maxima(m, mb, done, 1)
                        done += 1
                        if done == PIECES:
                            rows(m)

                for kt in range(KT):
                    kw = P if kt < KT - 1 else CTX
                    for j in range(2):
                        for blk in range(2):
                            cols = slice(blk * BLK, (blk + 1) * BLK)
                            half = 4 * kt + 2 * j + blk
                            if half >= 3:
                                pe.wait_ge(s["exp_ready"], 4 * KT * n + half - 2)
                            else:
                                wait(pe, s["exp_ready"], 4 * KT * n)
                            pe.matmul(ps[0:kw, half % 3, :], k_one[:, b, j, kt * P:kt * P + kw], q_one[:, b, j, cols],
                                      start=True, stop=False)
                            pe.matmul(ps[0:kw, half % 3, :], k_two[:, b, j, kt * P:kt * P + kw], q_two[:, b, j, cols],
                                      start=False, stop=True).then_inc(s["score_ps"], 1)
                            more()
                        if (kt, j) == (0, 0) and not last:
                            project_q(m, mb)
                        if (kt, j) in ((0, 1), (1, 0)) and not first:
                            leave(n - 1, kt, None if last else m)
                        if (kt, j) == (2, 0) and not last:
                            project_k(m, mb)
                            project_ctx(m, mb)
                        if (kt, j) == (2, 1) and not last:
                            project_v(m, mb)
                        if j and kt:
                            values(n, b, kt - 1, more)
                if not last:
                    kt = KT
                    while done < PIECES:
                        more()
                values(n, b, KT - 1)
                if last:
                    pe.wait_ge(s["x_added"], 2 * n)
                denominators(n)
                if last:
                    leave_last(n)

            def leave_last(n):
                pe.wait_ge(s["heads_ready"], n + 1)
                for c in range(C):
                    if c:
                        pe.wait_ge(s["x_added"], 2 * n + 1)
                    for blk in range(2):
                        mm = pe.matmul(ps[:, 6 + blk, :], wo[:, c * P:(c + 1) * P], heads[:, blk * BLK:(blk + 1) * BLK],
                                       start=True, stop=True)
                    mm.then_inc(s["y_ps"], 1)

            pe.wait_ge(s["zeroed"], 7)
            units(pe, body, prologue)

        @block.scalar
        def _(act):
            def q_hi(m, b):
                act.wait_ge(s["q_ps"], m + 1)
                for j in range(2):
                    act.activation(q_one[OWN[j], b, j, :], bank_pair(6)[OWN[j]], ACT.Copy).then_inc(s["q_hi"], 1)

            def k_hi(m, b):
                act.wait_ge(s["k_ps"], m + 1)
                for j in range(2):
                    act.activation(k_one[OWN[j], b, j, 0:S], bank_pair(6)[OWN[j]], ACT.Copy).then_inc(s["k_hi"], 1)

            def ctx_copy(m, b):
                act.wait_ge(s["ctx_ps"], m + 1)
                for j in range(2):
                    act.activation(k_one[OWN[j], b, j, S:KEYS], ps[OWN[j], 3, 0:CTX], ACT.Copy).then_inc(s["ctx_hi"], 1)
                act.activation(v_tok[0:CTX, b, KT - 1, :], ps[0:CTX, 3, P:2 * P], ACT.Copy).then_inc(s["ctx_v"], 1)

            def v_copy(m, b):
                act.wait_ge(s["v_ps"], m + 1)
                act.activation(v_tok[:, b, 0:KT - 1, :], ps[:, 6:8, :].rearrange("p b (t n) -> p (b t) n", n=P),
                               ACT.Copy).then_inc(s["v_ready"], 1)

            def send_rows(m, b):
                act.wait_ge(s["rows_ready"], m + 1)
                for j in range(2):
                    act.dma_start(q_two[AUX[j]:AUX[j] + 1, b, j, :].bitcast(F32).rearrange("o (t n) -> o t n", n=P),
                                  nmax_rows[j * QT:(j + 1) * QT, :].bitcast(F32)).then_inc(s["row_ready"], 16)

            def prologue(m, b):
                q_hi(m, b)
                k_hi(m, b)
                ctx_copy(m, b)
                v_copy(m, b)
                send_rows(m, b)

            def body(n, b, first, last):
                m, mb = n + 1, 1 - b
                for kt in range(KT):
                    kw = P if kt < KT - 1 else CTX
                    for j in range(2):
                        if kt >= RING:
                            act.wait_ge(s["pv_ps"], KT * n + kt - RING + 1)
                            act.wait_ge(s["summed"], 2 * (KT - 1) * n + 2 * max(kt - RING, 1))
                        for blk in range(2):
                            half = 4 * kt + 2 * j + blk
                            act.wait_ge(s["score_ps"], 4 * KT * n + half + 1)
                            act.activation(probs[0:kw, j, kt % RING, blk * BLK:(blk + 1) * BLK], ps[0:kw, half % 3, :],
                                           ACT.Exp, scale=1.0 / 8.0).then_inc(s["exp_ready"], 1)
                        if last:
                            continue
                        if (kt, j) == (0, 0):
                            q_hi(m, mb)
                        if (kt, j) == (2, 0):
                            k_hi(m, mb)
                            ctx_copy(m, mb)
                        if (kt, j) == (2, 1):
                            v_copy(m, mb)
                if not last:
                    send_rows(m, mb)
                act.wait_ge(s["den_ps"], n + 1)
                for blk in range(2):
                    act.activation(logden[:, blk * BLK:(blk + 1) * BLK], ps[:, DEN_BANKS[blk], :],
                                   ACT.Ln).then_inc(s["logden_ready"], 1)
                act.wait_ge(s["logden_ready"], 2 * n + 2)
                act.activation(rden[:, :], logden[:, :], ACT.Exp, scale=-1.0).then_inc(s["rden_ready"], 1)

            act.wait_ge(s["zeroed"], 7)
            units(act, body, prologue)

        @block.vector
        def _(dve):
            def prepare_q(m, b):
                for j in range(2):
                    dve.wait_ge(s["q_hi"], 2 * m + j + 1)
                    dve.tensor_tensor(q_two[OWN[j], b, j, :], bank_pair(6)[OWN[j]], q_one[OWN[j], b, j, :].bitcast(F32),
                                      ALU.subtract).then_inc(s["q_lo"], 1)
                for j in range(2):
                    dve.tensor_copy(q_one[OTHER[j], b, j, :], q_one[OWN[j], b, j, :].bitcast(F32)).then_inc(s["q_dup"], 1)

            def prepare_k(m, b):
                for j in range(2):
                    dve.wait_ge(s["k_hi"], 2 * m + j + 1)
                    dve.tensor_tensor(k_one[OTHER[j], b, j, 0:S], bank_pair(6)[OWN[j]], k_one[OWN[j], b, j, 0:S].bitcast(F32),
                                      ALU.subtract).then_inc(s["k_lo"], 1)
                dve.wait_ge(s["ctx_v"], m + 1)
                for j in range(2):
                    dve.wait_ge(s["ctx_hi"], 2 * m + j + 1)
                    dve.tensor_tensor(k_one[OTHER[j], b, j, S:KEYS], ps[OWN[j], 3, 0:CTX],
                                      k_one[OWN[j], b, j, S:KEYS].bitcast(F32), ALU.subtract).then_inc(s["ctx_lo"], 1)
                for j in range(2):
                    dve.tensor_copy(k_two[OWN[j], b, j, 0:KEYS], k_one[OWN[j], b, j, 0:KEYS].bitcast(F32)).then_inc(s["k_second"], 1)
                for i in range(PIECES):
                    dve.wait_ge(s["piece_ps"], PIECES * m + i + 1)
                    dve.tensor_reduce(part_max[:, i // 3, i % 3:i % 3 + 1], ps[:, MAX_BANKS[i % 3], 0:PIECE], AX.X,
                                      ALU.max).then_inc(s["piece_max"], 1)
                dve.wait_ge(s["piece_max"], PIECES * m + PIECES)
                dve.tensor_reduce(nmax[:, :], part_max[:, :, :], AX.X, ALU.max, negate=True).then_inc(s["nmax_ready"], 1)
                wait(dve, s["row_ready"], 32 * m)
                dve.wait_ge(s["rows_ps"], m + 1)
                dve.tensor_copy(nmax_rows[:, :], ps[0:UNITS, 7, 0:P]).then_inc(s["rows_ready"], 1)

            def add(n, b, c):
                dve.wait_ge(s["y_ps"], 2 * n + c + 1)
                part = x[:, c, b * S:(b + 1) * S]
                dve.tensor_tensor(part, part, bank_pair(6), ALU.add).then_inc(s["x_added"], 1)

            def body(n, b, first, last):
                if not last:
                    prepare_q(n + 1, 1 - b)
                if not first:
                    for c in range(C):
                        add(n - 1, 1 - b, c)
                if not last:
                    prepare_k(n + 1, 1 - b)
                dve.wait_ge(s["rden_ready"], n + 1)
                dve.wait_ge(s["pv_ps"], KT * n + KT)
                dve.tensor_tensor(heads[:, :], bank_pair(4), rden[:, :], ALU.mult).then_inc(s["heads_ready"], 1)
                if last:
                    for c in range(C):
                        add(n, b, c)
                    dve.wait_ge(s["x_added"], 2 * n + 2)

            def prologue(m, b):
                prepare_q(m, b)
                prepare_k(m, b)

            for buf in (q_two, k_one, k_two, v_tok):
                dve.memset(buf[:, :, :, :] if buf is v_tok else buf[:, :, :, :].bitcast(F32), 0.0).then_inc(s["zeroed"], 1)
            dve.wait_ge(s["zeroed"], 4)
            for j in range(2):
                dve.memset(k_two[AUX[j]:AUX[j] + 1, :, j, :].bitcast(F32), 1.0).then_inc(s["zeroed"], 1)
            dve.memset(part_max[:, :, :], 0.0).then_inc(s["zeroed"], 1)
            dve.wait_ge(s["zeroed"], 7)
            units(dve, body, prologue)

        @block.gpsimd
        def _(pool):
            def body(n, b, first, last):
                for kt in range(1, KT):
                    kw = P if kt < KT - 1 else CTX
                    for j in range(2):
                        pool.wait_ge(s["exp_ready"], 4 * KT * n + 4 * kt + 2 * j + 2)
                        if kt == 1:
                            before = probs[:, j, 0, :]
                            wait(pool, s["den_ps"], n)
                        else:
                            before = key_sums[0:kw, j, :]
                            pool.wait_ge(s["summed"], 2 * (KT - 1) * n + 2 * (kt - 2) + j + 1)
                        pool.tensor_tensor(key_sums[0:kw, j, :], before, probs[0:kw, j, kt % RING, :],
                                           ALU.add).then_inc(s["summed"], 1)

            units(pool, body)


def chain(engine, sem):
    count = [0]

    def step(instruction):
        count[0] += 1
        instruction.then_inc(sem, 1)
        engine.wait_ge(sem, count[0])
    return step


def top_experts(dve, step, order, score, left, index, keep, first, onehots, tops):
    wide = [P, TILES, E]
    for k, hot in enumerate(onehots):
        src = left if k else score
        step(dve.tensor_reduce(tops[k], src[:, :, :], AX.X, ALU.max))
        step(dve.tensor_tensor(index[:, :, :], src[:, :, :], tops[k].unsqueeze(2).broadcast_to(wide), ALU.is_equal))
        step(dve.tensor_tensor(index[:, :, :], index[:, :, :], order[:, :].unsqueeze(1).broadcast_to(wide), ALU.mult))
        step(dve.tensor_reduce(first, index[:, :, :], AX.X, ALU.max))
        step(dve.tensor_tensor(hot[:, :, :], index[:, :, :], first.unsqueeze(2).broadcast_to(wide), ALU.is_equal))
        if k + 1 < len(onehots):
            step(dve.tensor_scalar(keep[:, :, :], hot[:, :, :], -1.0, 1.0, ALU.mult, ALU.add))
            step(dve.tensor_tensor(index[:, :, :], score[:, :, :], keep[:, :, :], ALU.mult))
            step(dve.tensor_scalar(keep[:, :, :], hot[:, :, :], -3.0e38, None, ALU.mult))
            step(dve.tensor_tensor(left[:, :, :], index[:, :, :], keep[:, :, :], ALU.add))


def router_stage(nc, stage, kind, consts, y, router_w, bias, small, order, temperature, gates_t, gates_dram, weights):
    G = B * E
    wide = [P, TILES, E]
    with ExitStack() as stack:
        sc = Scope(nc, stack, stage)
        score, left, index, keep, gates, expd = (sc.sb(n, wide) for n in ("score", "left", "index", "keep", "gates", "expd"))
        hot = [sc.sb(f"hot{k}", wide) for k in range(1 if kind == "top1" else 2)]
        rowv = sc.sb("rowv", [P, 8, TILES])
        colv = sc.sb("colv", [P, 5, G])
        temp = sc.sb("temp", [P, 2])
        ps = sc.psum()
        small_loaded, logits_ps, dve_step = sc.sem("small_loaded"), sc.sem("logits_ps"), sc.sem("dve_step")
        act_asked, act_done = sc.sem("act_asked"), sc.sem("act_done")
        maxima_ready, maxima_all = sc.sem("maxima_ready"), sc.sem("maxima_all")
        sums_ready, sums_all = sc.sem("sums_ready"), sc.sem("sums_all")
        gates_ready, turned_ps, gates_copied, stored = (sc.sem(n) for n in ("gates_ready", "turned_ps", "gates_copied", "stored"))
        rounds = 3 if kind == "sinkhorn" else 0
        block = stack.enter_context(nc.Block())

        @block.sync
        def _(sp):
            for dst, src in small:
                sp.dma_start(dst, src).then_inc(small_loaded, 16)
            for dst, src, loaded in weights:
                sp.dma_start(dst, src).then_inc(loaded, 16)
            sp.wait_ge(gates_copied, 1)
            sp.dma_start(gates_dram, gates_t[:, :]).then_inc(stored, 16)
            sp.wait_ge(stored, 16)

        @block.tensor
        def _(pe):
            pe.wait_ge(small_loaded, 16 * len(small))
            for t in range(TILES):
                for c in range(C):
                    mm = pe.matmul(ps[:, 0, t * E:(t + 1) * E], y[:, c, t * P:(t + 1) * P], router_w[:, c, :],
                                   start=c == 0, stop=c == C - 1)
            mm.then_inc(logits_ps, 1)
            for r in range(rounds):
                pe.wait_ge(sums_ready, r + 1)
                pe.matmul(ps[:, 1, 0:G], consts["ones"][:, :], colv[:, 3, :], start=True, stop=True).then_inc(sums_all, 1)
            pe.wait_ge(gates_ready, 1)
            for t in range(TILES):
                mm = pe.transpose(ps[0:E, 4 + t // 4, (t % 4) * P:(t % 4 + 1) * P], gates[:, t, :], consts["ident"][:, :])
            mm.then_inc(turned_ps, 1)

        @block.vector
        def _(dve):
            step = chain(dve, dve_step)
            asked = [0]

            def act_does():
                asked[0] += 1
                dve.sem_inc(act_asked, 1)
                dve.wait_ge(act_done, asked[0])

            def per_token(v):
                return v.unsqueeze(2).broadcast_to(wide)

            def by_expert(v):
                return v.rearrange("p (b t) e -> p b e t", b=B)

            def per_expert(v):
                return v.rearrange("p (b e) -> p b e", b=B).unsqueeze(3).broadcast_to([P, B, E, TILES // B])

            def grouped(v):
                return v.rearrange("p (b e) -> p b e", b=B)

            dve.wait_ge(small_loaded, 16 * len(small))
            dve.wait_ge(logits_ps, 1)
            logits = ps[:, 0, 0:TILES * E].rearrange("p (t e) -> p t e", e=E)
            if bias is not None:
                step(dve.tensor_tensor(score[:, :, :], logits, bias.unsqueeze(1).broadcast_to(wide), ALU.add))
            else:
                step(dve.tensor_copy(score[:, :, :], logits))
            if kind == "sinkhorn":
                s4 = by_expert(score[:, :, :])
                step(dve.tensor_scalar(temp[:, 0:1], temperature, 0.1, None, ALU.max))
                step(dve.reciprocal(temp[:, 1:2], temp[:, 0:1]))
                step(dve.tensor_scalar(score[:, :, :], score[:, :, :], temp[:, 1:2], None, ALU.mult))
                for r in range(rounds):
                    step(dve.tensor_reduce(rowv[:, 0, :], score[:, :, :], AX.X, ALU.max))
                    step(dve.tensor_tensor(score[:, :, :], score[:, :, :], per_token(rowv[:, 0, :]), ALU.subtract))
                    act_does()
                    step(dve.tensor_reduce(rowv[:, 1, :], expd[:, :, :], AX.X, ALU.add))
                    act_does()
                    step(dve.tensor_tensor(score[:, :, :], score[:, :, :], per_token(rowv[:, 2, :]), ALU.subtract))
                    step(dve.tensor_reduce(grouped(colv[:, 0, :]), s4, AX.X, ALU.max))
                    dve.sem_inc(maxima_ready, 1)
                    dve.wait_ge(maxima_all, r + 1)
                    step(dve.tensor_tensor(s4, s4, per_expert(colv[:, 1, :]), ALU.subtract))
                    act_does()
                    step(dve.tensor_reduce(grouped(colv[:, 3, :]), by_expert(expd[:, :, :]), AX.X, ALU.add))
                    dve.sem_inc(sums_ready, 1)
                    dve.wait_ge(sums_all, r + 1)
                    act_does()
                    step(dve.tensor_tensor(s4, s4, per_expert(colv[:, 4, :]), ALU.subtract))
                act_does()
                step(dve.tensor_reduce(rowv[:, 3, :], expd[:, :, :], AX.X, ALU.add))
                step(dve.tensor_scalar(rowv[:, 3, :], rowv[:, 3, :], 1e-8, None, ALU.add))
                step(dve.reciprocal(rowv[:, 4, :], rowv[:, 3, :]))
                step(dve.tensor_tensor(score[:, :, :], expd[:, :, :], per_token(rowv[:, 4, :]), ALU.mult))
            tops = [rowv[:, 5, :], rowv[:, 6, :]]
            top_experts(dve, step, order, score, left, index, keep, rowv[:, 7, :], hot, tops)
            if kind == "top1":
                dve.tensor_copy(gates[:, :, :], hot[0][:, :, :]).then_inc(gates_ready, 1)
                return
            if kind == "top2":
                step(dve.tensor_tensor(rowv[:, 0, :], tops[1], tops[0], ALU.subtract))
                act_does()
                step(dve.tensor_scalar(rowv[:, 2, :], rowv[:, 1, :], 1.0, None, ALU.add))
                step(dve.reciprocal(rowv[:, 3, :], rowv[:, 2, :]))
                step(dve.tensor_tensor(rowv[:, 4, :], rowv[:, 1, :], rowv[:, 3, :], ALU.mult))
            else:
                step(dve.tensor_tensor(rowv[:, 0, :], tops[1], tops[0], ALU.add))
                step(dve.tensor_scalar(rowv[:, 1, :], rowv[:, 0, :], 1e-8, None, ALU.add))
                step(dve.reciprocal(rowv[:, 2, :], rowv[:, 1, :]))
                step(dve.tensor_tensor(rowv[:, 3, :], tops[0], rowv[:, 2, :], ALU.mult))
                step(dve.tensor_tensor(rowv[:, 4, :], tops[1], rowv[:, 2, :], ALU.mult))
            for k in range(2):
                step(dve.tensor_tensor(hot[k][:, :, :], hot[k][:, :, :], per_token(rowv[:, 3 + k, :]), ALU.mult))
            dve.tensor_tensor(gates[:, :, :], hot[0][:, :, :], hot[1][:, :, :], ALU.add).then_inc(gates_ready, 1)

        @block.scalar
        def _(act):
            def answer(n, out, in_, func):
                act.wait_ge(act_asked, n)
                act.activation(out, in_, func).then_inc(act_done, 1)

            for r in range(rounds):
                answer(4 * r + 1, expd[:, :, :], score[:, :, :], ACT.Exp)
                answer(4 * r + 2, rowv[:, 2, :], rowv[:, 1, :], ACT.Ln)
                answer(4 * r + 3, expd[:, :, :], score[:, :, :], ACT.Exp)
                answer(4 * r + 4, colv[:, 4, :], ps[:, 1, 0:G], ACT.Ln)
            if kind == "sinkhorn":
                answer(4 * rounds + 1, expd[:, :, :], score[:, :, :], ACT.Exp)
            if kind == "top2":
                answer(1, rowv[:, 1, :], rowv[:, 0, :], ACT.Exp)
            act.wait_ge(turned_ps, 1)
            act.activation(gates_t[:, :], ps[0:E, 4:8, :].rearrange("p b n -> p (b n)"), ACT.Copy).then_inc(gates_copied, 1)

        if rounds:
            @block.gpsimd
            def _(pool):
                for r in range(rounds):
                    pool.wait_ge(maxima_ready, r + 1)
                    pool.partition_all_reduce(colv[:, 1, :], colv[:, 0, :], P, bass.bass_isa.ReduceOp.max).then_inc(maxima_all, 1)


def experts_stage(nc, stage, func, x, y, hidden, w_in, w_out, b_in, b_out, gates_t, gates_dram, raw_in, raw_out,
                  raw_loaded, plus):
    MC = hidden // P
    pairs = w_in.shape[2]
    PARTS = pairs + 1
    STEPS = NBLK * MC
    NS, NH = 2, 4
    CREDIT = 4
    with ExitStack() as stack:
        sc = Scope(nc, stack, stage)
        y_hi = sc.sb("y_hi", [P, C, T], F32R)
        y_lo = sc.sb("y_lo", [P, C, T], F32R)
        in_split = sc.sb("in_split", [P, 2, 2, pairs, C, hidden], F32R)
        out_split = sc.sb("out_split", [P, 2, 2, MC, D], F32R)
        gate = sc.sb("gate", [P, 2, T])
        bias_in = sc.sb("bias_in", [P, 2, MC]) if b_in is not None else None
        GATE_LOADS = 16 if b_in is None else 32
        active = sc.sb("active", [P, NS, BLK])
        product = sc.sb("product", [P, NS, BLK]) if pairs == 2 else active
        gated = sc.sb("gated", [P, NS, BLK])
        split = sc.sb("split", [P, NH, 2, BLK], F32R)
        ps = sc.psum()
        s = {n: sc.sem(n) for n in """hidden_ps active_ready product_ready gated_ready hi_ready lo_ready out_ps x_added
             y_hi_ready y_lo_ready w_hi_ready w_lo_ready plus_added""".split()}
        gate_loaded = [sc.sem(f"gate_loaded{u}") for u in range(2)]
        if pairs == 1:
            s["product_ready"] = s["active_ready"]
        with nc.Block() as starting:
            @starting.vector
            def _(dve):
                for name in ["active_ready", "gated_ready", "lo_ready", "out_ps", "x_added"] + ["product_ready"] * (pairs == 2):
                    dve.sem_inc(s[name], CREDIT)

        block = stack.enter_context(nc.Block())

        def after(engine, name, n, more=0):
            engine.wait_ge(s[name], n + (more + CREDIT))

        def blocks_of(t):
            return slice(t * BLK, (t + 1) * BLK)

        def experts(engine, body):
            with engine.Fori(0, E // 2 - 1) as g:
                for u in range(2):
                    body(2 * g + u, u, False)
            for u in range(2):
                body(E - 2 + u, u, u == 1)

        def splits(e, u, q):
            return [q // 2 - 1] if q % 2 == 0 and 0 <= q // 2 - 1 < PARTS else []

        def part_of(j, raw, u=None, which=None):
            if raw:
                return (raw_in[:, j] if j < pairs else raw_out[:, :, :])
            return in_split[:, u, which, j] if j < pairs else out_split[:, u, which]

        @block.sync
        def _(sp):
            def load_weights(e):
                sp.dma_start(raw_in[:, :, :, :], w_in[e].rearrange("o p i c n -> p (o i) c n")).then_inc(raw_loaded, 16)
                sp.dma_start(raw_out[:, :, :], w_out[e].rearrange("o p m n -> p (o m) n")).then_inc(raw_loaded, 16)

            def load_gates(e, u):
                sp.dma_start(gate[:, u, :], gates_dram[e].broadcast_to([P, T])).then_inc(gate_loaded[u], 16)
                if b_in is not None:
                    sp.dma_start(bias_in[:, u, :], b_in[e].rearrange("o p m -> p (o m)")).then_inc(gate_loaded[u], 16)

            for u in range(2):
                load_gates(slice(u, u + 1), u)
            sp.wait_ge(s["w_lo_ready"], PARTS)
            load_weights(slice(1, 2))
            with sp.Fori(0, E // 2 - 1) as g:
                for u in range(2):
                    sp.wait_ge(s["w_lo_ready"], PARTS * (2 * g + u + 2))
                    load_weights(bass.ds(2 * g + u + 2, 1))
                    after(sp, "gated_ready", STEPS * (2 * g + u + 1))
                    load_gates(bass.ds(2 * g + u + 2, 1), u)

        @block.tensor
        def _(pe):
            def into_hidden(e, u, q):
                t, m = divmod(q, MC)
                if q == 0:
                    pe.wait_ge(s["w_lo_ready"], PARTS * (e + 1))
                if m == 0:
                    pe.wait_ge(s["y_lo_ready"], t + 1)
                after(pe, "product_ready", STEPS * e, q - 1)
                for i in range(pairs):
                    k = 0
                    for w_part, y_part in ((0, y_hi), (0, y_lo), (1, y_hi)):
                        for c in range(C):
                            mm = pe.matmul(ps[:, pairs * (q % 2) + i, :], in_split[:, u, w_part, i, c, m * P:(m + 1) * P],
                                           y_part[:, c, blocks_of(t)], start=k == 0, stop=k == 3 * C - 1)
                            k += 1
                mm.then_inc(s["hidden_ps"], 1)

            def out(e, u, q, last):
                t, m = divmod(q, MC)
                after(pe, "lo_ready", STEPS * e, q + 1)
                if m == 0:
                    after(pe, "x_added", NBLK * e, t - 1)
                for c in range(C):
                    bank = ps[:, 4 + 2 * (t % 2) + c, :]
                    with_bias = last and m == 0 and b_out is not None
                    if with_bias:
                        pe.matmul(bank, b_out[:, c * P:(c + 1) * P], gates_t[:, blocks_of(t)], start=True, stop=False)
                    for k, (w_part, h_part) in enumerate(((0, 0), (0, 1), (1, 0))):
                        mm = pe.matmul(bank, out_split[:, u, w_part, m, c * P:(c + 1) * P], split[:, q % NH, h_part, :],
                                       start=m == 0 and k == 0 and not with_bias, stop=m == MC - 1 and k == 2)
                mm.then_inc(s["out_ps"], 1)

            def body(e, u, last):
                for q in range(STEPS):
                    if q + 2 < STEPS:
                        into_hidden(e, u, q + 2)
                    elif not last:
                        into_hidden(e + 1, 1 - u, q + 2 - STEPS)
                    out(e, u, q, last)

            into_hidden(0, 0, 0)
            into_hidden(0, 0, 1)
            experts(pe, body)

        @block.scalar
        def _(act):
            def activate(e, u, q):
                m = q % MC
                act.wait_ge(s["hidden_ps"], STEPS * e + q + 1)
                after(act, "product_ready" if pairs == 2 else "gated_ready", STEPS * e, q - 1)
                bias = 0.0
                if b_in is not None:
                    bias = bias_in[:, u, m:m + 1]
                    if q == 0:
                        act.wait_ge(gate_loaded[u], 16 * e + (GATE_LOADS - 16 * u))
                act.activation(active[:, q % NS, :], ps[:, pairs * (q % 2), :], func, bias=bias).then_inc(s["active_ready"], 1)

            def hi(e, q):
                after(act, "gated_ready", STEPS * e, q + 1)
                after(act, "out_ps", STEPS * e, q + 1 - NH)
                act.activation(split[:, q % NH, 0, :], gated[:, q % NS, :], ACT.Copy).then_inc(s["hi_ready"], 1)

            def weights_hi(e, u, j):
                act.activation(part_of(j, False, u, 0), part_of(j, True), ACT.Copy).then_inc(s["w_hi_ready"], 1)

            def body(e, u, last):
                for q in range(STEPS):
                    if q + 1 < STEPS:
                        activate(e, u, q + 1)
                    elif not last:
                        activate(e + 1, 1 - u, 0)
                    hi(e, q)
                    for j in splits(e, u, q) if not last else []:
                        if j == 0:
                            act.wait_ge(raw_loaded, 32 * (e + 1) + 32)
                            after(act, "out_ps", STEPS * e)
                        weights_hi(e + 1, 1 - u, j)

            act.wait_ge(raw_loaded, 32)
            for j in range(PARTS):
                weights_hi(0, 0, j)
            for t in range(NBLK):
                act.activation(y_hi[:, :, blocks_of(t)], y[:, :, blocks_of(t)], ACT.Copy).then_inc(s["y_hi_ready"], 1)
            activate(0, 0, 0)
            experts(act, body)

        @block.vector
        def _(dve):
            def multiply(e, q):
                after(dve, "active_ready", STEPS * e, q + 1)
                after(dve, "gated_ready", STEPS * e, q - 1)
                dve.tensor_tensor(product[:, q % NS, :], active[:, q % NS, :], ps[:, pairs * (q % 2) + 1, :],
                                  ALU.mult).then_inc(s["product_ready"], 1)

            def lo(e, q):
                dve.wait_ge(s["hi_ready"], STEPS * e + q + 1)
                dve.tensor_tensor(split[:, q % NH, 1, :], gated[:, q % NS, :], split[:, q % NH, 0, :].bitcast(F32),
                                  ALU.subtract).then_inc(s["lo_ready"], 1)

            def weights_lo(e, u, j):
                dve.wait_ge(s["w_hi_ready"], PARTS * e + j + 1)
                dve.tensor_tensor(part_of(j, False, u, 1), part_of(j, True), part_of(j, False, u, 0).bitcast(F32),
                                  ALU.subtract).then_inc(s["w_lo_ready"], 1)

            def body(e, u, last):
                for q in range(STEPS):
                    t, m = divmod(q, MC)
                    if pairs == 2:
                        if q + 1 < STEPS:
                            multiply(e, q + 1)
                        elif not last:
                            multiply(e + 1, 0)
                    lo(e, q)
                    for j in splits(e, u, q) if not last else []:
                        weights_lo(e + 1, 1 - u, j)
                    if m == MC - 1:
                        after(dve, "out_ps", STEPS * e, q + 1)
                        part = x[:, :, blocks_of(t)]
                        dve.tensor_tensor(part, part, ps[:, 4 + 2 * (t % 2):6 + 2 * (t % 2), :], ALU.add).then_inc(s["x_added"], 1)

            for j in range(PARTS):
                weights_lo(0, 0, j)
            for t in range(NBLK):
                cells = (slice(None), slice(None), blocks_of(t))
                for more in plus:
                    dve.tensor_tensor(x[cells], x[cells], more[cells], ALU.add).then_inc(s["plus_added"], 1)
                dve.wait_ge(s["y_hi_ready"], t + 1)
                dve.tensor_tensor(y_lo[cells], y[cells], y_hi[cells].bitcast(F32), ALU.subtract).then_inc(s["y_lo_ready"], 1)
            if pairs == 2:
                multiply(0, 0)
            experts(dve, body)
            after(dve, "x_added", NBLK * E)

        @block.gpsimd
        def _(pool):
            with pool.Fori(0, E // 2) as g:
                for u in range(2):
                    e = 2 * g + u
                    pool.wait_ge(gate_loaded[u], GATE_LOADS * (g + 1))
                    for q in range(STEPS):
                        after(pool, "product_ready", STEPS * e, q + 1)
                        after(pool, "lo_ready", STEPS * e, q - 1)
                        pool.tensor_tensor(gated[:, q % NS, :], product[:, q % NS, :], gate[:, u, blocks_of(q // MC)],
                                           ALU.mult).then_inc(s["gated_ready"], 1)


def moe(nc, name, kind, func, hidden, consts, x, y, t, plus):
    with ExitStack() as stack:
        sc = Scope(nc, stack, name)
        w_in, w_out = t[f"{name}_w_in"], t[f"{name}_w_out"]
        raw_in = sc.sb("raw_in", [P, w_in.shape[2], C, hidden])
        raw_out = sc.sb("raw_out", [P, hidden // P, D])
        raw_loaded = sc.sem("raw_loaded")
        weights = [(raw_in[:, :, :, :], w_in[0], raw_loaded), (raw_out[:, :, :], w_out[0], raw_loaded)]
        router_w = sc.sb("router_w", [P, C, E])
        order = sc.sb("order", [P, E])
        small = [(router_w[:, :, :], t[f"{name}_router_w"]), (order[:, :], t["c_order"])]
        bias = temperature = b_in = b_out = None
        if f"{name}_router_b" in t:
            bias_t = sc.sb("router_b", [P, E])
            small.append((bias_t[:, :], t[f"{name}_router_b"]))
            bias = bias_t[:, :]
        if kind == "sinkhorn":
            temp_t = sc.sb("temperature", [P, 1])
            small.append((temp_t[:, :], t[f"{name}_temperature"]))
            temperature = temp_t[:, 0:1]
        if f"{name}_b_in" in t:
            b_in = t[f"{name}_b_in"]
            b_out = sc.sb("b_out", [E, D])
            small.append((b_out[:, :], t[f"{name}_b_out"]))
        gates_t = sc.sb("gates_t", [E, T])
        gates_dram = t["scratch_gates_" + name]
        router_stage(nc, name + "r", kind, consts, y, router_w, bias, small, order, temperature, gates_t, gates_dram, weights)
        experts_stage(nc, name + "e", func, x, y, hidden, w_in, w_out, b_in, b_out, gates_t, gates_dram, raw_in, raw_out,
                      raw_loaded, plus)


def context_attention(nc, name, consts, x, y, ctx, t):
    HG, DH = 8, 16
    GK = HG * CTX
    HALF = GK // 2
    CH = [(k * P, min(P, GK - k * P)) for k in range(-(-GK // P))]
    FULL = len(CH) - 1
    SHORT = CH[-1][1]
    TB = BLK // P

    def slot(g, i):
        return g * FULL + i if i < FULL else C * FULL + g

    with ExitStack() as stack:
        sc = Scope(nc, stack, name)
        w = {k: sc.sb(k, [P, C, D]) for k in ("wq", "wk", "wv", "wo")}
        bias = {k: sc.sb(k, [P, C]) for k in ("bq", "bk", "bv", "bo")}
        mask = sc.sb("mask", [P, HG])
        q = sc.sb("q", [P, C, T])
        k_feat, v_feat = sc.sb("k_feat", [P, C, B * CTX]), sc.sb("v_feat", [P, C, B * CTX])
        k_spread, v_spread = sc.sb("k_spread", [P, B, C, GK]), sc.sb("v_spread", [P, B, C, GK])
        v_rows = sc.sb("v_rows", [P, B, C, len(CH), P])
        with ExitStack() as setup:
            ss = Scope(nc, setup, name + "s")
            ps = ss.psum()
            loaded, kv_ps, kv_ready, spread_ready, turned_ps, turned, q_ps, q_ready = (
                ss.sem(n) for n in "loaded kv_ps kv_ready spread_ready turned_ps turned q_ps q_ready".split())
            loads = [(v[:, :, :], t[f"{name}_{k}"]) for k, v in w.items()] + \
                    [(v[:, :], t[f"{name}_{k}"]) for k, v in bias.items()] + [(mask[:, :], t["c_head_mask"])]
            block = setup.enter_context(nc.Block())

            @block.sync
            def _(sp):
                for dst, src in loads:
                    sp.dma_start(dst, src).then_inc(loaded, 16)
                sp.wait_ge(loaded, 16 * len(loads))

            @block.tensor
            def _(pe):
                pe.wait_ge(loaded, 16 * len(loads))
                for i, m in enumerate(("wk", "wv")):
                    for g in range(C):
                        for c in range(C):
                            mm = pe.matmul(ps[:, i, g * B * CTX:(g + 1) * B * CTX], w[m][:, c, g * P:(g + 1) * P],
                                           ctx[:, c, :], start=c == 0, stop=c == C - 1)
                    mm.then_inc(kv_ps, 1)
                for n in range(NBLK * C):
                    blk, g = divmod(n, C)
                    if n >= 4:
                        pe.wait_ge(q_ready, n - 3)
                    for c in range(C):
                        mm = pe.matmul(ps[:, 2 + n % 4, :], w["wq"][:, c, g * P:(g + 1) * P],
                                       y[:, c, blk * BLK:(blk + 1) * BLK], start=c == 0, stop=c == C - 1)
                    mm.then_inc(q_ps, 1)
                for n in range(B * C):
                    b, g = divmod(n, C)
                    pe.wait_ge(spread_ready, 2 * n + 2)
                    if n:
                        pe.wait_ge(turned, 2 * n)
                    for k, (r0, rows) in enumerate(CH):
                        mm = pe.transpose(ps[0:rows, 6 + k // 4, (k % 4) * P:(k % 4 + 1) * P],
                                          v_spread[:, b, g, r0:r0 + rows], consts["ident"][:, :])
                    mm.then_inc(turned_ps, 1)

            @block.scalar
            def _(act):
                for i, (dst, bv) in enumerate(((k_feat, "bk"), (v_feat, "bv"))):
                    act.wait_ge(kv_ps, i + 1)
                    for g in range(C):
                        act.activation(dst[:, g, :], ps[:, i, g * B * CTX:(g + 1) * B * CTX], ACT.Identity,
                                       bias=bias[bv][:, g:g + 1]).then_inc(kv_ready, 1)
                for n in range(NBLK * C):
                    blk, g = divmod(n, C)
                    act.wait_ge(q_ps, n + 1)
                    act.activation(q[:, g, blk * BLK:(blk + 1) * BLK], ps[:, 2 + n % 4, :], ACT.Identity,
                                   bias=bias["bq"][:, g:g + 1]).then_inc(q_ready, 1)

            @block.vector
            def _(dve):
                dve.wait_ge(kv_ready, 4)
                for b in range(B):
                    for g in range(C):
                        for dst, src in ((k_spread, k_feat), (v_spread, v_feat)):
                            dve.tensor_tensor(dst[:, b, g, :].rearrange("p (h k) -> p h k", h=HG),
                                              src[:, g, b * CTX:(b + 1) * CTX].unsqueeze(1).broadcast_to([P, HG, CTX]),
                                              mask[:, :].unsqueeze(2).broadcast_to([P, HG, CTX]),
                                              ALU.mult).then_inc(spread_ready, 1)
                for n in range(B * C):
                    b, g = divmod(n, C)
                    dve.wait_ge(turned_ps, n + 1)
                    dve.tensor_copy(v_rows[:, b, g, 0:4, :], ps[:, 6, :].rearrange("p (k n) -> p k n", n=P)).then_inc(turned, 1)
                    rows = CH[4][1]
                    dve.tensor_copy(v_rows[0:rows, b, g, 4, :], ps[0:rows, 7, 0:P]).then_inc(turned, 1)

        with ExitStack() as main:
            ms = Scope(nc, main, name + "m")
            NK = C * len(CH)
            diff = ms.sb("diff", [P, 2, C, GK])
            expd = ms.sb("expd", [P, 2, C, GK])
            probs = ms.sb("probs", [P, 2, C, GK])
            probs_t = ms.sb("probs_t", [P, 2, NK, BLK])
            attended = ms.sb("attended", [P, 2, C, BLK])
            top, total, share = (ms.sb(n, [P, 2, 2 * C, HG // 2]) for n in ("top", "total", "share"))
            ps = ms.psum()
            names = """score_ps top_ready diff_ready exp_ready sum_ready share_ready probs_ready turned_ps turned
                       out_ps out_ready y_ps x_added"""
            s = {n: ms.sem(n) for n in names.split()}
            block = main.enter_context(nc.Block())
            by_head = [P, 2 * C, HG // 2, CTX]

            def heads_of(buf, n):
                return buf[:, n % 2].rearrange("p g (a h k) -> p (g a) h k", a=2, h=HG // 2)

            @block.tensor
            def _(pe):
                def scores(n):
                    if n:
                        pe.wait_ge(s["diff_ready"], n)
                    for i in range(2 * C):
                        mm = pe.matmul(ps[:, i, 0:HALF], q[:, i // 2, n * P:(n + 1) * P],
                                       k_spread[:, n * P // S, i // 2, (i % 2) * HALF:(i % 2 + 1) * HALF],
                                       start=True, stop=True)
                    mm.then_inc(s["score_ps"], 1)

                scores(0)
                for n in range(TILES):
                    if n + 1 < TILES:
                        scores(n + 1)
                    pe.wait_ge(s["probs_ready"], n + 1)
                    if n:
                        pe.wait_ge(s["turned"], 2 * n)
                    for k in range(NK):
                        g, i = divmod(k, len(CH))
                        r0, rows = CH[i]
                        k = slot(g, i)
                        mm = pe.transpose(ps[0:rows, 4 + k // 4, (k % 4) * P:(k % 4 + 1) * P],
                                          probs[:, n % 2, g, r0:r0 + rows], consts["ident"][:, :])
                    mm.then_inc(s["turned_ps"], 1)
                    if n % TB != TB - 1:
                        continue
                    blk = n // TB
                    pe.wait_ge(s["turned"], 2 * n + 2)
                    for g in range(C):
                        if g:
                            pe.wait_ge(s["out_ready"], C * blk + g)
                        elif blk:
                            pe.wait_ge(s["x_added"], C * blk)
                        for i, (r0, rows) in enumerate(CH):
                            mm = pe.matmul(ps[:, 7, :], v_rows[0:rows, n * P // S, g, i, :],
                                           probs_t[0:rows, blk % 2, slot(g, i), :], start=i == 0, stop=i == len(CH) - 1)
                        mm.then_inc(s["out_ps"], 1)
                    pe.wait_ge(s["out_ready"], C * blk + C)
                    for c in range(C):
                        if c:
                            pe.wait_ge(s["x_added"], C * blk + c)
                        for g in range(C):
                            mm = pe.matmul(ps[:, 7, :], w["wo"][:, g, c * P:(c + 1) * P], attended[:, blk % 2, g, :],
                                           start=g == 0, stop=g == C - 1)
                        mm.then_inc(s["y_ps"], 1)

            @block.vector
            def _(dve):
                def before_exp(n):
                    dve.wait_ge(s["score_ps"], n + 1)
                    banks = ps[:, 0:2 * C, 0:HALF].rearrange("p a (h k) -> p a h k", k=CTX)
                    if n >= 2:
                        dve.wait_ge(s["exp_ready"], n - 1)
                    dve.tensor_reduce(top[:, n % 2], banks, AX.X, ALU.max).then_inc(s["top_ready"], 1)
                    dve.wait_ge(s["top_ready"], n + 1)
                    dve.tensor_tensor(heads_of(diff, n), banks, top[:, n % 2].unsqueeze(3).broadcast_to(by_head),
                                      ALU.subtract).then_inc(s["diff_ready"], 1)

                before_exp(0)
                for n in range(TILES):
                    if n + 1 < TILES:
                        before_exp(n + 1)
                    dve.wait_ge(s["exp_ready"], n + 1)
                    dve.tensor_reduce(total[:, n % 2], heads_of(expd, n), AX.X, ALU.add).then_inc(s["sum_ready"], 1)
                    dve.wait_ge(s["sum_ready"], n + 1)
                    if n >= 2:
                        dve.wait_ge(s["probs_ready"], n - 1)
                    dve.reciprocal(share[:, n % 2], total[:, n % 2]).then_inc(s["share_ready"], 1)
                    if n % TB == TB - 1:
                        blk = n // TB
                        for c in range(C):
                            dve.wait_ge(s["y_ps"], C * blk + c + 1)
                            part = x[:, c, blk * BLK:(blk + 1) * BLK]
                            dve.scalar_tensor_tensor(out=part, in0=ps[:, 7, :], scalar=bias["bo"][:, c:c + 1], in1=part,
                                                     op0=ALU.add, op1=ALU.add).then_inc(s["x_added"], 1)

            @block.scalar
            def _(act):
                def exp(n):
                    act.wait_ge(s["diff_ready"], n + 1)
                    if n >= 2:
                        act.wait_ge(s["probs_ready"], n - 1)
                        act.wait_ge(s["sum_ready"], n - 1)
                    act.activation(expd[:, n % 2].rearrange("p g k -> p (g k)"), diff[:, n % 2].rearrange("p g k -> p (g k)"),
                                   ACT.Exp, scale=DH ** -0.5).then_inc(s["exp_ready"], 1)

                exp(0)
                for n in range(TILES):
                    if n + 1 < TILES:
                        exp(n + 1)
                    blk, i = divmod(n, TB)
                    act.wait_ge(s["turned_ps"], n + 1)
                    if blk >= 2:
                        act.wait_ge(s["out_ps"], C * (blk - 1))
                    banks = ps[:, 4:7, :].rearrange("p b (k n) -> p (b k) n", n=P)
                    for rows, k0, k1 in ((P, 0, C * FULL), (SHORT, C * FULL, NK)):
                        act.activation(probs_t[0:rows, blk % 2, k0:k1, i * P:(i + 1) * P], banks[0:rows, k0:k1],
                                       ACT.Copy).then_inc(s["turned"], 1)
                    if i == TB - 1:
                        for g in range(C):
                            act.wait_ge(s["out_ps"], C * blk + g + 1)
                            if blk >= 2:
                                act.wait_ge(s["y_ps"], C * (blk - 1))
                            act.activation(attended[:, blk % 2, g, :], ps[:, 7, :], ACT.Copy).then_inc(s["out_ready"], 1)

            @block.gpsimd
            def _(pool):
                for n in range(TILES):
                    pool.wait_ge(s["share_ready"], n + 1)
                    if n >= 2:
                        pool.wait_ge(s["turned_ps"], n - 1)
                    pool.tensor_tensor(heads_of(probs, n), heads_of(expd, n),
                                       share[:, n % 2].unsqueeze(3).broadcast_to(by_head), ALU.mult).then_inc(s["probs_ready"], 1)


def self_attention(nc, consts, h, r, t):
    GROUPS, NH, DH = 4, 4, 16
    HR = P // 2
    KT = S // P
    QB = S // BLK
    STEPS = QB * KT
    RING = 3
    AUX = 32
    V0 = 32
    PIECES = NH * KT * QB
    den, y_out, half, value, piece, rows = "den", "y", "half", "value", "piece", "rows"
    Q0, Q1, K0, K1 = 0, 2, 4, 6
    LEAVING = [(den, 0), (den, 1)] + [(y_out, i) for i in range(4)]
    schedule = [[(den, 0), (den, 1), (half, Q0), (half, Q0 + 1)], [(y_out, i) for i in range(4)], [(half, K0)],
                [(half, K0 + 1), (half, Q1)]] + [[] for _ in range(STEPS - 4)]
    PER_STEP = 6
    for i in range(PIECES):
        schedule[4 + i // PER_STEP].append((piece, i))
    for i, late in enumerate([(half, Q1 + 1), (half, K1), (half, K1 + 1), (value, 0), (value, 1)]):
        schedule[4 + i].append(late)
    schedule[STEPS - 1].append((rows, 0))
    NEXT = [[job for job in jobs if job not in LEAVING] for jobs in schedule]
    NJ, NL = sum(map(len, NEXT)), len(LEAVING)
    assert NJ % 3 == 0 and NL % 3 == 0, "each unit starts with the same bank"
    UNITS = GROUPS * B

    def place_of(job, plan):
        return [j for jobs in plan for j in jobs].index(job)

    def jobs_of(first, last):
        if first:
            return NEXT
        return [[job for job in jobs if job in LEAVING] for jobs in schedule] if last else schedule

    def first_job(n, first):
        return NJ if first else (NJ + NL) * n + NJ - NL

    with ExitStack() as stack:
        sc = Scope(nc, stack, "F1")
        w_in = sc.sb("w_in", [P, 5, C, P])
        w_out = sc.sb("w_out", [P, D])
        cols = sc.sb("cols", [P, 5])
        ones_at = sc.sb("ones_at", [P, P])
        den_to = sc.sb("den_to", [P, P])
        rounded = sc.sb("rounded", [P, 2, BLK], F32R)
        q_split = sc.sb("q_split", [P, B, 2, S], F32R)
        k_split = sc.sb("k_split", [P, B, NH, S], F32R)
        v_tok = sc.sb("v_tok", [P, B, KT, P])
        probs = sc.sb("probs", [P, RING, NH, BLK])
        part_max = sc.sb("part_max", [P, NH * KT, QB])
        nmax = sc.sb("nmax", [P, NH * KT])
        nmax_rows = sc.sb("nmax_rows", [NH * KT, P], F32R)
        raw = sc.sb("raw", [P, S])
        dens = sc.sb("dens", [P, S])
        logden = sc.sb("logden", [P, S])
        rden = sc.sb("rden", [P, S])
        heads = sc.sb("heads", [P, S])
        ps = sc.psum()
        names = """setup zeroed in_loaded out_loaded job_ps taken rounded_ready nmax_ready row_ready
                   score_ps exp_ready pv_ps raw_ready logden_ready rden_ready heads_ready"""
        s = {n: sc.sem(n) for n in names.split()}
        block = stack.enter_context(nc.Block())

        def units(engine, body):
            for b in range(B):
                body(b, b, b == 0, False)
            with engine.Fori(1, GROUPS - 1) as g:
                for b in range(B):
                    body(B * g + b, b, False, False)
            for b in range(B):
                body(UNITS - B + b, b, False, b == B - 1)

        @block.sync
        def _(sp):
            def load_in(g):
                sp.dma_start(w_in[:, :, :, :], t["F1_w_in"][g].rearrange("o p t c n -> p (o t) c n")).then_inc(s["in_loaded"], 16)

            def load_out(g):
                sp.dma_start(w_out[:, :], t["F1_w_out"][g].rearrange("o p n -> p (o n)")).then_inc(s["out_loaded"], 16)

            def reload(g, first):
                n, plan = B * g, jobs_of(first, False)
                if not first:
                    sp.wait_ge(s["taken"], first_job(n, False) + place_of((y_out, 3), plan) + 1)
                    load_out(bass.ds(g, 1))
                sp.wait_ge(s["taken"], first_job(n, first) + place_of((value, 1), plan) + 1)
                load_in(slice(1, 2) if first else bass.ds(g + 1, 1))

            for dst, src in ((cols[:, :], t["F1_cols"]), (ones_at[:, :], t["F1_ones_at"]), (den_to[:, :], t["F1_den_to"])):
                sp.dma_start(dst, src).then_inc(s["setup"], 16)
            load_in(slice(0, 1))
            load_out(slice(0, 1))
            reload(0, True)
            with sp.Fori(1, GROUPS - 1) as g:
                reload(g, False)
            last_group = GROUPS - 1
            sp.wait_ge(s["taken"], first_job(B * last_group, False) + place_of((y_out, 3), schedule) + 1)
            load_out(slice(last_group, last_group + 1))

        @block.tensor
        def _(pe):
            def fill(kind, i, m, mb, left, base, place):
                if not (isinstance(base, int) and base + place < 3):
                    pe.wait_ge(s["taken"], base + place - 2)
                bank = ps[:, 3 + place % 3, :]
                if kind == den:
                    pe.wait_ge(s["raw_ready"], left + 1)
                    mm = pe.matmul(bank, den_to[:, :], raw[:, i * BLK:(i + 1) * BLK], start=True, stop=True)
                elif kind == y_out:
                    c, blk = divmod(i, QB)
                    pe.wait_ge(s["heads_ready"], left + 1)
                    mm = pe.matmul(bank, w_out[:, c * P:(c + 1) * P], heads[:, blk * BLK:(blk + 1) * BLK], start=True, stop=True)
                elif kind == half:
                    o, blk = divmod(i, QB)
                    for c in range(C):
                        mm = pe.matmul(bank, w_in[:, o, c, :], r[:, c, mb * S + blk * BLK:mb * S + (blk + 1) * BLK],
                                       start=c == 0, stop=c == C - 1)
                elif kind == value:
                    for kt in range(KT // 2):
                        t0 = mb * S + (i * (KT // 2) + kt) * P
                        for c in range(C):
                            mm = pe.matmul(bank[:, kt * P:(kt + 1) * P], r[:, c, t0:t0 + P], w_in[:, 4, c, :],
                                           start=c == 0, stop=c == C - 1)
                elif kind == piece:
                    if i == 0:
                        pe.wait_ge(s["taken"], base + place)
                    hd, qt, kb = i // (KT * QB), i // QB % KT, i % QB
                    mm = pe.matmul(bank, q_split[:, mb, hd // 2, qt * P:(qt + 1) * P],
                                   k_split[:, mb, hd, kb * BLK:(kb + 1) * BLK], start=True, stop=True)
                else:
                    pe.wait_ge(s["nmax_ready"], m + 1)
                    mm = pe.transpose(bank[0:NH * KT, 0:P], nmax[:, :], consts["ident"][:, :])
                mm.then_inc(s["job_ps"], 1)

            def pv(n, b, i, between):
                blk, kt = divmod(i, KT)
                pe.wait_ge(s["exp_ready"], NH * STEPS * n + NH * i + NH)
                if i == 0:
                    wait(pe, s["raw_ready"], n)
                for hd in range(NH):
                    mm = pe.matmul(ps[V0 * hd:V0 * hd + V0, 6 + blk, :], v_tok[:, b, kt, V0 * hd:V0 * hd + V0],
                                   probs[:, i % RING, hd, :], start=kt == 0, stop=kt == KT - 1)
                    if hd == NH - 1:
                        mm.then_inc(s["pv_ps"], 1)
                    between()

            def body(n, b, first, last):
                base, place = first_job(n, first), 0
                if b == 1:
                    pe.wait_ge(s["out_loaded"], 8 * n + 8)
                    if not last:
                        pe.wait_ge(s["in_loaded"], 8 * n + 24)
                pe.wait_ge(s["row_ready"], 64 * n + 64)
                for i, jobs in enumerate(jobs_of(first, last)):
                    blk, kt = divmod(i, KT)
                    done = 0

                    def next_job(early=False):
                        nonlocal place, done
                        if done < len(jobs) and (not early or jobs[done][0] in (piece, rows)):
                            fill(*jobs[done], n + 1, 1 - b, n - 1, base, place)
                            place, done = place + 1, done + 1

                    for hd in range(NH):
                        k = NH * i + hd
                        if k >= 3:
                            pe.wait_ge(s["exp_ready"], NH * STEPS * n + k - 2)
                        else:
                            wait(pe, s["exp_ready"], NH * STEPS * n)
                        pe.matmul(ps[:, k % 3, :], k_split[:, b, hd, kt * P:(kt + 1) * P],
                                  q_split[:, b, hd // 2, blk * BLK:(blk + 1) * BLK], start=True, stop=True)\
                          .then_inc(s["score_ps"], 1)
                        next_job(early=True)
                    if i:
                        pv(n, b, i - 1, next_job)
                    while done < len(jobs):
                        next_job()
                pv(n, b, STEPS - 1, lambda: None)
                if last:
                    for place, (kind, i) in enumerate(LEAVING):
                        fill(kind, i, None, None, n, base + NL, place)

            pe.wait_ge(s["setup"], 48)
            pe.wait_ge(s["in_loaded"], 16)
            place = 0
            for jobs in NEXT:
                for kind, i in jobs:
                    fill(kind, i, 0, 0, None, 0, place)
                    place += 1
            units(pe, body)

        HALVES = [i for jobs in NEXT for kind, i in jobs if kind == half]

        @block.scalar
        def _(act):
            def round_half(i, m, base, plan):
                k = HALVES.index(i)
                place = place_of((half, i), plan)
                act.wait_ge(s["job_ps"], base + place + 1)
                if k >= 2:
                    act.wait_ge(s["taken"], base + place_of((half, HALVES[k - 2]), plan) + 1)
                out, bank = rounded[:, k % 2, :], ps[:, 3 + place % 3, :]
                if i < K0:
                    act.activation(out, bank, ACT.Copy, scale=cols[:, 0:1]).then_inc(s["rounded_ready"], 1)
                else:
                    act.activation(out, bank, ACT.Identity, scale=cols[:, 2:3], bias=cols[:, 4:5]).then_inc(s["rounded_ready"], 1)

            def send_rows(b, base, plan):
                act.wait_ge(s["taken"], base + place_of((rows, 0), plan) + 1)
                for hd in range(NH):
                    row = AUX + HR * (hd % 2)
                    act.dma_start(q_split[row:row + 1, b, hd // 2, :].bitcast(F32).rearrange("o (t n) -> o t n", n=P),
                                  nmax_rows[hd * KT:(hd + 1) * KT, :].bitcast(F32)).then_inc(s["row_ready"], 16)

            def invert(n, base, plan):
                act.wait_ge(s["taken"], base + place_of((den, 1), plan) + 1)
                act.activation(logden[:, :], dens[:, :], ACT.Ln).then_inc(s["logden_ready"], 1)
                act.wait_ge(s["logden_ready"], n + 1)
                act.activation(rden[:, :], logden[:, :], ACT.Exp, scale=-1.0).then_inc(s["rden_ready"], 1)

            def body(n, b, first, last):
                base, plan = first_job(n, first), jobs_of(first, last)
                for i, jobs in enumerate(plan):
                    if i >= RING:
                        act.wait_ge(s["pv_ps"], STEPS * n + i - RING + 1)
                    for hd in range(NH):
                        k = NH * i + hd
                        act.wait_ge(s["score_ps"], NH * STEPS * n + k + 1)
                        act.activation(probs[:, i % RING, hd, :], ps[:, k % 3, :], ACT.Exp,
                                       scale=DH ** -0.5).then_inc(s["exp_ready"], 1)
                        if (rows, 0) in jobs and hd == 2:
                            send_rows(1 - b, base, plan)
                    if (den, 0) in jobs:
                        invert(n - 1, base, plan)
                    for kind, index in jobs:
                        if kind == half:
                            round_half(index, n + 1, base, plan)
                if last:
                    invert(n, base + NL, [LEAVING])

            act.wait_ge(s["setup"], 48)
            for i in HALVES:
                round_half(i, 0, 0, NEXT)
            send_rows(0, 0, NEXT)
            units(act, body)

        @block.vector
        def _(dve):
            def empty(kind, i, m, mb, left, base, place):
                if kind == half:
                    dve.wait_ge(s["rounded_ready"], len(HALVES) * m + HALVES.index(i) + 1)
                elif (kind, i) == (den, 0):
                    dve.wait_ge(s["pv_ps"], STEPS * (left + 1))
                    dve.tensor_copy(raw[:, :], ps[:, 6:8, :].rearrange("p b n -> p (b n)")).then_inc(s["raw_ready"], 1)
                elif kind == rows:
                    dve.wait_ge(s["taken"], base + place)
                    dve.tensor_reduce(nmax[:, :], part_max[:, :, :], AX.X, ALU.max, negate=True).then_inc(s["nmax_ready"], 1)
                    wait(dve, s["row_ready"], 64 * m)
                if kind != half:
                    dve.wait_ge(s["job_ps"], base + place + 1)
                bank = ps[:, 3 + place % 3, :]
                if kind == den:
                    op = dve.tensor_copy(dens[:, i * BLK:(i + 1) * BLK], bank)
                elif kind == y_out:
                    c, blk = divmod(i, QB)
                    part = h[:, c, mb * S + blk * BLK:mb * S + (blk + 1) * BLK]
                    op = dve.tensor_tensor(part, part, bank, ALU.add)
                elif kind == half:
                    o, blk = divmod(i, QB)
                    k = HALVES.index(i)
                    cells = slice(blk * BLK, (blk + 1) * BLK)
                    if i < K0:
                        op = dve.scalar_tensor_tensor(out=q_split[:, mb, o, cells], in0=bank, scalar=cols[:, 1:2],
                                                      in1=rounded[:, k % 2, :].bitcast(F32), op0=ALU.mult, op1=ALU.add)
                    else:
                        for j in range(2):
                            rr = slice(HR * j, HR * j + HR)
                            op = dve.scalar_tensor_tensor(out=k_split[rr, mb, 2 * (o - 2) + j, cells], in0=bank[rr],
                                                          scalar=cols[rr, 3:4], in1=rounded[rr, k % 2, :].bitcast(F32),
                                                          op0=ALU.mult, op1=ALU.add)
                elif kind == value:
                    kt = i * (KT // 2)
                    op = dve.tensor_tensor(v_tok[:, mb, kt:kt + KT // 2, :], bank.rearrange("p (t n) -> p t n", n=P),
                                           ones_at[:, :].unsqueeze(1).broadcast_to([P, KT // 2, P]), ALU.add)
                elif kind == piece:
                    op = dve.tensor_reduce(part_max[:, i // QB, i % QB:i % QB + 1], bank, AX.X, ALU.max)
                else:
                    op = dve.tensor_copy(nmax_rows[:, :], bank[0:NH * KT, 0:P])
                op.then_inc(s["taken"], 1)

            def divide(left):
                dve.wait_ge(s["rden_ready"], left + 1)
                dve.wait_ge(s["raw_ready"], left + 1)
                dve.tensor_tensor(heads[:, :], raw[:, :], rden[:, :], ALU.mult).then_inc(s["heads_ready"], 1)

            def body(n, b, first, last):
                base, place = first_job(n, first), 0
                for jobs in jobs_of(first, last):
                    for kind, i in jobs:
                        empty(kind, i, n + 1, 1 - b, n - 1, base, place)
                        place += 1
                        if (kind, i) == (den, 1):
                            divide(n - 1)
                if last:
                    for place, (kind, i) in enumerate(LEAVING):
                        empty(kind, i, None, b, n, base + NL, place)
                        if (kind, i) == (den, 1):
                            divide(n)
                    dve.wait_ge(s["taken"], base + 2 * NL)

            dve.memset(k_split[:, :, :, :].bitcast(F32), 0.0).then_inc(s["zeroed"], 1)
            dve.wait_ge(s["zeroed"], 1)
            dve.wait_ge(s["setup"], 48)
            place = 0
            for jobs in NEXT:
                for kind, i in jobs:
                    empty(kind, i, 0, 0, None, 0, place)
                    place += 1
            units(dve, body)

def align_stage(nc, consts, x, y, ctx, t):
    CK = 16
    W = S // CK
    SLOTS = CTX + CK - 1
    PAD = CK - 1
    ROWS = CTX + 2 * PAD
    LANES = 32 * B
    BIG = 1.0e30

    def dram(name):
        return nc.dram_tensor(f"align_{name}", [B, ROWS, S], F32).ap()

    def skewed(a, b):
        return bass.AP(a.tensor, b * ROWS * S + PAD * W, [[S - W, CK], [S, SLOTS], [1, W]])

    def straight(a, first=0):
        return a[:, PAD + first:PAD + first + CTX, :].rearrange("b r n -> r b n")

    cost_dram, total_dram, path_dram = dram("cost"), dram("total"), dram("path")
    move_dram = [dram(f"move{n}") for n in range(3)]

    def pads(a):
        return [a[:, r:r + PAD, :].rearrange("b r n -> r b n") for r in (0, PAD + CTX)]

    with ExitStack() as stack:
        sc = Scope(nc, stack, "G1")
        fill = sc.sb("fill", [PAD, 2, B, S])
        ctx_sq, y_sq = sc.sb("ctx_sq", [P, C, B * CTX]), sc.sb("y_sq", [P, C, T])
        norm = sc.sb("norm", [CTX, B])
        sums, dist2, dist = (sc.sb(n, [CTX, 2, BLK]) for n in ("sums", "dist2", "dist"))
        cost = sc.sb("cost", [CTX, T])
        ps = sc.psum()
        names = "filled ctx_squared y_squared norm_ps norm_ready prod_ps sums_ready dist2_ready dist_ready cost_ready stored"
        s = {n: sc.sem(n) for n in names.split()}
        block = stack.enter_context(nc.Block())

        @block.gpsimd
        def _(pool):
            pool.memset(fill[:, 0], BIG).then_inc(s["filled"], 1)
            pool.memset(fill[:, 1], 0.0).then_inc(s["filled"], 1)
            for c in range(C):
                pool.tensor_tensor(ctx_sq[:, c, :], ctx[:, c, :], ctx[:, c, :], ALU.mult).then_inc(s["ctx_squared"], 1)

        @block.scalar
        def _(act):
            for n in range(NBLK):
                act.activation(y_sq[:, :, n * BLK:(n + 1) * BLK], y[:, :, n * BLK:(n + 1) * BLK], ACT.Square)\
                   .then_inc(s["y_squared"], 1)
            for n in range(NBLK):
                act.wait_ge(s["dist_ready"], n + 1)
                act.activation(cost[:, n * BLK:(n + 1) * BLK], dist[:, n % 2, :], ACT.Sqrt).then_inc(s["cost_ready"], 1)

        @block.tensor
        def _(pe):
            pe.wait_ge(s["ctx_squared"], C)
            for b in range(B):
                for c in range(C):
                    mm = pe.matmul(ps[0:CTX, 0, b:b + 1], ctx_sq[:, c, b * CTX:(b + 1) * CTX], consts["ones"][:, 0:1],
                                   start=c == 0, stop=c == C - 1)
            mm.then_inc(s["norm_ps"], 1)
            for n in range(NBLK):
                b = n * BLK // S
                if n >= 2:
                    pe.wait_ge(s["dist2_ready"], n - 1)
                pe.wait_ge(s["y_squared"], n + 1)
                for c in range(C):
                    pe.matmul(ps[0:CTX, 2 + n % 2, :], consts["ones"][:, 0:CTX], y_sq[:, c, n * BLK:(n + 1) * BLK],
                              start=c == 0, stop=c == C - 1)
                for c in range(C):
                    mm = pe.matmul(ps[0:CTX, 4 + n % 2, :], ctx[:, c, b * CTX:(b + 1) * CTX], y[:, c, n * BLK:(n + 1) * BLK],
                                   start=c == 0, stop=c == C - 1)
                mm.then_inc(s["prod_ps"], 1)

        @block.vector
        def _(dve):
            dve.wait_ge(s["norm_ps"], 1)
            dve.tensor_copy(norm[:, :], ps[0:CTX, 0, 0:B]).then_inc(s["norm_ready"], 1)
            dve.wait_ge(s["norm_ready"], 1)
            for n in range(NBLK):
                b = n * BLK // S
                dve.wait_ge(s["prod_ps"], n + 1)
                if n >= 2:
                    dve.wait_ge(s["cost_ready"], n - 1)
                dve.tensor_scalar(sums[:, n % 2, :], ps[0:CTX, 2 + n % 2, :], norm[:, b:b + 1], None, ALU.add)\
                   .then_inc(s["sums_ready"], 1)
                dve.wait_ge(s["sums_ready"], n + 1)
                dve.scalar_tensor_tensor(out=dist2[:, n % 2, :], in0=ps[0:CTX, 4 + n % 2, :], scalar=-2.0,
                                         in1=sums[:, n % 2, :], op0=ALU.mult, op1=ALU.add).then_inc(s["dist2_ready"], 1)
                dve.wait_ge(s["dist2_ready"], n + 1)
                dve.tensor_scalar(dist[:, n % 2, :], dist2[:, n % 2, :], 0.0, None, ALU.max).then_inc(s["dist_ready"], 1)

        @block.sync
        def _(sp):
            sp.wait_ge(s["filled"], 2)
            count = 0
            for n, arrays in enumerate(([cost_dram], move_dram)):
                for a in arrays:
                    for dst in pads(a):
                        sp.dma_start(dst, fill[:, n]).then_inc(s["stored"], 16)
                        count += 16
            sp.wait_ge(s["cost_ready"], NBLK)
            sp.dma_start(straight(cost_dram), cost[:, :].rearrange("r (b n) -> r b n", b=B)).then_inc(s["stored"], 16)
            sp.wait_ge(s["stored"], count + 16)

    with ExitStack() as stack:
        sc = Scope(nc, stack, "G2")
        cost = sc.sb("cost", [LANES, SLOTS, W])
        total = sc.sb("total", [LANES, SLOTS + 1, 1 + W])
        start = sc.sb("start", [LANES, 1 + W])
        above = sc.sb("above", [LANES, W])
        filled, loaded, edge_ready, above_ready, row_ready, stored = (
            sc.sem(n) for n in "filled loaded edge_ready above_ready row_ready stored".split())
        from_left = [min(q + 1, CK) for q in range(CK)] + list(range(CK, 32))
        block = stack.enter_context(nc.Block())

        @block.gpsimd
        def _(pool):
            pool.memset(cost[:, :, :], BIG).then_inc(filled, 1)
            pool.memset(total[:, :, :], BIG).then_inc(filled, 1)

        @block.sync
        def _(sp):
            sp.wait_ge(filled, 2)
            for b in range(B):
                sp.dma_start(cost[32 * b:32 * b + CK], skewed(cost_dram, b)).then_inc(loaded, 16)
            sp.dma_start(total[:, 0, :], t["G_start"]).then_inc(loaded, 16)
            sp.wait_ge(row_ready, SLOTS)
            for b in range(B):
                sp.dma_start(skewed(total_dram, b), total[32 * b:32 * b + CK, 1:, 1:]).then_inc(stored, 16)
            sp.wait_ge(stored, 32)

        @block.vector
        def _(dve):
            dve.wait_ge(loaded, 48)
            for n in range(SLOTS):
                if n:
                    dve.wait_ge(row_ready, n)
                dve.stream_shuffle(total[:, n + 1, 0:1], total[:, n, W:W + 1], from_left).then_inc(edge_ready, 1)
                dve.tensor_tensor(above[:, :], total[:, n, 1:], total[:, n, 0:W], ALU.min).then_inc(above_ready, 1)
                dve.wait_ge(edge_ready, n + 1)
                dve.wait_ge(above_ready, n + 1)
                dve.tensor_tensor_scan(total[:, n + 1, 1:], above[:, :], cost[:, n, :], initial=total[:, n + 1, 0:1],
                                       op0=ALU.min, op1=ALU.add).then_inc(row_ready, 1)

    with ExitStack() as stack:
        sc = Scope(nc, stack, "G3")
        here, over = sc.sb("here", [CTX, B, 1 + S]), sc.sb("over", [CTX, B, 1 + S])
        least, not_diag = sc.sb("least", [CTX, B, S]), sc.sb("not_diag", [CTX, B, S])
        up, diag, left = (sc.sb(n, [CTX, B, S + 1]) for n in ("up", "diag", "left"))
        filled, loaded, dve_step, stored = (sc.sem(n) for n in "filled loaded dve_step stored".split())
        block = stack.enter_context(nc.Block())

        @block.gpsimd
        def _(pool):
            for a in (here, over):
                pool.memset(a[:, :, 0:1], BIG).then_inc(filled, 1)
            pool.memset(over[0:1, :, 1:], BIG).then_inc(filled, 1)
            for a in (diag, left):
                pool.memset(a[:, :, S:S + 1], 0.0).then_inc(filled, 1)

        @block.sync
        def _(sp):
            sp.dma_start(here[:, :, 1:], straight(total_dram)).then_inc(loaded, 16)
            sp.dma_start(over[1:, :, 1:], straight(total_dram)[0:CTX - 1]).then_inc(loaded, 16)
            sp.wait_ge(dve_step, 6)
            for a, dst in ((up[:, :, 0:S], 0), (diag[:, :, 1:], 1), (left[:, :, 1:], 2)):
                sp.dma_start(straight(move_dram[dst]), a).then_inc(stored, 16)
            sp.wait_ge(stored, 48)

        @block.vector
        def _(dve):
            step = chain(dve, dve_step)
            dve.wait_ge(filled, 5)
            dve.wait_ge(loaded, 32)
            c_up, c_diag, c_left = over[:, :, 1:], over[:, :, 0:S], here[:, :, 0:S]
            step(dve.tensor_tensor(least[:, :, :], c_up, c_left, ALU.min))
            step(dve.tensor_tensor(diag[:, :, 0:S], c_diag, least[:, :, :], ALU.is_le))
            step(dve.tensor_tensor(least[:, :, :], c_up, c_left, ALU.is_le))
            step(dve.tensor_scalar(not_diag[:, :, :], diag[:, :, 0:S], -1.0, 1.0, ALU.mult, ALU.add))
            step(dve.tensor_tensor(up[:, :, 0:S], least[:, :, :], not_diag[:, :, :], ALU.mult))
            step(dve.tensor_tensor(left[:, :, 0:S], not_diag[:, :, :], up[:, :, 0:S], ALU.subtract))

    with ExitStack() as stack:
        sc = Scope(nc, stack, "G4")
        move = [sc.sb(f"move{n}", [LANES, SLOTS + 1, W]) for n in range(2)]
        left = sc.sb("left", [LANES, SLOTS, W])
        path = sc.sb("path", [LANES, SLOTS + 1, W + 1])
        below = sc.sb("below", [LANES, 2, W])
        enter = sc.sb("enter", [LANES, W])
        filled, loaded, edge_ready, below_ready, enter_ready, row_ready, stored = (
            sc.sem(n) for n in "filled loaded edge_ready below_ready enter_ready row_ready stored".split())
        from_right = [CK] + list(range(CK - 1)) + list(range(CK, 32))
        block = stack.enter_context(nc.Block())

        @block.gpsimd
        def _(pool):
            for a in (*move, left, path):
                pool.memset(a[:, :, :], 0.0).then_inc(filled, 1)
            pool.wait_ge(filled, 4)
            pool.memset(move[0][:, SLOTS, :], 1.0).then_inc(filled, 1)

        @block.sync
        def _(sp):
            sp.wait_ge(filled, 5)
            for b in range(B):
                for a, src in zip((*move, left), move_dram):
                    sp.dma_start(a[32 * b:32 * b + CK, 0:SLOTS], skewed(src, b)).then_inc(loaded, 16)
            sp.dma_start(path[:, SLOTS, :], t["G_end"]).then_inc(loaded, 16)
            sp.wait_ge(row_ready, SLOTS)
            for b in range(B):
                sp.dma_start(skewed(path_dram, b), path[32 * b:32 * b + CK, 0:SLOTS, 0:W]).then_inc(stored, 16)
            sp.wait_ge(stored, 32)

        @block.vector
        def _(dve):
            dve.wait_ge(loaded, 16 * (3 * B + 1))
            for i, n in enumerate(reversed(range(SLOTS))):
                if i:
                    dve.wait_ge(row_ready, i)
                dve.stream_shuffle(path[:, n, W:W + 1], path[:, n + 1, 0:1], from_right).then_inc(edge_ready, 1)
                for m in range(2):
                    dve.tensor_tensor(below[:, m, :], path[:, n + 1, m:m + W], move[m][:, n + 1, :], ALU.mult)\
                       .then_inc(below_ready, 1)
                dve.wait_ge(below_ready, 2 * i + 2)
                dve.tensor_tensor(enter[:, :], below[:, 0, :], below[:, 1, :], ALU.add).then_inc(enter_ready, 1)
                dve.wait_ge(edge_ready, i + 1)
                dve.wait_ge(enter_ready, i + 1)
                dve.tensor_tensor_scan(path[:, n, W - 1::-1], left[:, n, ::-1], enter[:, ::-1],
                                       initial=path[:, n, W:W + 1], op0=ALU.mult, op1=ALU.add).then_inc(row_ready, 1)

    with ExitStack() as stack:
        sc = Scope(nc, stack, "G5")
        path = sc.sb("path", [CTX, B, S])
        ctx_rows = sc.sb("ctx_rows", [CTX, B, D])
        ps = sc.psum()
        loaded, out_ps, x_added = (sc.sem(n) for n in "loaded out_ps x_added".split())
        block = stack.enter_context(nc.Block())

        @block.sync
        def _(sp):
            sp.dma_start(path[:, :, :], straight(path_dram)).then_inc(loaded, 16)
            sp.dma_start(ctx_rows[:, :, :], t["G_ctx_rows"]).then_inc(loaded, 16)

        @block.tensor
        def _(pe):
            pe.wait_ge(loaded, 32)
            for n in range(NBLK):
                b, blk = divmod(n, S // BLK)
                for c in range(C):
                    mm = pe.matmul(ps[:, C * n + c, :], ctx_rows[:, b, c * P:(c + 1) * P], path[:, b, blk * BLK:(blk + 1) * BLK],
                                   start=True, stop=True)
                mm.then_inc(out_ps, 1)

        @block.vector
        def _(dve):
            for n in range(NBLK):
                dve.wait_ge(out_ps, n + 1)
                part = x[:, :, n * BLK:(n + 1) * BLK]
                dve.tensor_tensor(part, part, ps[:, C * n:C * n + C, :], ALU.add).then_inc(x_added, 1)
            dve.wait_ge(x_added, NBLK)


def slots_stage(nc, consts, x, y, t):
    N, PS = 64, 32
    SL = N * PS
    Q = SL // BLK
    TB = S // P
    G = SL // P
    GE = P // PS
    slots_dram = nc.dram_tensor("slots", [B, P, C, SL], F32).ap()
    made_dram = nc.dram_tensor("made", [B, P, G, D], F32).ap()
    with ExitStack() as outer:
        oc = Scope(nc, outer, "H")
        y_tok = oc.sb("y_tok", [P, TILES, D])
        logits = oc.sb("logits", [P, TILES, SL])

        with ExitStack() as stack:
            sc = Scope(nc, stack, "H0")
            ps = sc.psum()
            turned_ps, turned = sc.sem("turned_ps"), sc.sem("turned")
            with nc.Block() as block:
                @block.tensor
                def _(pe):
                    for n in range(TILES // 2):
                        for k in range(2):
                            for c in range(C):
                                tile = 2 * n + k
                                mm = pe.transpose(ps[:, n, k * D + c * P:k * D + (c + 1) * P],
                                                  y[:, c, tile * P:(tile + 1) * P], consts["ident"][:, :])
                        mm.then_inc(turned_ps, 1)

                @block.vector
                def _(dve):
                    for n in range(TILES // 2):
                        dve.wait_ge(turned_ps, n + 1)
                        dve.tensor_copy(y_tok[:, 2 * n:2 * n + 2, :], ps[:, n, :].rearrange("p (k d) -> p k d", k=2))\
                           .then_inc(turned, 1)

        with ExitStack() as stack:
            sc = Scope(nc, stack, "H1")
            phi = sc.sb("phi", [P, 2, C, BLK])
            diff = sc.sb("diff", [P, 2, BLK])
            dispatch = sc.sb("dispatch", [P, 2, B, BLK])
            staged = sc.sb("staged", [P, B, C, BLK])
            ps = sc.psum()
            names = "logits_ps kept0 kept1 diff_ready dispatch_ready slots_ps staged_ready stored"
            s = {n: sc.sem(n) for n in names.split()}
            phi_loaded = [sc.sem(f"phi_loaded{n}") for n in range(2)]
            LAG = 1
            steps = [(q, m) for q in range(Q) for m in range(TB)]
            block = stack.enter_context(nc.Block())

            @block.sync
            def _(sp):
                for q in range(Q):
                    if q >= 2:
                        sp.wait_ge(s["logits_ps"], TB * (q - 1))
                    sp.dma_start(phi[:, q % 2], t["H_phi"][q]).then_inc(phi_loaded[q % 2], 16)
                    if q >= 1:
                        sp.wait_ge(s["staged_ready"], B * q)
                        for b in range(B):
                            sp.dma_start(slots_dram[b][:, :, (q - 1) * BLK:q * BLK], staged[:, b]).then_inc(s["stored"], 16)
                sp.wait_ge(s["staged_ready"], B * Q)
                for b in range(B):
                    sp.dma_start(slots_dram[b][:, :, (Q - 1) * BLK:Q * BLK], staged[:, b]).then_inc(s["stored"], 16)
                sp.wait_ge(s["stored"], 16 * B * Q)

            @block.tensor
            def _(pe):
                def gather(n):
                    q, m = steps[n]
                    pe.wait_ge(s["dispatch_ready"], B * n + B)
                    if m == 0 and q:
                        pe.wait_ge(s["staged_ready"], B * q)
                    for b in range(B):
                        for c in range(C):
                            mm = pe.matmul(ps[:, 4 + C * b + c, :], y_tok[:, b * TB + m, c * P:(c + 1) * P],
                                           dispatch[:, n % 2, b, :], start=m == 0, stop=m == TB - 1)
                    mm.then_inc(s["slots_ps"], 1)

                for n, (q, m) in enumerate(steps):
                    if m == 0:
                        pe.wait_ge(phi_loaded[q % 2], 16 * (q // 2 + 1))
                    if n >= 2:
                        pe.wait_ge(s["kept0"], n - 1)
                        pe.wait_ge(s["kept1"], n - 1)
                    for b in range(B):
                        for c in range(C):
                            mm = pe.matmul(ps[:, 2 * (n % 2) + b, :], y[:, c, (b * TB + m) * P:(b * TB + m + 1) * P],
                                           phi[:, q % 2, c, :], start=c == 0, stop=c == C - 1)
                    mm.then_inc(s["logits_ps"], 1)
                    if n >= LAG:
                        gather(n - LAG)
                gather(len(steps) - 1)

            @block.scalar
            def _(act):
                for n, (q, m) in enumerate(steps):
                    act.wait_ge(s["logits_ps"], n + 1)
                    act.activation(logits[:, m, q * BLK:(q + 1) * BLK], ps[:, 2 * (n % 2), :], ACT.Copy).then_inc(s["kept0"], 1)
                    act.wait_ge(s["diff_ready"], n + 1)
                    if n >= 2:
                        act.wait_ge(s["slots_ps"], n - 1)
                    for b in range(B):
                        act.activation(dispatch[:, n % 2, b, :], diff[:, n % 2, :], ACT.Sigmoid,
                                       scale=1.0 - 2.0 * b).then_inc(s["dispatch_ready"], 1)

            def stage_out(dve, q, b):
                dve.wait_ge(s["slots_ps"], TB * (q + 1))
                if q:
                    dve.wait_ge(s["stored"], 16 * B * q)
                dve.tensor_copy(staged[:, b], ps[:, 4 + C * b:4 + C * b + C, :]).then_inc(s["staged_ready"], 1)

            @block.vector
            def _(dve):
                for n, (q, m) in enumerate(steps):
                    dve.wait_ge(s["logits_ps"], n + 1)
                    dve.tensor_copy(logits[:, TB + m, q * BLK:(q + 1) * BLK], ps[:, 2 * (n % 2) + 1, :]).then_inc(s["kept1"], 1)
                    if m == 0 and q:
                        for b in range(B):
                            stage_out(dve, q - 1, b)
                for b in range(B):
                    stage_out(dve, Q - 1, b)

            @block.gpsimd
            def _(pool):
                for n, (q, m) in enumerate(steps):
                    pool.wait_ge(s["kept0"], n + 1)
                    pool.wait_ge(s["kept1"], n + 1)
                    if n >= 2:
                        pool.wait_ge(s["dispatch_ready"], B * (n - 1))
                    cols = slice(q * BLK, (q + 1) * BLK)
                    pool.tensor_tensor(diff[:, n % 2, :], logits[:, m, cols], logits[:, TB + m, cols],
                                       ALU.subtract).then_inc(s["diff_ready"], 1)

        slots = [y[:, :, :], y_tok[:, :, :].rearrange("p t d -> p (t d)").rearrange("p (c n) -> p c n", c=C)]
        with ExitStack() as stack:
            sc = Scope(nc, stack, "H2")
            RING = 3
            w = sc.sb("w", [P, RING, C, D])
            bias = sc.sb("bias", [P, 2, D])
            made = sc.sb("made", [P, 2, B, D])
            ps = sc.psum()
            names = "slots_loaded expert_ps group_ps made_ready"
            s = {n: sc.sem(n) for n in names.split()}
            w_loaded = [sc.sem(f"w_loaded{n}") for n in range(RING)]
            bias_loaded = [sc.sem(f"bias_loaded{n}") for n in range(2)]
            stored = [sc.sem(f"stored{n}") for n in range(2)]
            block = stack.enter_context(nc.Block())

            @block.sync
            def _(sp):
                for b in range(B):
                    sp.dma_start(slots[b], slots_dram[b]).then_inc(s["slots_loaded"], 16)
                for n in range(N):
                    if n >= RING:
                        sp.wait_ge(s["expert_ps"], n - RING + 1)
                    sp.dma_start(w[:, n % RING], t["H_w"][n]).then_inc(w_loaded[n % RING], 16)

            def store(pool, g):
                pool.wait_ge(s["made_ready"], g + 1)
                pool.dma_start(made_dram[:, :, g, :].rearrange("b p d -> p b d"), made[:, g % 2]).then_inc(stored[g % 2], 16)

            @block.gpsimd
            def _(pool):
                for g in range(G):
                    if g >= 2:
                        pool.wait_ge(s["made_ready"], g - 1)
                    pool.dma_start(bias[:, g % 2, :], t["H_b"][g]).then_inc(bias_loaded[g % 2], 16)
                    if g:
                        store(pool, g - 1)
                store(pool, G - 1)
                for n in range(2):
                    pool.wait_ge(stored[n], 16 * G // 2)

            @block.tensor
            def _(pe):
                pe.wait_ge(s["slots_loaded"], 16 * B)
                for n in range(N):
                    g, i = divmod(n, GE)
                    pe.wait_ge(w_loaded[n % RING], 16 * (n // RING + 1))
                    if i == 0 and g >= 2:
                        pe.wait_ge(s["made_ready"], g - 1)
                    for b in range(B):
                        for c in range(C):
                            mm = pe.matmul(ps[PS * i:PS * i + PS, 2 * (g % 2) + b, 0:D], slots[b][:, c, n * PS:(n + 1) * PS],
                                           w[:, n % RING, c, :], start=c == 0, stop=c == C - 1)
                    mm.then_inc(s["expert_ps"], 1)

            @block.vector
            def _(dve):
                for g in range(G):
                    dve.wait_ge(s["expert_ps"], GE * (g + 1))
                    dve.wait_ge(bias_loaded[g % 2], 16 * (g // 2 + 1))
                    if g >= 2:
                        dve.wait_ge(stored[g % 2], 16 * (g // 2))
                    dve.tensor_tensor(made[:, g % 2], ps[:, 2 * (g % 2):2 * (g % 2) + 2, 0:D],
                                      bias[:, g % 2, :].unsqueeze(1).broadcast_to([P, B, D]), ALU.add).then_inc(s["made_ready"], 1)

        outs = [y[:, :, :].rearrange("p c n -> p (c n)").rearrange("p (g d) -> p g d", d=D), y_tok[:, :, :]]
        with ExitStack() as stack:
            sc = Scope(nc, stack, "H3")
            nmax, total, share = (sc.sb(n, [P, TILES]) for n in ("nmax", "total", "share"))
            ps = sc.psum()
            names = "made_loaded max_ready exp_ready share_ready combine_ready turned_ps turned_a turned_b out_ps x_added"
            s = {n: sc.sem(n) for n in names.split()}
            BT = BLK // P
            block = stack.enter_context(nc.Block())

            @block.sync
            def _(sp):
                for b in range(B):
                    sp.dma_start(outs[b], made_dram[b]).then_inc(s["made_loaded"], 16)

            @block.tensor
            def _(pe):
                def out(blk):
                    if blk == 0:
                        pe.wait_ge(s["made_loaded"], 16 * B)
                    pe.wait_ge(s["turned_a"], BT * (blk + 1))
                    pe.wait_ge(s["turned_b"], BT * (blk + 1))
                    if blk >= 2:
                        pe.wait_ge(s["x_added"], blk - 1)
                    b = blk * BLK // S
                    for c in range(C):
                        for g in range(G):
                            mm = pe.matmul(ps[:, 4 + 2 * (blk % 2) + c, :], outs[b][:, g, c * P:(c + 1) * P],
                                           logits[:, BT * blk:BT * blk + BT, g * P:(g + 1) * P], start=g == 0, stop=g == G - 1)
                    mm.then_inc(s["out_ps"], 1)

                for n in range(TILES):
                    pe.wait_ge(s["combine_ready"], n + 1)
                    if n:
                        pe.wait_ge(s["turned_a"], n)
                        pe.wait_ge(s["turned_b"], n)
                    for g in range(G):
                        mm = pe.transpose(ps[:, g // 4, (g % 4) * P:(g % 4 + 1) * P], logits[:, n, g * P:(g + 1) * P],
                                          consts["ident"][:, :])
                    mm.then_inc(s["turned_ps"], 1)
                    if n % BT == 1 and n > BT:
                        out(n // BT - 1)
                out(TILES // BT - 1)

            def add(dve, blk):
                dve.wait_ge(s["out_ps"], blk + 1)
                part = x[:, :, blk * BLK:(blk + 1) * BLK]
                dve.tensor_tensor(part, part, ps[:, 4 + 2 * (blk % 2):6 + 2 * (blk % 2), :], ALU.add).then_inc(s["x_added"], 1)

            @block.vector
            def _(dve):
                def maximum(n):
                    dve.tensor_reduce(nmax[:, n:n + 1], logits[:, n, :], AX.X, ALU.max, negate=True).then_inc(s["max_ready"], 1)

                maximum(0)
                for n in range(TILES):
                    if n + 1 < TILES:
                        maximum(n + 1)
                    dve.wait_ge(s["exp_ready"], n + 1)
                    dve.reciprocal(share[:, n:n + 1], total[:, n:n + 1]).then_inc(s["share_ready"], 1)
                    dve.wait_ge(s["share_ready"], n + 1)
                    dve.tensor_scalar(logits[:, n, :], logits[:, n, :], share[:, n:n + 1], None, ALU.mult)\
                       .then_inc(s["combine_ready"], 1)
                    dve.wait_ge(s["turned_ps"], n + 1)
                    dve.tensor_copy(logits[:, n, SL // 2:], ps[:, 2:4, :].rearrange("p b n -> p (b n)")).then_inc(s["turned_b"], 1)
                    if n % BT == 2 and n > BT:
                        add(dve, n // BT - 1)
                add(dve, TILES // BT - 1)
                dve.wait_ge(s["x_added"], NBLK)

            @block.scalar
            def _(act):
                def exp(n):
                    act.wait_ge(s["max_ready"], n + 1)
                    act.activation(logits[:, n, :], logits[:, n, :], ACT.Exp, bias=nmax[:, n:n + 1],
                                   accum_out=total[:, n:n + 1]).then_inc(s["exp_ready"], 1)

                exp(0)
                for n in range(TILES):
                    if n + 1 < TILES:
                        exp(n + 1)
                    act.wait_ge(s["turned_ps"], n + 1)
                    act.activation(logits[:, n, 0:SL // 2], ps[:, 0:2, :].rearrange("p b n -> p (b n)"), ACT.Copy)\
                       .then_inc(s["turned_a"], 1)


def program(nc, t, out, stop=99, only=None):
    on = lambda k: stop >= k if only is None else k == only
    t = dict(t)
    for name in "BDF":
        t["scratch_gates_" + name] = nc.dram_tensor(f"gates_{name}", [E, T], F32).ap()
    with ExitStack() as stack:
        sc = Scope(nc, stack, "g")
        x = sc.sb("x", [P, C, T])
        y = sc.sb("y", [P, C, T])
        ctx = sc.sb("ctx", [P, C, B * CTX])
        names = ["mean", "ident", "ones"]
        consts = {n: sc.sb(n, [P, P]) for n in names}
        consts["eps"] = sc.sb("eps", [P, 1])
        load_stage(nc, "load", [(x[:, :, :], t["x"]), (ctx[:, :, :], t["ctx"]), (consts["eps"][:, :], t["c_eps"])]
                   + [(consts[n][:, :], t["c_" + n]) for n in names])
        if on(1):
            with ExitStack() as layer:
                ls = Scope(nc, layer, "A0")
                ctx_n = ls.sb("ctx_n", [P, C, B * CTX])
                lnw = {k: ls.sb(k, [P, C]) for k in ("ln1_w", "ln1_b", "ln2_w", "ln2_b")}
                load_stage(nc, "loadA", [(v[:, :], t["L0_xattn_" + k]) for k, v in lnw.items()])
                norm_stage(nc, "nA1", consts, norm_jobs(x, y))
                norm_stage(nc, "nA2", consts, norm_jobs(y, y, scale=lnw["ln2_w"], shift=lnw["ln2_b"])
                           + [(ctx, ctx_n, 0, B * CTX, False, lnw["ln1_w"], lnw["ln1_b"])])
                latent_attention(nc, consts, x, y, ctx_n, t["A_wqkv"], t["A_wo"])
        if on(2):
            norm_stage(nc, "nB", consts, norm_jobs(x, y))
            moe(nc, "B", "top1", ACT.Gelu, D, consts, x, y, t, [])
        if on(3):
            norm_stage(nc, "nC", consts, norm_jobs(x, y))
            context_attention(nc, "C", consts, x, y, ctx, t)
        if on(4):
            norm_stage(nc, "nD", consts, norm_jobs(x, y))
            moe(nc, "D", "sinkhorn", ACT.Relu, 2 * D, consts, x, y, t, [y])
        if on(5):
            norm_stage(nc, "nE", consts, norm_jobs(x, y))
            context_attention(nc, "E", consts, x, y, ctx, t)
        if on(6):
            norm_stage(nc, "nF", consts, norm_jobs(x, y))
            with ExitStack() as layer:
                ls = Scope(nc, layer, "F0")
                r = ls.sb("r", [P, C, T])
                lnw = {k: ls.sb(k, [P, C]) for k in ("ln1_w", "ln2_w")}
                load_stage(nc, "loadF", [(v[:, :], t["F_" + k]) for k, v in lnw.items()])
                norm_stage(nc, "nF1", consts, norm_jobs(y, r, rms=True, scale=lnw["ln1_w"]))
                self_attention(nc, consts, y, r, t)
                norm_stage(nc, "nF2", consts, norm_jobs(y, r, rms=True, scale=lnw["ln2_w"]))
                moe(nc, "F", "top2", ACT.Silu, 2 * D, consts, x, r, t, [y])
        if on(7):
            norm_stage(nc, "nG", consts, norm_jobs(x, y))
            align_stage(nc, consts, x, y, ctx, t)
        if on(8):
            norm_stage(nc, "nH", consts, norm_jobs(x, y))
            slots_stage(nc, consts, x, y, t)
        with ExitStack() as last:
            stored = Scope(nc, last, "out").sem("stored")
            with nc.Block() as block:
                @block.sync
                def _(sp):
                    sp.dma_start(out, x[:, :, :]).then_inc(stored, 16)
                    sp.wait_ge(stored, 16)


def lay_out(np, i):
    def feat(a):
        return a.T.reshape(-1, P, a.shape[0]).transpose(1, 0, 2)

    def rows(w):
        return w.reshape(-1, P, w.shape[-1]).transpose(1, 0, 2)

    def column(v):
        return v.reshape(-1, P).T

    def everywhere(v):
        return np.broadcast_to(v, (P,) + v.shape)

    def experts(name, w_in, w_out):
        w = np.stack(w_in, axis=1)
        t[name + "_w_in"] = w.reshape(E, len(w_in), C, P, -1).transpose(0, 3, 1, 2, 4)
        t[name + "_w_out"] = w_out.reshape(E, -1, P, D).transpose(0, 2, 1, 3)

    t = {"x": feat(i["x"].reshape(T, D)), "ctx": feat(i["ctx_1024"].reshape(B * CTX, D)),
         "c_mean": np.full((P, P), 1.0 / D, np.float32), "c_ident": np.eye(P, dtype=np.float32),
         "c_ones": np.ones((P, P), np.float32), "c_eps": np.full((P, 1), EPS, np.float32),
         "c_order": everywhere(np.arange(E, 0, -1, dtype=np.float32))}
    for k in ("ln1_w", "ln1_b", "ln2_w", "ln2_b"):
        t["L0_xattn_" + k] = column(i["L0_xattn_" + k])
    wq, wkv = i["L0_xattn_Wq"], i["L0_xattn_Wkv"]
    stacked = np.stack([wq, wkv[:, :1024], wkv[:, 1024:]])
    t["A_wqkv"] = stacked.reshape(3, C, P, 8, P).transpose(3, 2, 0, 1, 4)
    t["A_wo"] = i["L0_xattn_Wo"].reshape(8, P, D)
    experts("B", [i["L0_ffn_W1"]], i["L0_ffn_W2"])
    t["B_router_w"], t["B_router_b"] = rows(i["L0_ffn_Wg"]), everywhere(i["L0_ffn_bg"])
    t["B_b_in"] = i["L0_ffn_b1"].reshape(E, C, P).transpose(0, 2, 1)
    t["B_b_out"] = i["L0_ffn_b2"]
    experts("D", [i["L1_ffn_wg"], i["L1_ffn_wp"]], i["L1_ffn_wo"])
    t["D_router_w"], t["D_router_b"] = rows(i["L1_ffn_router_w"].T), everywhere(i["L1_ffn_router_b"])
    t["D_temperature"] = everywhere(i["L1_ffn_temperature"])
    t["F_ln1_w"], t["F_ln2_w"] = column(i["L2_ffn_ln1_w"]), column(i["L2_ffn_ln2_w"])
    experts("F", [i["L2_ffn_w1"].transpose(0, 2, 1), i["L2_ffn_w3"].transpose(0, 2, 1)], i["L2_ffn_w2"].transpose(0, 2, 1))
    t["F_router_w"] = rows(i["L2_ffn_gate_w"].T)
    t["c_head_mask"] = np.repeat(np.eye(8, dtype=np.float32), 16, axis=0)
    wkv, bkv = i["L1_xattn_Wkv"], i["L1_xattn_bkv"]
    for name, ws in (("C", (i["L1_xattn_Wq"], wkv[:D], wkv[D:], i["L1_xattn_Wo"])),
                     ("E", [i["L2_xattn_" + k] for k in ("wq", "wk", "wv", "wo")])):
        for k, w in zip(("wq", "wk", "wv", "wo"), ws):
            t[f"{name}_{k}"] = rows(w.T)
    for name, bs in (("C", (i["L1_xattn_bq"], bkv[:D], bkv[D:], i["L1_xattn_bo"])),
                     ("E", [i["L2_xattn_" + k] for k in ("bq", "bk", "bv", "bo")])):
        for k, b in zip(("bq", "bk", "bv", "bo"), bs):
            t[f"{name}_{k}"] = column(b)
    hi_hi, lo_hi, hi_lo, aux = 0, 16, 48, 32

    def qk_rows(w):
        w = w.reshape(4, 2, 2, 16, D)
        out = np.zeros((4, 2, 2, 64, D), w.dtype)
        for at in (hi_hi, lo_hi, hi_lo):
            out[:, :, :, at:at + 16] = w
        return out.reshape(4, 2, P, D).transpose(0, 1, 3, 2)

    v = np.zeros((4, 4, 32, D), np.float32)
    v[:, :, :16] = i["L2_ffn_wv"].reshape(4, 4, 16, D)
    wo = np.zeros((4, 4, 32, D), np.float32)
    wo[:, :, :16] = i["L2_ffn_wo"].T.reshape(4, 4, 16, D)
    w_in = np.concatenate([qk_rows(i["L2_ffn_wq"]), qk_rows(i["L2_ffn_wk"]), v.reshape(4, 1, P, D).transpose(0, 1, 3, 2)], 1)
    t["F1_w_in"] = w_in.reshape(4, 5, C, P, P).transpose(0, 3, 1, 2, 4)
    t["F1_w_out"] = wo.reshape(4, P, D)
    cols = np.zeros((2, 64, 5), np.float32)
    cols[:, :, 0] = cols[:, :, 2] = 1
    cols[:, hi_lo:hi_lo + 16, 0], cols[:, hi_lo:hi_lo + 16, 1] = -1, 1
    cols[:, lo_hi:lo_hi + 16, 2], cols[:, lo_hi:lo_hi + 16, 3] = -1, 1
    cols[:, aux, 4] = 1
    t["F1_cols"] = cols.reshape(P, 5)
    t["F1_ones_at"] = everywhere(np.tile(np.repeat(np.array([0, 1], np.float32), 16), 4))
    den = np.zeros((4, 32, 4, 32), np.float32)
    for hd in range(4):
        den[hd, 16, hd, :] = 1
    t["F1_den_to"] = den.reshape(P, P)
    start = np.full((2, 32, 65), 1.0e30, np.float32)
    start[:, 15, 0] = 0
    end = np.zeros((2, 32, 65), np.float32)
    end[:, 0, 63] = 1
    t["G_start"], t["G_end"] = start.reshape(64, 65), end.reshape(64, 65)
    t["G_ctx_rows"] = i["ctx_1024"].transpose(1, 0, 2)
    t["H_phi"] = rows(i["L3_ffn_phi"].reshape(D, 2048)).reshape(P, C, 4, BLK).transpose(2, 0, 1, 3)
    t["H_w"] = i["L3_ffn_W"].reshape(64, C, P, D).transpose(0, 2, 1, 3)
    t["H_b"] = np.repeat(i["L3_ffn_b"], 32, axis=0).reshape(16, P, D)
    return {k: np.ascontiguousarray(v) for k, v in t.items()}


def kernel(**inputs):
    import numpy as np
    import concourse.bacc as bacc
    from concourse.bass_utils import run_bass_kernel_spmd as run

    nc = bacc.Bacc("TRN2", target_bir_lowering=False, num_devices=1)
    arrays = lay_out(np, {k: np.asarray(v) for k, v in inputs.items()})
    aps = {k: nc.dram_tensor(f"in_{k}", v.shape, mybir.dt.from_np(v.dtype), kind="ExternalInput").ap()
           for k, v in arrays.items()}
    out = nc.dram_tensor("out", [P, C, T], F32, kind="ExternalOutput").ap()
    program(nc, aps, out)
    got = run(nc, [{f"in_{k}": v for k, v in arrays.items()}], core_ids=[0]).results[0]["out"]
    return got.transpose(1, 0, 2).reshape(D, T).T.reshape(B, S, D)
```

```python
from contextlib import ExitStack

import concourse.bass as bass
from concourse import mybir

ALU = mybir.AluOpType
ACT = mybir.ActivationFunctionType
F32 = mybir.dt.float32
F32R = mybir.dt.float32r
AX = mybir.AxisListType

P = 128
B = 2
S = 1024
T = B * S
D = 256
C = D // P
CTX = 77
BLK = 512
NBLK = T // BLK
TILES = T // P
EPS = 1e-5
E = 8


class Scope:

    def __init__(self, nc, stack, stage):
        self.nc, self.stack, self.stage = nc, stack, stage
        self.semaphores = []
        stack.callback(self.clear)

    def clear(self):
        for s in self.semaphores:
            self.nc.gpsimd.sem_clear(s)

    def sb(self, name, shape, dt=F32):
        return self.stack.enter_context(self.nc.sbuf_tensor(f"{self.stage}_{name}", shape, dt))

    def psum(self, name="banks"):
        return self.stack.enter_context(self.nc.psum_tensor(f"{self.stage}_{name}", [P, 8, BLK], F32))

    def sem(self, name):
        self.semaphores.append(self.stack.enter_context(self.nc.semaphore(f"{self.stage}_{name}")))
        return self.semaphores[-1]


def load_stage(nc, stage, pairs):
    with ExitStack() as stack:
        loaded = Scope(nc, stack, stage).sem("loaded")
        with nc.Block() as block:
            @block.sync
            def _(sp):
                for dst, src in pairs:
                    sp.dma_start(dst, src).then_inc(loaded, 16)
                sp.wait_ge(loaded, 16 * len(pairs))


def norm_stage(nc, stage, consts, jobs, rms=False):
    GROUP = 4
    groups = [range(n, min(n + GROUP, len(jobs))) for n in range(0, len(jobs), GROUP)]
    with ExitStack() as stack:
        sc = Scope(nc, stack, stage)
        squared = sc.sb("squared", [P, GROUP, C, BLK])
        logvar = sc.sb("logvar", [P, GROUP, BLK])
        rstd = sc.sb("rstd", [P, GROUP, BLK])
        ps = sc.psum()
        mean_ready, centred_ready, squared_ready = sc.sem("mean_ready"), sc.sem("centred_ready"), sc.sem("squared_ready")
        var_ready, log_ready, rstd_ready = sc.sem("var_ready"), sc.sem("log_ready"), sc.sem("rstd_ready")
        normed, scaled = sc.sem("normed"), sc.sem("scaled")
        affine = [n for n, job in enumerate(jobs) if job[4] is not None]

        def centred(n):
            src, dst, t0, w, _, _ = jobs[n]
            return (src if rms else dst)[:, :, t0:t0 + w]

        with nc.Block() as block:
            @block.tensor
            def _(pe):
                def mean(n):
                    src, _, t0, w, _, _ = jobs[n]
                    if n >= GROUP:
                        pe.wait_ge(centred_ready, n - GROUP + 1)
                    for c in range(C):
                        mm = pe.matmul(ps[:, n % GROUP, 0:w], consts["mean"][:, :], src[:, c, t0:t0 + w],
                                       start=c == 0, stop=c == C - 1)
                    mm.then_inc(mean_ready, 1)

                AHEAD = 2
                for n in range(-AHEAD, len(jobs)):
                    if n + AHEAD < len(jobs) and not rms:
                        mean(n + AHEAD)
                    if n < 0:
                        continue
                    w = jobs[n][3]
                    pe.wait_ge(squared_ready, n + 1)
                    if n >= GROUP:
                        pe.wait_ge(log_ready, n - GROUP + 1)
                    for c in range(C):
                        mm = pe.matmul(ps[:, GROUP + n % GROUP, 0:w], consts["mean"][:, :], squared[:, n % GROUP, c, 0:w],
                                       start=c == 0, stop=c == C - 1)
                    mm.then_inc(var_ready, 1)

            @block.vector
            def _(dve):
                for group in groups:
                    for n in group if not rms else []:
                        src, dst, t0, w, _, _ = jobs[n]
                        dve.wait_ge(mean_ready, n + 1)
                        dve.tensor_tensor(centred(n), src[:, :, t0:t0 + w],
                                          ps[:, n % GROUP, 0:w].unsqueeze(1).broadcast_to([P, C, w]),
                                          ALU.subtract).then_inc(centred_ready, 1)
                    for n in group:
                        _, dst, t0, w, _, _ = jobs[n]
                        dve.wait_ge(rstd_ready, n + 1)
                        dve.tensor_tensor(dst[:, :, t0:t0 + w], centred(n),
                                          rstd[:, n % GROUP, 0:w].unsqueeze(1).broadcast_to([P, C, w]),
                                          ALU.mult).then_inc(normed, 1)

            @block.scalar
            def _(act):
                for group in groups:
                    for n in group:
                        if not rms:
                            act.wait_ge(centred_ready, n + 1)
                        if n >= GROUP:
                            act.wait_ge(var_ready, n - GROUP + 1)
                        act.activation(squared[:, n % GROUP, :, 0:jobs[n][3]], centred(n), ACT.Square).then_inc(squared_ready, 1)
                    for n in group:
                        w = jobs[n][3]
                        act.wait_ge(var_ready, n + 1)
                        act.activation(logvar[:, n % GROUP, 0:w], ps[:, GROUP + n % GROUP, 0:w], ACT.Ln,
                                       bias=consts["eps"][:, 0:1]).then_inc(log_ready, 1)
                    for n in group:
                        w = jobs[n][3]
                        act.wait_ge(log_ready, n + 1)
                        if n >= GROUP:
                            act.wait_ge(normed, n - GROUP + 1)
                        act.activation(rstd[:, n % GROUP, 0:w], logvar[:, n % GROUP, 0:w], ACT.Exp,
                                       scale=-0.5).then_inc(rstd_ready, 1)

            if affine:
                @block.gpsimd
                def _(pool):
                    for n in affine:
                        _, dst, t0, w, scale, shift = jobs[n]
                        pool.wait_ge(normed, n + 1)
                        for c in range(C):
                            part = dst[:, c, t0:t0 + w]
                            if shift is None:
                                pool.tensor_scalar(part, part, scale[:, c:c + 1], None, ALU.mult).then_inc(scaled, 1)
                            else:
                                pool.tensor_scalar(part, part, scale[:, c:c + 1], shift[:, c:c + 1],
                                                   ALU.mult, ALU.add).then_inc(scaled, 1)
                    pool.wait_ge(scaled, C * len(affine))


def norm_jobs(src, dst, scale=None, shift=None):
    return [(src, dst, n * BLK, BLK, scale, shift) for n in range(NBLK)]


def wait(engine, semaphore, value):
    if not isinstance(value, int) or value > 0:
        engine.wait_ge(semaphore, value)


def latent_attention(nc, consts, x, a, ctx_n, w_qkv, w_o):
    HP = 8
    DH = 64
    KEYS = S + CTX
    PIECE = KEYS // 3
    PW = PIECE + 1
    KT = S // P + 1
    QT = S // P
    UNITS = 2 * QT
    RING = 3
    assert PIECE * 3 == KEYS and PIECE % 2
    OWN = [slice(0, DH), slice(DH, P)]
    OTHER = [slice(DH, P), slice(0, DH)]
    AUX = [DH, 0]
    MAX_BANKS = (3, 6, 7)
    DEN_BANKS = (3, 6)
    PIECES = 3 * UNITS
    with ExitStack() as stack:
        sc = Scope(nc, stack, "A")
        wqkv = sc.sb("wqkv", [P, 3, C, P])
        wo = sc.sb("wo", [P, D])
        q_one = sc.sb("q_one", [P, 2, 2, S], F32R)
        q_two = sc.sb("q_two", [P, 2, 2, S], F32R)
        k_one = sc.sb("k_one", [P, 2, 2, KEYS + 1], F32R)
        k_two = sc.sb("k_two", [P, 2, 2, KEYS + 1], F32R)
        v_tok = sc.sb("v_tok", [P, 2, KT, P])
        probs = sc.sb("probs", [P, 2, RING, S])
        key_sums = sc.sb("key_sums", [P, 2, S])
        part_max = sc.sb("part_max", [P, UNITS, 3])
        nmax = sc.sb("nmax", [P, UNITS])
        nmax_rows = sc.sb("nmax_rows", [UNITS, P], F32R)
        logden = sc.sb("logden", [P, S])
        rden = sc.sb("rden", [P, S])
        heads = sc.sb("heads", [P, S])
        ps = sc.psum()
        names = """zeroed in_loaded out_loaded q_ps q_hi q_dup q_lo k_ps k_hi k_lo v_ps v_ready ctx_ps ctx_hi ctx_lo ctx_v
                   k_second piece_ps piece_max nmax_ready rows_ps rows_ready row_ready score_ps exp_ready
                   pv_ps summed den_ps logden_ready rden_ready heads_ready y_ps x_added"""
        s = {n: sc.sem(n) for n in names.split()}

        def bank_pair(b):
            return ps[:, b:b + 2, :].rearrange("p b n -> p (b n)")

        block = stack.enter_context(nc.Block())

        def units(engine, body, prologue=None):
            if prologue:
                prologue(0, 0)
            for b in range(B):
                body(b, b, b == 0, False)
            with engine.Fori(1, HP - 1) as hp:
                for b in range(B):
                    body(2 * hp + b, b, False, False)
            for b in range(B):
                body(2 * (HP - 1) + b, b, False, b == B - 1)

        @block.sync
        def _(sp):
            def load_in(pair):
                sp.dma_start(wqkv[:, :, :, :], w_qkv[pair].rearrange("o p t c n -> p (o t) c n")).then_inc(s["in_loaded"], 16)

            def load_out(pair):
                sp.dma_start(wo[:, :], w_o[pair].rearrange("o p n -> p (o n)")).then_inc(s["out_loaded"], 16)

            load_in(slice(0, 1))
            load_out(slice(0, 1))

            def reload(hp, pair):
                sp.wait_ge(s["v_ps"], 2 * hp)
                load_in(pair)
                sp.wait_ge(s["y_ps"], 4 * hp)
                load_out(pair)

            with sp.Fori(1, HP) as hp:
                reload(hp, bass.ds(hp, 1))

        @block.tensor
        def _(pe):
            def project(operand, b):
                for blk in range(2):
                    for c in range(C):
                        mm = pe.matmul(ps[:, 6 + blk, :], wqkv[:, operand, c, :],
                                       a[:, c, b * S + blk * BLK:b * S + (blk + 1) * BLK], start=c == 0, stop=c == C - 1)
                return mm

            def project_q(m, b):
                if b == 0:
                    pe.wait_ge(s["in_loaded"], 8 * m + 16)
                wait(pe, s["logden_ready"], 2 * m - 2)
                project(0, b).then_inc(s["q_ps"], 1)

            def project_k(m, b):
                if isinstance(m, int) and m < 2:
                    pe.wait_ge(s["q_lo"], 2 * m + 2)
                else:
                    pe.wait_ge(s["x_added"], 2 * m - 2)
                project(1, b).then_inc(s["k_ps"], 1)

            def project_ctx(m, b):
                for c in range(C):
                    pe.matmul(ps[:, 3, 0:CTX], wqkv[:, 1, c, :], ctx_n[:, c, b * CTX:(b + 1) * CTX],
                              start=c == 0, stop=c == C - 1)
                for c in range(C):
                    mm = pe.matmul(ps[0:CTX, 3, P:2 * P], ctx_n[:, c, b * CTX:(b + 1) * CTX], wqkv[:, 2, c, :],
                                   start=c == 0, stop=c == C - 1)
                mm.then_inc(s["ctx_ps"], 1)

            def project_v(m, b):
                pe.wait_ge(s["k_lo"], 2 * m + 2)
                for kt in range(KT - 1):
                    for c in range(C):
                        mm = pe.matmul(bank_pair(6)[:, kt * P:(kt + 1) * P], a[:, c, b * S + kt * P:b * S + (kt + 1) * P],
                                       wqkv[:, 2, c, :], start=c == 0, stop=c == C - 1)
                mm.then_inc(s["v_ps"], 1)

            def maxima(m, b, first, count):
                for i in range(first, min(first + count, PIECES)):
                    j, qt = divmod(i // 3, QT)
                    if i == 0:
                        pe.wait_ge(s["k_second"], 2 * m + 2)
                    elif i < 3:
                        pe.wait_ge(s["v_ready"], m + 1)
                    else:
                        pe.wait_ge(s["piece_max"], PIECES * m + i - 2)
                    pe.matmul(ps[:, MAX_BANKS[i % 3], 0:PW], q_one[:, b, j, qt * P:(qt + 1) * P],
                              k_one[:, b, j, (i % 3) * PIECE:(i % 3) * PIECE + PW], start=True, stop=True)\
                      .then_inc(s["piece_ps"], 1)

            def rows(m):
                pe.wait_ge(s["nmax_ready"], m + 1)
                pe.transpose(ps[0:UNITS, 7, 0:P], nmax[:, :], consts["ident"][:, :]).then_inc(s["rows_ps"], 1)

            def leave(n, c, q_after=None):
                if c == 0:
                    pe.wait_ge(s["heads_ready"], n + 1)
                    if q_after is not None:
                        pe.wait_ge(s["q_lo"], 2 * q_after + 2)
                else:
                    pe.wait_ge(s["x_added"], 2 * n + 1)
                for blk in range(2):
                    mm = pe.matmul(ps[:, 6 + blk, :], wo[:, c * P:(c + 1) * P], heads[:, blk * BLK:(blk + 1) * BLK],
                                   start=True, stop=True)
                mm.then_inc(s["y_ps"], 1)

            def values(n, b, kt, after=None):
                pe.wait_ge(s["exp_ready"], 4 * KT * n + 4 * kt + 4)
                if kt == 0:
                    wait(pe, s["heads_ready"], n)
                for blk in range(2):
                    for j in range(2):
                        mm = pe.matmul(ps[DH * j:DH * j + DH, 4 + blk, :], v_tok[:, b, kt, DH * j:DH * j + DH],
                                       probs[:, j, kt % RING, blk * BLK:(blk + 1) * BLK],
                                       start=kt == 0, stop=kt == KT - 1)
                        if (blk, j) == (1, 1):
                            mm.then_inc(s["pv_ps"], 1)
                        if after:
                            after()

            def denominators(n):
                pe.wait_ge(s["summed"], 2 * (KT - 1) * n + 2 * (KT - 1))
                pe.wait_ge(s["exp_ready"], 4 * KT * n + 4 * KT)
                for blk in range(2):
                    for j in range(2):
                        mm = pe.matmul(ps[DH * j:DH * j + DH, DEN_BANKS[blk], :], consts["ones"][:, 0:DH],
                                       key_sums[:, j, blk * BLK:(blk + 1) * BLK], start=True, stop=True)
                mm.then_inc(s["den_ps"], 1)

            def prologue(m, b):
                project_q(m, b)
                project_k(m, b)
                project_ctx(m, b)
                project_v(m, b)
                maxima(m, b, 0, PIECES)
                rows(m)

            def body(n, b, first, last):
                m, mb = n + 1, 1 - b
                if b == 1:
                    pe.wait_ge(s["out_loaded"], 8 * n + 8)
                pe.wait_ge(s["row_ready"], 32 * n + 32)
                pe.wait_ge(s["k_second"], 2 * n + 2)
                done = 0

                def more():
                    nonlocal done
                    if not last and kt >= 3 and done < PIECES:
                        maxima(m, mb, done, 1)
                        done += 1
                        if done == PIECES:
                            rows(m)

                for kt in range(KT):
                    kw = P if kt < KT - 1 else CTX
                    for j in range(2):
                        for blk in range(2):
                            cols = slice(blk * BLK, (blk + 1) * BLK)
                            half = 4 * kt + 2 * j + blk
                            if half >= 3:
                                pe.wait_ge(s["exp_ready"], 4 * KT * n + half - 2)
                            else:
                                wait(pe, s["exp_ready"], 4 * KT * n)
                            pe.matmul(ps[0:kw, half % 3, :], k_one[:, b, j, kt * P:kt * P + kw], q_one[:, b, j, cols],
                                      start=True, stop=False)
                            pe.matmul(ps[0:kw, half % 3, :], k_two[:, b, j, kt * P:kt * P + kw], q_two[:, b, j, cols],
                                      start=False, stop=True).then_inc(s["score_ps"], 1)
                            more()
                        if (kt, j) == (0, 0) and not last:
                            project_q(m, mb)
                        if kt == 1 and not first:
                            leave(n - 1, j, None if last else m)
                        if (kt, j) == (2, 0) and not last:
                            project_k(m, mb)
                            project_ctx(m, mb)
                        if j and kt:
                            values(n, b, kt - 1, more)
                        if (kt, j) == (2, 1) and not last:
                            project_v(m, mb)
                if not last:
                    kt = KT
                    while done < PIECES:
                        more()
                values(n, b, KT - 1)
                if last:
                    pe.wait_ge(s["x_added"], 2 * n)
                denominators(n)
                if last:
                    leave_last(n)

            def leave_last(n):
                pe.wait_ge(s["heads_ready"], n + 1)
                for c in range(C):
                    if c:
                        pe.wait_ge(s["x_added"], 2 * n + 1)
                    for blk in range(2):
                        mm = pe.matmul(ps[:, 6 + blk, :], wo[:, c * P:(c + 1) * P], heads[:, blk * BLK:(blk + 1) * BLK],
                                       start=True, stop=True)
                    mm.then_inc(s["y_ps"], 1)

            pe.wait_ge(s["zeroed"], 7)
            units(pe, body, prologue)

        @block.scalar
        def _(act):
            def q_hi(m, b):
                act.wait_ge(s["q_ps"], m + 1)
                for j in range(2):
                    act.activation(q_one[OWN[j], b, j, :], bank_pair(6)[OWN[j]], ACT.Copy).then_inc(s["q_hi"], 1)

            def k_hi(m, b):
                act.wait_ge(s["k_ps"], m + 1)
                for j in range(2):
                    act.activation(k_one[OWN[j], b, j, 0:S], bank_pair(6)[OWN[j]], ACT.Copy).then_inc(s["k_hi"], 1)

            def ctx_copy(m, b):
                act.wait_ge(s["ctx_ps"], m + 1)
                for j in range(2):
                    act.activation(k_one[OWN[j], b, j, S:KEYS], ps[OWN[j], 3, 0:CTX], ACT.Copy).then_inc(s["ctx_hi"], 1)
                act.activation(v_tok[0:CTX, b, KT - 1, :], ps[0:CTX, 3, P:2 * P], ACT.Copy).then_inc(s["ctx_v"], 1)

            def v_copy(m, b):
                act.wait_ge(s["v_ps"], m + 1)
                act.activation(v_tok[:, b, 0:KT - 1, :], ps[:, 6:8, :].rearrange("p b (t n) -> p (b t) n", n=P),
                               ACT.Copy).then_inc(s["v_ready"], 1)

            def send_rows(m, b):
                act.wait_ge(s["rows_ready"], m + 1)
                for j in range(2):
                    act.dma_start(q_two[AUX[j]:AUX[j] + 1, b, j, :].bitcast(F32).rearrange("o (t n) -> o t n", n=P),
                                  nmax_rows[j * QT:(j + 1) * QT, :].bitcast(F32)).then_inc(s["row_ready"], 16)

            def prologue(m, b):
                q_hi(m, b)
                k_hi(m, b)
                ctx_copy(m, b)
                v_copy(m, b)
                send_rows(m, b)

            def body(n, b, first, last):
                m, mb = n + 1, 1 - b
                for kt in range(KT):
                    kw = P if kt < KT - 1 else CTX
                    for j in range(2):
                        if kt >= RING:
                            act.wait_ge(s["pv_ps"], KT * n + kt - RING + 1)
                            act.wait_ge(s["summed"], 2 * (KT - 1) * n + 2 * max(kt - RING, 1))
                        for blk in range(2):
                            half = 4 * kt + 2 * j + blk
                            act.wait_ge(s["score_ps"], 4 * KT * n + half + 1)
                            act.activation(probs[0:kw, j, kt % RING, blk * BLK:(blk + 1) * BLK], ps[0:kw, half % 3, :],
                                           ACT.Exp, scale=1.0 / 8.0).then_inc(s["exp_ready"], 1)
                        if last:
                            continue
                        if (kt, j) == (0, 0):
                            q_hi(m, mb)
                        if (kt, j) == (2, 0):
                            k_hi(m, mb)
                            ctx_copy(m, mb)
                        if (kt, j) == (2, 1):
                            v_copy(m, mb)
                if not last:
                    send_rows(m, mb)
                act.wait_ge(s["den_ps"], n + 1)
                for blk in range(2):
                    act.activation(logden[:, blk * BLK:(blk + 1) * BLK], ps[:, DEN_BANKS[blk], :],
                                   ACT.Ln).then_inc(s["logden_ready"], 1)
                act.wait_ge(s["logden_ready"], 2 * n + 2)
                act.activation(rden[:, :], logden[:, :], ACT.Exp, scale=-1.0).then_inc(s["rden_ready"], 1)

            act.wait_ge(s["zeroed"], 7)
            units(act, body, prologue)

        @block.vector
        def _(dve):
            def prepare_q(m, b):
                for j in range(2):
                    dve.wait_ge(s["q_hi"], 2 * m + j + 1)
                    dve.tensor_tensor(q_two[OWN[j], b, j, :], bank_pair(6)[OWN[j]], q_one[OWN[j], b, j, :].bitcast(F32),
                                      ALU.subtract).then_inc(s["q_lo"], 1)
                for j in range(2):
                    dve.tensor_copy(q_one[OTHER[j], b, j, :], q_one[OWN[j], b, j, :].bitcast(F32)).then_inc(s["q_dup"], 1)

            def prepare_k(m, b):
                for j in range(2):
                    dve.wait_ge(s["k_hi"], 2 * m + j + 1)
                    dve.tensor_tensor(k_one[OTHER[j], b, j, 0:S], bank_pair(6)[OWN[j]], k_one[OWN[j], b, j, 0:S].bitcast(F32),
                                      ALU.subtract).then_inc(s["k_lo"], 1)
                dve.wait_ge(s["ctx_v"], m + 1)
                for j in range(2):
                    dve.wait_ge(s["ctx_hi"], 2 * m + j + 1)
                    dve.tensor_tensor(k_one[OTHER[j], b, j, S:KEYS], ps[OWN[j], 3, 0:CTX],
                                      k_one[OWN[j], b, j, S:KEYS].bitcast(F32), ALU.subtract).then_inc(s["ctx_lo"], 1)
                for j in range(2):
                    dve.tensor_copy(k_two[OWN[j], b, j, 0:KEYS], k_one[OWN[j], b, j, 0:KEYS].bitcast(F32)).then_inc(s["k_second"], 1)
                for i in range(PIECES):
                    dve.wait_ge(s["piece_ps"], PIECES * m + i + 1)
                    dve.tensor_reduce(part_max[:, i // 3, i % 3:i % 3 + 1], ps[:, MAX_BANKS[i % 3], 0:PIECE], AX.X,
                                      ALU.max).then_inc(s["piece_max"], 1)
                dve.wait_ge(s["piece_max"], PIECES * m + PIECES)
                dve.tensor_reduce(nmax[:, :], part_max[:, :, :], AX.X, ALU.max, negate=True).then_inc(s["nmax_ready"], 1)
                wait(dve, s["row_ready"], 32 * m)
                dve.wait_ge(s["rows_ps"], m + 1)
                dve.tensor_copy(nmax_rows[:, :], ps[0:UNITS, 7, 0:P]).then_inc(s["rows_ready"], 1)

            def add(n, b, c):
                dve.wait_ge(s["y_ps"], 2 * n + c + 1)
                part = x[:, c, b * S:(b + 1) * S]
                dve.tensor_tensor(part, part, bank_pair(6), ALU.add).then_inc(s["x_added"], 1)

            def body(n, b, first, last):
                if not last:
                    prepare_q(n + 1, 1 - b)
                if not first:
                    for c in range(C):
                        add(n - 1, 1 - b, c)
                if not last:
                    prepare_k(n + 1, 1 - b)
                dve.wait_ge(s["rden_ready"], n + 1)
                dve.wait_ge(s["pv_ps"], KT * n + KT)
                dve.tensor_tensor(heads[:, :], bank_pair(4), rden[:, :], ALU.mult).then_inc(s["heads_ready"], 1)
                if last:
                    for c in range(C):
                        add(n, b, c)
                    dve.wait_ge(s["x_added"], 2 * n + 2)

            def prologue(m, b):
                prepare_q(m, b)
                prepare_k(m, b)

            for buf in (q_two, k_one, k_two, v_tok):
                dve.memset(buf[:, :, :, :] if buf is v_tok else buf[:, :, :, :].bitcast(F32), 0.0).then_inc(s["zeroed"], 1)
            dve.wait_ge(s["zeroed"], 4)
            for j in range(2):
                dve.memset(k_two[AUX[j]:AUX[j] + 1, :, j, :].bitcast(F32), 1.0).then_inc(s["zeroed"], 1)
            dve.memset(part_max[:, :, :], 0.0).then_inc(s["zeroed"], 1)
            dve.wait_ge(s["zeroed"], 7)
            units(dve, body, prologue)

        @block.gpsimd
        def _(pool):
            def body(n, b, first, last):
                for kt in range(1, KT):
                    kw = P if kt < KT - 1 else CTX
                    for j in range(2):
                        pool.wait_ge(s["exp_ready"], 4 * KT * n + 4 * kt + 2 * j + 2)
                        if kt == 1:
                            before = probs[:, j, 0, :]
                            wait(pool, s["den_ps"], n)
                        else:
                            before = key_sums[0:kw, j, :]
                            pool.wait_ge(s["summed"], 2 * (KT - 1) * n + 2 * (kt - 2) + j + 1)
                        pool.tensor_tensor(key_sums[0:kw, j, :], before, probs[0:kw, j, kt % RING, :],
                                           ALU.add).then_inc(s["summed"], 1)

            units(pool, body)


def chain(engine, sem):
    count = [0]

    def step(instruction):
        count[0] += 1
        instruction.then_inc(sem, 1)
        engine.wait_ge(sem, count[0])
    return step


def top_experts(dve, step, order, score, left, index, keep, first, onehots, tops):
    wide = [P, TILES, E]
    for k, hot in enumerate(onehots):
        src = left if k else score
        step(dve.tensor_reduce(tops[k], src[:, :, :], AX.X, ALU.max))
        step(dve.tensor_tensor(index[:, :, :], src[:, :, :], tops[k].unsqueeze(2).broadcast_to(wide), ALU.is_equal))
        step(dve.tensor_tensor(index[:, :, :], index[:, :, :], order[:, :].unsqueeze(1).broadcast_to(wide), ALU.mult))
        step(dve.tensor_reduce(first, index[:, :, :], AX.X, ALU.max))
        step(dve.tensor_tensor(hot[:, :, :], index[:, :, :], first.unsqueeze(2).broadcast_to(wide), ALU.is_equal))
        if k + 1 < len(onehots):
            step(dve.tensor_scalar(keep[:, :, :], hot[:, :, :], -1.0, 1.0, ALU.mult, ALU.add))
            step(dve.tensor_tensor(index[:, :, :], score[:, :, :], keep[:, :, :], ALU.mult))
            step(dve.tensor_scalar(keep[:, :, :], hot[:, :, :], -3.0e38, None, ALU.mult))
            step(dve.tensor_tensor(left[:, :, :], index[:, :, :], keep[:, :, :], ALU.add))


def router_stage(nc, stage, kind, consts, y, router_w, bias, small, order, temperature, gates_t, gates_dram, weights,
                 split):
    G = B * E
    wide = [P, TILES, E]
    with ExitStack() as stack:
        sc = Scope(nc, stack, stage)
        score, left, index, keep, gates, expd = (sc.sb(n, wide) for n in ("score", "left", "index", "keep", "gates", "expd"))
        hot = [sc.sb(f"hot{k}", wide) for k in range(1 if kind == "top1" else 2)]
        rowv = sc.sb("rowv", [P, 8, TILES])
        colv = sc.sb("colv", [P, 5, G])
        temp = sc.sb("temp", [P, 2])
        ps = sc.psum()
        small_loaded, logits_ps, dve_step = sc.sem("small_loaded"), sc.sem("logits_ps"), sc.sem("dve_step")
        act_asked, act_done = sc.sem("act_asked"), sc.sem("act_done")
        maxima_ready, maxima_all = sc.sem("maxima_ready"), sc.sem("maxima_all")
        sums_ready, sums_all = sc.sem("sums_ready"), sc.sem("sums_all")
        gates_ready, turned_ps, gates_copied, stored = (sc.sem(n) for n in ("gates_ready", "turned_ps", "gates_copied", "stored"))
        rounds = 3 if kind == "sinkhorn" else 0
        block = stack.enter_context(nc.Block())

        @block.sync
        def _(sp):
            for dst, src in small:
                sp.dma_start(dst, src).then_inc(small_loaded, 16)
            for dst, src, loaded in weights:
                sp.dma_start(dst, src).then_inc(loaded, 16)
            sp.wait_ge(gates_copied, 1)
            sp.dma_start(gates_dram, gates_t[:, :]).then_inc(stored, 16)
            sp.wait_ge(stored, 16)

        @block.tensor
        def _(pe):
            pe.wait_ge(small_loaded, 16 * len(small))
            for t in range(TILES):
                for c in range(C):
                    mm = pe.matmul(ps[:, 0, t * E:(t + 1) * E], y[:, c, t * P:(t + 1) * P], router_w[:, c, :],
                                   start=c == 0, stop=c == C - 1)
            mm.then_inc(logits_ps, 1)
            for r in range(rounds):
                pe.wait_ge(sums_ready, r + 1)
                pe.matmul(ps[:, 1, 0:G], consts["ones"][:, :], colv[:, 3, :], start=True, stop=True).then_inc(sums_all, 1)
            pe.wait_ge(gates_ready, 1)
            for t in range(TILES):
                mm = pe.transpose(ps[0:E, 4 + t // 4, (t % 4) * P:(t % 4 + 1) * P], gates[:, t, :], consts["ident"][:, :])
            mm.then_inc(turned_ps, 1)

        @block.vector
        def _(dve):
            step = chain(dve, dve_step)
            asked = [0]

            def act_does():
                asked[0] += 1
                dve.sem_inc(act_asked, 1)
                dve.wait_ge(act_done, asked[0])

            def per_token(v):
                return v.unsqueeze(2).broadcast_to(wide)

            def by_expert(v):
                return v.rearrange("p (b t) e -> p b e t", b=B)

            def per_expert(v):
                return v.rearrange("p (b e) -> p b e", b=B).unsqueeze(3).broadcast_to([P, B, E, TILES // B])

            def grouped(v):
                return v.rearrange("p (b e) -> p b e", b=B)

            split.vector(dve)
            dve.wait_ge(small_loaded, 16 * len(small))
            dve.wait_ge(logits_ps, 1)
            logits = ps[:, 0, 0:TILES * E].rearrange("p (t e) -> p t e", e=E)
            if bias is not None:
                step(dve.tensor_tensor(score[:, :, :], logits, bias.unsqueeze(1).broadcast_to(wide), ALU.add))
            else:
                step(dve.tensor_copy(score[:, :, :], logits))
            if kind == "sinkhorn":
                s4 = by_expert(score[:, :, :])
                step(dve.tensor_scalar(temp[:, 0:1], temperature, 0.1, None, ALU.max))
                step(dve.reciprocal(temp[:, 1:2], temp[:, 0:1]))
                step(dve.tensor_scalar(score[:, :, :], score[:, :, :], temp[:, 1:2], None, ALU.mult))
                for r in range(rounds):
                    step(dve.tensor_reduce(rowv[:, 0, :], score[:, :, :], AX.X, ALU.max))
                    step(dve.tensor_tensor(score[:, :, :], score[:, :, :], per_token(rowv[:, 0, :]), ALU.subtract))
                    act_does()
                    step(dve.tensor_reduce(rowv[:, 1, :], expd[:, :, :], AX.X, ALU.add))
                    act_does()
                    step(dve.tensor_tensor(score[:, :, :], score[:, :, :], per_token(rowv[:, 2, :]), ALU.subtract))
                    step(dve.tensor_reduce(grouped(colv[:, 0, :]), s4, AX.X, ALU.max))
                    dve.sem_inc(maxima_ready, 1)
                    dve.wait_ge(maxima_all, r + 1)
                    step(dve.tensor_tensor(s4, s4, per_expert(colv[:, 1, :]), ALU.subtract))
                    act_does()
                    step(dve.tensor_reduce(grouped(colv[:, 3, :]), by_expert(expd[:, :, :]), AX.X, ALU.add))
                    dve.sem_inc(sums_ready, 1)
                    dve.wait_ge(sums_all, r + 1)
                    act_does()
                    step(dve.tensor_tensor(s4, s4, per_expert(colv[:, 4, :]), ALU.subtract))
                act_does()
                step(dve.tensor_reduce(rowv[:, 3, :], expd[:, :, :], AX.X, ALU.add))
                step(dve.tensor_scalar(rowv[:, 3, :], rowv[:, 3, :], 1e-8, None, ALU.add))
                step(dve.reciprocal(rowv[:, 4, :], rowv[:, 3, :]))
                step(dve.tensor_tensor(score[:, :, :], expd[:, :, :], per_token(rowv[:, 4, :]), ALU.mult))
            tops = [rowv[:, 5, :], rowv[:, 6, :]]
            top_experts(dve, step, order, score, left, index, keep, rowv[:, 7, :], hot, tops)
            if kind == "top1":
                dve.tensor_copy(gates[:, :, :], hot[0][:, :, :]).then_inc(gates_ready, 1)
                return
            if kind == "top2":
                step(dve.tensor_tensor(rowv[:, 0, :], tops[1], tops[0], ALU.subtract))
                act_does()
                step(dve.tensor_scalar(rowv[:, 2, :], rowv[:, 1, :], 1.0, None, ALU.add))
                step(dve.reciprocal(rowv[:, 3, :], rowv[:, 2, :]))
                step(dve.tensor_tensor(rowv[:, 4, :], rowv[:, 1, :], rowv[:, 3, :], ALU.mult))
            else:
                step(dve.tensor_tensor(rowv[:, 0, :], tops[1], tops[0], ALU.add))
                step(dve.tensor_scalar(rowv[:, 1, :], rowv[:, 0, :], 1e-8, None, ALU.add))
                step(dve.reciprocal(rowv[:, 2, :], rowv[:, 1, :]))
                step(dve.tensor_tensor(rowv[:, 3, :], tops[0], rowv[:, 2, :], ALU.mult))
                step(dve.tensor_tensor(rowv[:, 4, :], tops[1], rowv[:, 2, :], ALU.mult))
            for k in range(2):
                step(dve.tensor_tensor(hot[k][:, :, :], hot[k][:, :, :], per_token(rowv[:, 3 + k, :]), ALU.mult))
            dve.tensor_tensor(gates[:, :, :], hot[0][:, :, :], hot[1][:, :, :], ALU.add).then_inc(gates_ready, 1)

        @block.scalar
        def _(act):
            def answer(n, out, in_, func):
                act.wait_ge(act_asked, n)
                act.activation(out, in_, func).then_inc(act_done, 1)

            split.scalar(act)
            for r in range(rounds):
                answer(4 * r + 1, expd[:, :, :], score[:, :, :], ACT.Exp)
                answer(4 * r + 2, rowv[:, 2, :], rowv[:, 1, :], ACT.Ln)
                answer(4 * r + 3, expd[:, :, :], score[:, :, :], ACT.Exp)
                answer(4 * r + 4, colv[:, 4, :], ps[:, 1, 0:G], ACT.Ln)
            if kind == "sinkhorn":
                answer(4 * rounds + 1, expd[:, :, :], score[:, :, :], ACT.Exp)
            if kind == "top2":
                answer(1, rowv[:, 1, :], rowv[:, 0, :], ACT.Exp)
            act.wait_ge(turned_ps, 1)
            act.activation(gates_t[:, :], ps[0:E, 4:8, :].rearrange("p b n -> p (b n)"), ACT.Copy).then_inc(gates_copied, 1)

        if rounds:
            @block.gpsimd
            def _(pool):
                for r in range(rounds):
                    pool.wait_ge(maxima_ready, r + 1)
                    pool.partition_all_reduce(colv[:, 1, :], colv[:, 0, :], P, bass.bass_isa.ReduceOp.max).then_inc(maxima_all, 1)


class Split:

    def __init__(self, sc, x, y, raw_in, raw_out, raw_loaded, plus):
        self.x, self.y, self.raw_in, self.raw_out, self.raw_loaded, self.plus = x, y, raw_in, raw_out, raw_loaded, plus
        self.pairs = raw_in.shape[1]
        self.parts = self.pairs + 1
        self.y_hi = sc.sb("y_hi", [P, C, T], F32R)
        self.y_lo = sc.sb("y_lo", [P, C, T], F32R)
        self.into = sc.sb("in_split", [P, 2, 2] + list(raw_in.shape[1:]), F32R)
        self.out = sc.sb("out_split", [P, 2, 2] + list(raw_out.shape[1:]), F32R)
        names = "y_hi_ready y_lo_ready w_hi_ready w_lo_ready plus_added"
        self.sems = {n: sc.sem(n) for n in names.split()}

    def raw(self, j):
        return self.raw_in[:, j] if j < self.pairs else self.raw_out[:, :, :]

    def part(self, j, u, which):
        return self.into[:, u, which, j] if j < self.pairs else self.out[:, u, which]

    def weights_hi(self, act, u, j):
        act.activation(self.part(j, u, 0), self.raw(j), ACT.Copy).then_inc(self.sems["w_hi_ready"], 1)

    def weights_lo(self, dve, e, u, j):
        dve.wait_ge(self.sems["w_hi_ready"], self.parts * e + j + 1)
        dve.tensor_tensor(self.part(j, u, 1), self.raw(j), self.part(j, u, 0).bitcast(F32),
                          ALU.subtract).then_inc(self.sems["w_lo_ready"], 1)

    def scalar(self, act):
        for t in range(NBLK):
            cells = (slice(None), slice(None), slice(t * BLK, (t + 1) * BLK))
            act.activation(self.y_hi[cells], self.y[cells], ACT.Copy).then_inc(self.sems["y_hi_ready"], 1)
        act.wait_ge(self.raw_loaded, 32)
        for j in range(self.parts):
            self.weights_hi(act, 0, j)

    def vector(self, dve):
        for t in range(NBLK):
            cells = (slice(None), slice(None), slice(t * BLK, (t + 1) * BLK))
            for more in self.plus:
                dve.tensor_tensor(self.x[cells], self.x[cells], more[cells], ALU.add).then_inc(self.sems["plus_added"], 1)
            dve.wait_ge(self.sems["y_hi_ready"], t + 1)
            dve.tensor_tensor(self.y_lo[cells], self.y[cells], self.y_hi[cells].bitcast(F32),
                              ALU.subtract).then_inc(self.sems["y_lo_ready"], 1)
        for j in range(self.parts):
            self.weights_lo(dve, 0, 0, j)
        dve.wait_ge(self.sems["w_lo_ready"], self.parts)


def experts_stage(nc, stage, func, x, hidden, w_in, w_out, b_in, b_out, gates_t, gates_dram, spl):
    MC = hidden // P
    pairs = w_in.shape[2]
    PARTS = pairs + 1
    STEPS = NBLK * MC
    NS, NH = 2, 4
    CREDIT = 4
    with ExitStack() as stack:
        sc = Scope(nc, stack, stage)
        y_hi, y_lo, in_split, out_split, raw_loaded = spl.y_hi, spl.y_lo, spl.into, spl.out, spl.raw_loaded
        gate = sc.sb("gate", [P, 2, T])
        bias_in = sc.sb("bias_in", [P, 2, MC]) if b_in is not None else None
        GATE_LOADS = 16 if b_in is None else 32
        active = sc.sb("active", [P, NS, BLK])
        product = sc.sb("product", [P, NS, BLK]) if pairs == 2 else active
        gated = sc.sb("gated", [P, NS, BLK])
        split = sc.sb("split", [P, NH, 2, BLK], F32R)
        ps = sc.psum()
        s = {n: sc.sem(n) for n in """hidden_ps active_ready product_ready gated_ready hi_ready lo_ready out_ps x_added""".split()}
        s.update(spl.sems)
        gate_loaded = [sc.sem(f"gate_loaded{u}") for u in range(2)]
        if pairs == 1:
            s["product_ready"] = s["active_ready"]
        with nc.Block() as starting:
            @starting.vector
            def _(dve):
                for name in ["active_ready", "gated_ready", "lo_ready", "out_ps", "x_added"] + ["product_ready"] * (pairs == 2):
                    dve.sem_inc(s[name], CREDIT)

        block = stack.enter_context(nc.Block())

        def after(engine, name, n, more=0):
            engine.wait_ge(s[name], n + (more + CREDIT))

        def blocks_of(t):
            return slice(t * BLK, (t + 1) * BLK)

        def experts(engine, body):
            with engine.Fori(0, E // 2 - 1) as g:
                for u in range(2):
                    body(2 * g + u, u, False)
            for u in range(2):
                body(E - 2 + u, u, u == 1)

        def splits(e, u, q):
            return [q // 2 - 1] if q % 2 == 0 and 0 <= q // 2 - 1 < PARTS else []

        @block.sync
        def _(sp):
            def load_weights(e):
                sp.dma_start(spl.raw_in[:, :, :, :], w_in[e].rearrange("o p i c n -> p (o i) c n")).then_inc(raw_loaded, 16)
                sp.dma_start(spl.raw_out[:, :, :], w_out[e].rearrange("o p m n -> p (o m) n")).then_inc(raw_loaded, 16)

            def load_gates(e, u):
                sp.dma_start(gate[:, u, :], gates_dram[e].broadcast_to([P, T])).then_inc(gate_loaded[u], 16)
                if b_in is not None:
                    sp.dma_start(bias_in[:, u, :], b_in[e].rearrange("o p m -> p (o m)")).then_inc(gate_loaded[u], 16)

            for u in range(2):
                load_gates(slice(u, u + 1), u)
            sp.wait_ge(s["w_lo_ready"], PARTS)
            load_weights(slice(1, 2))
            with sp.Fori(0, E // 2 - 1) as g:
                for u in range(2):
                    sp.wait_ge(s["w_lo_ready"], PARTS * (2 * g + u + 2))
                    load_weights(bass.ds(2 * g + u + 2, 1))
                    after(sp, "gated_ready", STEPS * (2 * g + u + 1))
                    load_gates(bass.ds(2 * g + u + 2, 1), u)

        @block.tensor
        def _(pe):
            def into_hidden(e, u, q):
                t, m = divmod(q, MC)
                if q == 0:
                    pe.wait_ge(s["w_lo_ready"], PARTS * (e + 1))
                if m == 0:
                    pe.wait_ge(s["y_lo_ready"], t + 1)
                after(pe, "product_ready", STEPS * e, q - 1)
                for i in range(pairs):
                    k = 0
                    for w_part, y_part in ((0, y_hi), (0, y_lo), (1, y_hi)):
                        for c in range(C):
                            mm = pe.matmul(ps[:, pairs * (q % 2) + i, :], in_split[:, u, w_part, i, c, m * P:(m + 1) * P],
                                           y_part[:, c, blocks_of(t)], start=k == 0, stop=k == 3 * C - 1)
                            k += 1
                mm.then_inc(s["hidden_ps"], 1)

            def out(e, u, q, last):
                t, m = divmod(q, MC)
                after(pe, "lo_ready", STEPS * e, q + 1)
                if m == 0:
                    after(pe, "x_added", NBLK * e, t - 1)
                for c in range(C):
                    bank = ps[:, 4 + 2 * (t % 2) + c, :]
                    with_bias = last and m == 0 and b_out is not None
                    if with_bias:
                        pe.matmul(bank, b_out[:, c * P:(c + 1) * P], gates_t[:, blocks_of(t)], start=True, stop=False)
                    for k, (w_part, h_part) in enumerate(((0, 0), (0, 1), (1, 0))):
                        mm = pe.matmul(bank, out_split[:, u, w_part, m, c * P:(c + 1) * P], split[:, q % NH, h_part, :],
                                       start=m == 0 and k == 0 and not with_bias, stop=m == MC - 1 and k == 2)
                mm.then_inc(s["out_ps"], 1)

            def body(e, u, last):
                for q in range(STEPS):
                    if q + 2 < STEPS:
                        into_hidden(e, u, q + 2)
                    elif not last:
                        into_hidden(e + 1, 1 - u, q + 2 - STEPS)
                    out(e, u, q, last)

            into_hidden(0, 0, 0)
            into_hidden(0, 0, 1)
            experts(pe, body)

        @block.scalar
        def _(act):
            def activate(e, u, q):
                m = q % MC
                act.wait_ge(s["hidden_ps"], STEPS * e + q + 1)
                after(act, "product_ready" if pairs == 2 else "gated_ready", STEPS * e, q - 1)
                bias = 0.0
                if b_in is not None:
                    bias = bias_in[:, u, m:m + 1]
                    if q == 0:
                        act.wait_ge(gate_loaded[u], 16 * e + (GATE_LOADS - 16 * u))
                act.activation(active[:, q % NS, :], ps[:, pairs * (q % 2), :], func, bias=bias).then_inc(s["active_ready"], 1)

            def hi(e, q):
                after(act, "gated_ready", STEPS * e, q + 1)
                after(act, "out_ps", STEPS * e, q + 1 - NH)
                act.activation(split[:, q % NH, 0, :], gated[:, q % NS, :], ACT.Copy).then_inc(s["hi_ready"], 1)

            def body(e, u, last):
                for q in range(STEPS):
                    if q + 1 < STEPS:
                        activate(e, u, q + 1)
                    elif not last:
                        activate(e + 1, 1 - u, 0)
                    hi(e, q)
                    for j in splits(e, u, q) if not last else []:
                        if j == 0:
                            act.wait_ge(raw_loaded, 32 * (e + 1) + 32)
                            after(act, "out_ps", STEPS * e)
                        spl.weights_hi(act, 1 - u, j)

            activate(0, 0, 0)
            experts(act, body)

        @block.vector
        def _(dve):
            def multiply(e, q):
                after(dve, "active_ready", STEPS * e, q + 1)
                after(dve, "gated_ready", STEPS * e, q - 1)
                dve.tensor_tensor(product[:, q % NS, :], active[:, q % NS, :], ps[:, pairs * (q % 2) + 1, :],
                                  ALU.mult).then_inc(s["product_ready"], 1)

            def lo(e, q):
                dve.wait_ge(s["hi_ready"], STEPS * e + q + 1)
                dve.tensor_tensor(split[:, q % NH, 1, :], gated[:, q % NS, :], split[:, q % NH, 0, :].bitcast(F32),
                                  ALU.subtract).then_inc(s["lo_ready"], 1)

            def body(e, u, last):
                for q in range(STEPS):
                    t, m = divmod(q, MC)
                    if pairs == 2:
                        if q + 1 < STEPS:
                            multiply(e, q + 1)
                        elif not last:
                            multiply(e + 1, 0)
                    lo(e, q)
                    for j in splits(e, u, q) if not last else []:
                        spl.weights_lo(dve, e + 1, 1 - u, j)
                    if m == MC - 1:
                        after(dve, "out_ps", STEPS * e, q + 1)
                        part = x[:, :, blocks_of(t)]
                        dve.tensor_tensor(part, part, ps[:, 4 + 2 * (t % 2):6 + 2 * (t % 2), :], ALU.add).then_inc(s["x_added"], 1)

            if pairs == 2:
                multiply(0, 0)
            experts(dve, body)
            after(dve, "x_added", NBLK * E)

        @block.gpsimd
        def _(pool):
            with pool.Fori(0, E // 2) as g:
                for u in range(2):
                    e = 2 * g + u
                    pool.wait_ge(gate_loaded[u], GATE_LOADS * (g + 1))
                    for q in range(STEPS):
                        after(pool, "product_ready", STEPS * e, q + 1)
                        after(pool, "lo_ready", STEPS * e, q - 1)
                        pool.tensor_tensor(gated[:, q % NS, :], product[:, q % NS, :], gate[:, u, blocks_of(q // MC)],
                                           ALU.mult).then_inc(s["gated_ready"], 1)


def moe(nc, name, kind, func, hidden, consts, x, y, t, plus):
    with ExitStack() as stack:
        sc = Scope(nc, stack, name)
        w_in, w_out = t[f"{name}_w_in"], t[f"{name}_w_out"]
        raw_in = sc.sb("raw_in", [P, w_in.shape[2], C, hidden])
        raw_out = sc.sb("raw_out", [P, hidden // P, D])
        raw_loaded = sc.sem("raw_loaded")
        weights = [(raw_in[:, :, :, :], w_in[0], raw_loaded), (raw_out[:, :, :], w_out[0], raw_loaded)]
        router_w = sc.sb("router_w", [P, C, E])
        order = sc.sb("order", [P, E])
        small = [(router_w[:, :, :], t[f"{name}_router_w"]), (order[:, :], t["c_order"])]
        bias = temperature = b_in = b_out = None
        if f"{name}_router_b" in t:
            bias_t = sc.sb("router_b", [P, E])
            small.append((bias_t[:, :], t[f"{name}_router_b"]))
            bias = bias_t[:, :]
        if kind == "sinkhorn":
            temp_t = sc.sb("temperature", [P, 1])
            small.append((temp_t[:, :], t[f"{name}_temperature"]))
            temperature = temp_t[:, 0:1]
        if f"{name}_b_in" in t:
            b_in = t[f"{name}_b_in"]
            b_out = sc.sb("b_out", [E, D])
            small.append((b_out[:, :], t[f"{name}_b_out"]))
        gates_t = sc.sb("gates_t", [E, T])
        gates_dram = t["scratch_gates_" + name]
        spl = Split(sc, x, y, raw_in, raw_out, raw_loaded, plus)
        router_stage(nc, name + "r", kind, consts, y, router_w, bias, small, order, temperature, gates_t, gates_dram, weights,
                     spl)
        experts_stage(nc, name + "e", func, x, hidden, w_in, w_out, b_in, b_out, gates_t, gates_dram, spl)


def context_attention(nc, name, consts, x, y, ctx, t):
    HG, DH = 8, 16
    GK = HG * CTX
    HALF = GK // 2
    CH = [(k * P, min(P, GK - k * P)) for k in range(-(-GK // P))]
    FULL = len(CH) - 1
    SHORT = CH[-1][1]
    TB = BLK // P

    def slot(g, i):
        return g * FULL + i if i < FULL else C * FULL + g

    with ExitStack() as stack:
        sc = Scope(nc, stack, name)
        w = {k: sc.sb(k, [P, C, D]) for k in ("wq", "wk", "wv", "wo")}
        bias = {k: sc.sb(k, [P, C]) for k in ("bq", "bk", "bv", "bo")}
        mask = sc.sb("mask", [P, HG])
        q = sc.sb("q", [P, C, T])
        k_feat, v_feat = sc.sb("k_feat", [P, C, B * CTX]), sc.sb("v_feat", [P, C, B * CTX])
        k_spread, v_spread = sc.sb("k_spread", [P, B, C, GK]), sc.sb("v_spread", [P, B, C, GK])
        v_rows = sc.sb("v_rows", [P, B, C, len(CH), P])
        with ExitStack() as setup:
            ss = Scope(nc, setup, name + "s")
            ps = ss.psum()
            loaded, kv_ps, kv_ready, spread_ready, turned_ps, turned, q_ps, q_ready = (
                ss.sem(n) for n in "loaded kv_ps kv_ready spread_ready turned_ps turned q_ps q_ready".split())
            loads = [(v[:, :, :], t[f"{name}_{k}"]) for k, v in w.items()] + \
                    [(v[:, :], t[f"{name}_{k}"]) for k, v in bias.items()] + [(mask[:, :], t["c_head_mask"])]
            block = setup.enter_context(nc.Block())

            @block.sync
            def _(sp):
                for dst, src in loads:
                    sp.dma_start(dst, src).then_inc(loaded, 16)
                sp.wait_ge(loaded, 16 * len(loads))

            @block.tensor
            def _(pe):
                pe.wait_ge(loaded, 16 * len(loads))
                for i, m in enumerate(("wk", "wv")):
                    for g in range(C):
                        for c in range(C):
                            mm = pe.matmul(ps[:, i, g * B * CTX:(g + 1) * B * CTX], w[m][:, c, g * P:(g + 1) * P],
                                           ctx[:, c, :], start=c == 0, stop=c == C - 1)
                    mm.then_inc(kv_ps, 1)
                for n in range(NBLK * C):
                    blk, g = divmod(n, C)
                    if n >= 4:
                        pe.wait_ge(q_ready, n - 3)
                    for c in range(C):
                        mm = pe.matmul(ps[:, 2 + n % 4, :], w["wq"][:, c, g * P:(g + 1) * P],
                                       y[:, c, blk * BLK:(blk + 1) * BLK], start=c == 0, stop=c == C - 1)
                    mm.then_inc(q_ps, 1)
                for n in range(B * C):
                    b, g = divmod(n, C)
                    pe.wait_ge(spread_ready, 2 * n + 2)
                    if n:
                        pe.wait_ge(turned, 2 * n)
                    for k, (r0, rows) in enumerate(CH):
                        mm = pe.transpose(ps[0:rows, 6 + k // 4, (k % 4) * P:(k % 4 + 1) * P],
                                          v_spread[:, b, g, r0:r0 + rows], consts["ident"][:, :])
                    mm.then_inc(turned_ps, 1)

            @block.scalar
            def _(act):
                for i, (dst, bv) in enumerate(((k_feat, "bk"), (v_feat, "bv"))):
                    act.wait_ge(kv_ps, i + 1)
                    for g in range(C):
                        act.activation(dst[:, g, :], ps[:, i, g * B * CTX:(g + 1) * B * CTX], ACT.Identity,
                                       bias=bias[bv][:, g:g + 1]).then_inc(kv_ready, 1)
                for n in range(NBLK * C):
                    blk, g = divmod(n, C)
                    act.wait_ge(q_ps, n + 1)
                    act.activation(q[:, g, blk * BLK:(blk + 1) * BLK], ps[:, 2 + n % 4, :], ACT.Identity,
                                   bias=bias["bq"][:, g:g + 1]).then_inc(q_ready, 1)

            @block.vector
            def _(dve):
                dve.wait_ge(kv_ready, 4)
                for b in range(B):
                    for g in range(C):
                        for dst, src in ((k_spread, k_feat), (v_spread, v_feat)):
                            dve.tensor_tensor(dst[:, b, g, :].rearrange("p (h k) -> p h k", h=HG),
                                              src[:, g, b * CTX:(b + 1) * CTX].unsqueeze(1).broadcast_to([P, HG, CTX]),
                                              mask[:, :].unsqueeze(2).broadcast_to([P, HG, CTX]),
                                              ALU.mult).then_inc(spread_ready, 1)
                for n in range(B * C):
                    b, g = divmod(n, C)
                    dve.wait_ge(turned_ps, n + 1)
                    dve.tensor_copy(v_rows[:, b, g, 0:4, :], ps[:, 6, :].rearrange("p (k n) -> p k n", n=P)).then_inc(turned, 1)
                    rows = CH[4][1]
                    dve.tensor_copy(v_rows[0:rows, b, g, 4, :], ps[0:rows, 7, 0:P]).then_inc(turned, 1)

        with ExitStack() as main:
            ms = Scope(nc, main, name + "m")
            NK = C * len(CH)
            diff = ms.sb("diff", [P, 2, C, GK])
            expd = ms.sb("expd", [P, 2, C, GK])
            probs = ms.sb("probs", [P, 2, C, GK])
            probs_t = ms.sb("probs_t", [P, 2, NK, BLK])
            attended = ms.sb("attended", [P, 2, C, BLK])
            top, total, share = (ms.sb(n, [P, 2, 2 * C, HG // 2]) for n in ("top", "total", "share"))
            ps = ms.psum()
            names = """score_ps top_ready diff_ready exp_ready sum_ready share_ready probs_ready turned_ps turned
                       out_ps out_ready y_ps x_added"""
            s = {n: ms.sem(n) for n in names.split()}
            block = main.enter_context(nc.Block())
            by_head = [P, 2 * C, HG // 2, CTX]

            def heads_of(buf, n):
                return buf[:, n % 2].rearrange("p g (a h k) -> p (g a) h k", a=2, h=HG // 2)

            @block.tensor
            def _(pe):
                def scores(n):
                    if n:
                        pe.wait_ge(s["diff_ready"], n)
                    for i in range(2 * C):
                        mm = pe.matmul(ps[:, i, 0:HALF], q[:, i // 2, n * P:(n + 1) * P],
                                       k_spread[:, n * P // S, i // 2, (i % 2) * HALF:(i % 2 + 1) * HALF],
                                       start=True, stop=True)
                    mm.then_inc(s["score_ps"], 1)

                def finish(blk, j):
                    if j < C:
                        pe.wait_ge(s["turned"], 2 * TB * (blk + 1))
                        if j:
                            pe.wait_ge(s["out_ready"], C * blk + j)
                        elif blk:
                            pe.wait_ge(s["x_added"], C * blk)
                        for i, (r0, rows) in enumerate(CH):
                            mm = pe.matmul(ps[:, 7, :], v_rows[0:rows, blk * BLK // S, j, i, :],
                                           probs_t[0:rows, blk % 2, slot(j, i), :], start=i == 0, stop=i == len(CH) - 1)
                        mm.then_inc(s["out_ps"], 1)
                    else:
                        c = j - C
                        pe.wait_ge(s["out_ready"], C * blk + C)
                        if c:
                            pe.wait_ge(s["x_added"], C * blk + c)
                        for g in range(C):
                            mm = pe.matmul(ps[:, 7, :], w["wo"][:, g, c * P:(c + 1) * P], attended[:, blk % 2, g, :],
                                           start=g == 0, stop=g == C - 1)
                        mm.then_inc(s["y_ps"], 1)

                scores(0)
                scores(1)
                for n in range(TILES):
                    if n + 2 < TILES:
                        scores(n + 2)
                    pe.wait_ge(s["probs_ready"], n + 1)
                    if n:
                        pe.wait_ge(s["turned"], 2 * n)
                    for k in range(NK):
                        g, i = divmod(k, len(CH))
                        r0, rows = CH[i]
                        k = slot(g, i)
                        mm = pe.transpose(ps[0:rows, 4 + k // 4, (k % 4) * P:(k % 4 + 1) * P],
                                          probs[:, n % 2, g, r0:r0 + rows], consts["ident"][:, :])
                    mm.then_inc(s["turned_ps"], 1)
                    if n >= TB:
                        finish(n // TB - 1, n % TB)
                for j in range(2 * C):
                    finish(NBLK - 1, j)

            @block.vector
            def _(dve):
                def before_exp(n):
                    dve.wait_ge(s["score_ps"], n + 1)
                    banks = ps[:, 0:2 * C, 0:HALF].rearrange("p a (h k) -> p a h k", k=CTX)
                    if n >= 2:
                        dve.wait_ge(s["exp_ready"], n - 1)
                    dve.tensor_reduce(top[:, n % 2], banks, AX.X, ALU.max).then_inc(s["top_ready"], 1)
                    dve.wait_ge(s["top_ready"], n + 1)
                    dve.tensor_tensor(heads_of(diff, n), banks, top[:, n % 2].unsqueeze(3).broadcast_to(by_head),
                                      ALU.subtract).then_inc(s["diff_ready"], 1)

                def add(blk, c):
                    dve.wait_ge(s["y_ps"], C * blk + c + 1)
                    part = x[:, c, blk * BLK:(blk + 1) * BLK]
                    dve.scalar_tensor_tensor(out=part, in0=ps[:, 7, :], scalar=bias["bo"][:, c:c + 1], in1=part,
                                             op0=ALU.add, op1=ALU.add).then_inc(s["x_added"], 1)

                before_exp(0)
                for n in range(TILES):
                    if n + 1 < TILES:
                        before_exp(n + 1)
                    dve.wait_ge(s["exp_ready"], n + 1)
                    dve.tensor_reduce(total[:, n % 2], heads_of(expd, n), AX.X, ALU.add).then_inc(s["sum_ready"], 1)
                    dve.wait_ge(s["sum_ready"], n + 1)
                    if n >= 2:
                        dve.wait_ge(s["probs_ready"], n - 1)
                    dve.reciprocal(share[:, n % 2], total[:, n % 2]).then_inc(s["share_ready"], 1)
                    if n > TB and (n - 1) % TB >= C:
                        add((n - 1) // TB - 1, (n - 1) % TB - C)
                add(NBLK - 2, C - 1)
                for c in range(C):
                    add(NBLK - 1, c)

            @block.scalar
            def _(act):
                def exp(n):
                    act.wait_ge(s["diff_ready"], n + 1)
                    if n >= 2:
                        act.wait_ge(s["probs_ready"], n - 1)
                        act.wait_ge(s["sum_ready"], n - 1)
                    act.activation(expd[:, n % 2].rearrange("p g k -> p (g k)"), diff[:, n % 2].rearrange("p g k -> p (g k)"),
                                   ACT.Exp, scale=DH ** -0.5).then_inc(s["exp_ready"], 1)

                def attend(blk, g):
                    act.wait_ge(s["out_ps"], C * blk + g + 1)
                    if blk >= 2:
                        act.wait_ge(s["y_ps"], C * (blk - 1))
                    act.activation(attended[:, blk % 2, g, :], ps[:, 7, :], ACT.Copy).then_inc(s["out_ready"], 1)

                exp(0)
                for n in range(TILES):
                    if n + 1 < TILES:
                        exp(n + 1)
                    blk, i = divmod(n, TB)
                    if n > TB and (n - 1) % TB < C:
                        attend((n - 1) // TB - 1, (n - 1) % TB)
                    act.wait_ge(s["turned_ps"], n + 1)
                    if blk >= 2:
                        act.wait_ge(s["out_ps"], C * (blk - 1))
                    banks = ps[:, 4:7, :].rearrange("p b (k n) -> p (b k) n", n=P)
                    for rows, k0, k1 in ((P, 0, C * FULL), (SHORT, C * FULL, NK)):
                        act.activation(probs_t[0:rows, blk % 2, k0:k1, i * P:(i + 1) * P], banks[0:rows, k0:k1],
                                       ACT.Copy).then_inc(s["turned"], 1)
                for g in range(C):
                    attend(NBLK - 1, g)

            @block.gpsimd
            def _(pool):
                for n in range(TILES):
                    pool.wait_ge(s["share_ready"], n + 1)
                    if n >= 2:
                        pool.wait_ge(s["turned_ps"], n - 1)
                    pool.tensor_tensor(heads_of(probs, n), heads_of(expd, n),
                                       share[:, n % 2].unsqueeze(3).broadcast_to(by_head), ALU.mult).then_inc(s["probs_ready"], 1)


def self_attention(nc, consts, h, r, t):
    GROUPS, NH, DH = 4, 4, 16
    HR = P // 2
    KT = S // P
    QB = S // BLK
    STEPS = QB * KT
    RING = 3
    AUX = 32
    V0 = 32
    PIECES = NH * KT * QB
    den, y_out, both, spread, value, piece, rows = "den", "y", "both", "spread", "value", "piece", "rows"
    VALUES = [range(0, 3), range(3, 6), range(6, KT)]
    Q0, Q1, K0, K1 = 0, 2, 4, 6
    LEAVING = [(den, 0), (den, 1)] + [(y_out, i) for i in range(4)]
    schedule = [[(den, 0), (den, 1), (both, 0), (both, 1)], [(y_out, i) for i in range(4)],
                [(spread, Q0), (spread, Q0 + 1), (spread, K0), (spread, K0 + 1)]] + [[] for _ in range(STEPS - 3)]
    for i in range(PIECES):
        schedule[3 + i * (STEPS - 4) // PIECES].append((piece, i))
    for i, late in enumerate([[(spread, Q1), (spread, Q1 + 1)], [(spread, K1), (spread, K1 + 1)]] + [[(value, k)] for k in range(3)]):
        schedule[3 + i] += late
    schedule[STEPS - 1].append((rows, 0))
    NEXT = [[job for job in jobs if job not in LEAVING] for jobs in schedule]
    NJ, NL = sum(map(len, NEXT)), len(LEAVING)
    assert NJ % 3 == 0 and NL % 3 == 0, "each unit starts with the same bank"
    UNITS = GROUPS * B

    def place_of(job, plan):
        return [j for jobs in plan for j in jobs].index(job)

    def jobs_of(first, last):
        if first:
            return NEXT
        return [[job for job in jobs if job in LEAVING] for jobs in schedule] if last else schedule

    def first_job(n, first):
        return NJ if first else (NJ + NL) * n + NJ - NL

    with ExitStack() as stack:
        sc = Scope(nc, stack, "F1")
        w_in = sc.sb("w_in", [P, 2, C, P])
        w_out = sc.sb("w_out", [P, D])
        k_one = sc.sb("k_one", [P, 1])
        place_hi_lo = sc.sb("place_hi_lo", [P, 4, 2, P], F32R)
        ones_at = sc.sb("ones_at", [P, P])
        den_to = sc.sb("den_to", [P, P])
        qk_hi = sc.sb("qk_hi", [P, QB, BLK], F32R)
        qk_lo = sc.sb("qk_lo", [P, QB, BLK], F32R)
        q_split = sc.sb("q_split", [P, B, 2, S], F32R)
        k_split = sc.sb("k_split", [P, B, NH, S], F32R)
        v_tok = sc.sb("v_tok", [P, B, KT, P])
        probs = sc.sb("probs", [P, RING, NH, BLK])
        part_max = sc.sb("part_max", [P, NH * KT, QB])
        nmax = sc.sb("nmax", [P, NH * KT])
        nmax_rows = sc.sb("nmax_rows", [NH * KT, P], F32R)
        raw = sc.sb("raw", [P, S])
        dens = sc.sb("dens", [P, S])
        logden = sc.sb("logden", [P, S])
        rden = sc.sb("rden", [P, S])
        heads = sc.sb("heads", [P, S])
        ps = sc.psum()
        names = """setup zeroed in_loaded out_loaded job_ps taken hi_ready nmax_ready row_ready
                   score_ps exp_ready pv_ps raw_ready logden_ready rden_ready heads_ready"""
        s = {n: sc.sem(n) for n in names.split()}
        block = stack.enter_context(nc.Block())

        def units(engine, body):
            for b in range(B):
                body(b, b, b == 0, False)
            with engine.Fori(1, GROUPS - 1) as g:
                for b in range(B):
                    body(B * g + b, b, False, False)
            for b in range(B):
                body(UNITS - B + b, b, False, b == B - 1)

        @block.sync
        def _(sp):
            def load_in(g):
                sp.dma_start(w_in[:, :, :, :], t["F1_w_in"][g].rearrange("o p t c n -> p (o t) c n")).then_inc(s["in_loaded"], 16)

            def load_out(g):
                sp.dma_start(w_out[:, :], t["F1_w_out"][g].rearrange("o p n -> p (o n)")).then_inc(s["out_loaded"], 16)

            def reload(g, first):
                n, plan = B * g, jobs_of(first, False)
                if not first:
                    sp.wait_ge(s["taken"], first_job(n, False) + place_of((y_out, 3), plan) + 1)
                    load_out(bass.ds(g, 1))
                sp.wait_ge(s["taken"], first_job(n, first) + place_of((value, 2), plan) + 1)
                load_in(slice(1, 2) if first else bass.ds(g + 1, 1))

            for dst, src in ((k_one[:, :], t["F1_k_one"]), (ones_at[:, :], t["F1_ones_at"]), (den_to[:, :], t["F1_den_to"]),
                             (raw[:, :], t["F1_place"])):
                sp.dma_start(dst, src).then_inc(s["setup"], 16)
            load_in(slice(0, 1))
            load_out(slice(0, 1))
            reload(0, True)
            with sp.Fori(1, GROUPS - 1) as g:
                reload(g, False)
            last_group = GROUPS - 1
            sp.wait_ge(s["taken"], first_job(B * last_group, False) + place_of((y_out, 3), schedule) + 1)
            load_out(slice(last_group, last_group + 1))

        @block.tensor
        def _(pe):
            def fill(kind, i, m, mb, left, base, place, plan=None):
                if not (isinstance(base, int) and base + place < 3):
                    pe.wait_ge(s["taken"], base + place - 2)
                bank = ps[:, 3 + place % 3, :]
                if kind == den:
                    pe.wait_ge(s["raw_ready"], left + 1)
                    mm = pe.matmul(bank, den_to[:, :], raw[:, i * BLK:(i + 1) * BLK], start=True, stop=True)
                elif kind == y_out:
                    c, blk = divmod(i, QB)
                    pe.wait_ge(s["heads_ready"], left + 1)
                    mm = pe.matmul(bank, w_out[:, c * P:(c + 1) * P], heads[:, blk * BLK:(blk + 1) * BLK], start=True, stop=True)
                elif kind == both:
                    for c in range(C):
                        mm = pe.matmul(bank, w_in[:, 0, c, :], r[:, c, mb * S + i * BLK:mb * S + (i + 1) * BLK],
                                       start=c == 0, stop=c == C - 1)
                elif kind == spread:
                    o, blk = divmod(i, QB)
                    pe.wait_ge(s["taken"], base + place_of((both, blk), plan) + 1)
                    pe.matmul(bank, place_hi_lo[:, o, 0, :], qk_hi[:, blk, :], start=True, stop=False)
                    mm = pe.matmul(bank, place_hi_lo[:, o, 1, :], qk_lo[:, blk, :], start=False, stop=True)
                elif kind == value:
                    for at, kt in enumerate(VALUES[i]):
                        t0 = mb * S + kt * P
                        for c in range(C):
                            mm = pe.matmul(bank[:, at * P:(at + 1) * P], r[:, c, t0:t0 + P], w_in[:, 1, c, :],
                                           start=c == 0, stop=c == C - 1)
                elif kind == piece:
                    if i == 0:
                        pe.wait_ge(s["taken"], base + place)
                    hd, qt, kb = i // (KT * QB), i // QB % KT, i % QB
                    mm = pe.matmul(bank, q_split[:, mb, hd // 2, qt * P:(qt + 1) * P],
                                   k_split[:, mb, hd, kb * BLK:(kb + 1) * BLK], start=True, stop=True)
                else:
                    pe.wait_ge(s["nmax_ready"], m + 1)
                    mm = pe.transpose(bank[0:NH * KT, 0:P], nmax[:, :], consts["ident"][:, :])
                mm.then_inc(s["job_ps"], 1)

            def pv(n, b, i, between):
                blk, kt = divmod(i, KT)
                pe.wait_ge(s["exp_ready"], NH * STEPS * n + NH * i + NH)
                if i == 0:
                    wait(pe, s["raw_ready"], n)
                for hd in range(NH):
                    mm = pe.matmul(ps[V0 * hd:V0 * hd + V0, 6 + blk, :], v_tok[:, b, kt, V0 * hd:V0 * hd + V0],
                                   probs[:, i % RING, hd, :], start=kt == 0, stop=kt == KT - 1)
                    if hd == NH - 1:
                        mm.then_inc(s["pv_ps"], 1)
                    between()

            def body(n, b, first, last):
                base, place = first_job(n, first), 0
                if b == 1:
                    pe.wait_ge(s["out_loaded"], 8 * n + 8)
                    if not last:
                        pe.wait_ge(s["in_loaded"], 8 * n + 24)
                pe.wait_ge(s["row_ready"], 64 * n + 64)
                plan = jobs_of(first, last)
                for i, jobs in enumerate(plan):
                    blk, kt = divmod(i, KT)
                    done = 0

                    def next_job(early=False):
                        nonlocal place, done
                        if done < len(jobs) and (not early or jobs[done][0] in (piece, rows)):
                            fill(*jobs[done], n + 1, 1 - b, n - 1, base, place, plan)
                            place, done = place + 1, done + 1

                    for hd in range(NH):
                        k = NH * i + hd
                        if k >= 3:
                            pe.wait_ge(s["exp_ready"], NH * STEPS * n + k - 2)
                        else:
                            wait(pe, s["exp_ready"], NH * STEPS * n)
                        pe.matmul(ps[:, k % 3, :], k_split[:, b, hd, kt * P:(kt + 1) * P],
                                  q_split[:, b, hd // 2, blk * BLK:(blk + 1) * BLK], start=True, stop=True)\
                          .then_inc(s["score_ps"], 1)
                        next_job(early=True)
                    if i:
                        pv(n, b, i - 1, next_job)
                    while done < len(jobs):
                        next_job()
                pv(n, b, STEPS - 1, lambda: None)
                if last:
                    for place, (kind, i) in enumerate(LEAVING):
                        fill(kind, i, None, None, n, base + NL, place)

            pe.wait_ge(s["setup"], 64)
            pe.wait_ge(s["in_loaded"], 16)
            pe.wait_ge(s["zeroed"], 2)
            place = 0
            for jobs in NEXT:
                for kind, i in jobs:
                    fill(kind, i, 0, 0, None, 0, place, NEXT)
                    place += 1
            units(pe, body)

        @block.scalar
        def _(act):
            def round_both(blk, base, plan):
                place = place_of((both, blk), plan)
                act.wait_ge(s["job_ps"], base + place + 1)
                act.activation(qk_hi[:, blk, :], ps[:, 3 + place % 3, :], ACT.Copy).then_inc(s["hi_ready"], 1)

            def send_rows(b, base, plan):
                act.wait_ge(s["taken"], base + place_of((rows, 0), plan) + 1)
                for hd in range(NH):
                    row = AUX + HR * (hd % 2)
                    act.dma_start(q_split[row:row + 1, b, hd // 2, :].bitcast(F32).rearrange("o (t n) -> o t n", n=P),
                                  nmax_rows[hd * KT:(hd + 1) * KT, :].bitcast(F32)).then_inc(s["row_ready"], 16)

            def invert(n, base, plan):
                act.wait_ge(s["taken"], base + place_of((den, 1), plan) + 1)
                act.activation(logden[:, :], dens[:, :], ACT.Ln).then_inc(s["logden_ready"], 1)
                act.wait_ge(s["logden_ready"], n + 1)
                act.activation(rden[:, :], logden[:, :], ACT.Exp, scale=-1.0).then_inc(s["rden_ready"], 1)

            def body(n, b, first, last):
                base, plan = first_job(n, first), jobs_of(first, last)
                for i, jobs in enumerate(plan):
                    if i >= RING:
                        act.wait_ge(s["pv_ps"], STEPS * n + i - RING + 1)
                    for hd in range(NH):
                        k = NH * i + hd
                        act.wait_ge(s["score_ps"], NH * STEPS * n + k + 1)
                        act.activation(probs[:, i % RING, hd, :], ps[:, k % 3, :], ACT.Exp,
                                       scale=DH ** -0.5).then_inc(s["exp_ready"], 1)
                        if (rows, 0) in jobs and hd == 2:
                            send_rows(1 - b, base, plan)
                    if (den, 0) in jobs:
                        invert(n - 1, base, plan)
                    for kind, index in jobs:
                        if kind == both:
                            round_both(index, base, plan)
                if last:
                    invert(n, base + NL, [LEAVING])

            act.wait_ge(s["setup"], 64)
            for blk in range(QB):
                round_both(blk, 0, NEXT)
            send_rows(0, 0, NEXT)
            units(act, body)

        @block.vector
        def _(dve):
            def empty(kind, i, m, mb, left, base, place):
                if kind == both:
                    dve.wait_ge(s["hi_ready"], QB * m + i + 1)
                elif (kind, i) == (den, 0):
                    dve.wait_ge(s["pv_ps"], STEPS * (left + 1))
                    dve.tensor_copy(raw[:, :], ps[:, 6:8, :].rearrange("p b n -> p (b n)")).then_inc(s["raw_ready"], 1)
                elif kind == rows:
                    dve.wait_ge(s["taken"], base + place)
                    dve.tensor_reduce(nmax[:, :], part_max[:, :, :], AX.X, ALU.max, negate=True).then_inc(s["nmax_ready"], 1)
                    wait(dve, s["row_ready"], 64 * m)
                if kind != both:
                    dve.wait_ge(s["job_ps"], base + place + 1)
                bank = ps[:, 3 + place % 3, :]
                if kind == den:
                    op = dve.tensor_copy(dens[:, i * BLK:(i + 1) * BLK], bank)
                elif kind == y_out:
                    c, blk = divmod(i, QB)
                    part = h[:, c, mb * S + blk * BLK:mb * S + (blk + 1) * BLK]
                    op = dve.tensor_tensor(part, part, bank, ALU.add)
                elif kind == both:
                    op = dve.tensor_tensor(qk_lo[:, i, :], bank, qk_hi[:, i, :].bitcast(F32), ALU.subtract)
                elif kind == spread:
                    o, blk = divmod(i, QB)
                    cells = slice(blk * BLK, (blk + 1) * BLK)
                    if i < K0:
                        op = dve.tensor_copy(q_split[:, mb, o, cells], bank)
                    else:
                        for j in range(2):
                            rr = slice(HR * j, HR * j + HR)
                            op = dve.tensor_scalar(k_split[rr, mb, 2 * (o - 2) + j, cells], bank[rr], k_one[rr, 0:1], None,
                                                   ALU.add)
                elif kind == value:
                    kts = VALUES[i]
                    op = dve.tensor_tensor(v_tok[:, mb, kts.start:kts.stop, :],
                                           bank[:, 0:len(kts) * P].rearrange("p (t n) -> p t n", n=P),
                                           ones_at[:, :].unsqueeze(1).broadcast_to([P, len(kts), P]), ALU.add)
                elif kind == piece:
                    op = dve.tensor_reduce(part_max[:, i // QB, i % QB:i % QB + 1], bank, AX.X, ALU.max)
                else:
                    op = dve.tensor_copy(nmax_rows[:, :], bank[0:NH * KT, 0:P])
                op.then_inc(s["taken"], 1)

            def divide(left):
                dve.wait_ge(s["rden_ready"], left + 1)
                dve.wait_ge(s["raw_ready"], left + 1)
                dve.tensor_tensor(heads[:, :], raw[:, :], rden[:, :], ALU.mult).then_inc(s["heads_ready"], 1)

            def body(n, b, first, last):
                base, place = first_job(n, first), 0
                for jobs in jobs_of(first, last):
                    for kind, i in jobs:
                        empty(kind, i, n + 1, 1 - b, n - 1, base, place)
                        place += 1
                        if (kind, i) == (den, 1):
                            divide(n - 1)
                if last:
                    for place, (kind, i) in enumerate(LEAVING):
                        empty(kind, i, None, b, n, base + NL, place)
                        if (kind, i) == (den, 1):
                            divide(n)
                    dve.wait_ge(s["taken"], base + 2 * NL)

            dve.memset(k_split[:, :, :, :].bitcast(F32), 0.0).then_inc(s["zeroed"], 1)
            dve.wait_ge(s["zeroed"], 1)
            dve.wait_ge(s["setup"], 64)
            dve.tensor_copy(place_hi_lo[:, :, :, :], raw[:, :].rearrange("p (o h n) -> p o h n", o=4, h=2)).then_inc(s["zeroed"], 1)
            place = 0
            for jobs in NEXT:
                for kind, i in jobs:
                    empty(kind, i, 0, 0, None, 0, place)
                    place += 1
            units(dve, body)

def align_stage(nc, consts, x, y, ctx, t):
    CK = 16
    W = S // CK
    SLOTS = CTX + CK - 1
    PAD = CK - 1
    ROWS = CTX + 2 * PAD
    LANES = 32 * B
    BIG = 1.0e30

    def dram(name):
        return nc.dram_tensor(f"align_{name}", [B, ROWS, S], F32).ap()

    def skewed(a, b):
        return bass.AP(a.tensor, b * ROWS * S + PAD * W, [[S - W, CK], [S, SLOTS], [1, W]])

    def straight(a, first=0):
        return a[:, PAD + first:PAD + first + CTX, :].rearrange("b r n -> r b n")

    cost_dram, total_dram, path_dram = dram("cost"), dram("total"), dram("path")
    move_dram = [dram(f"move{n}") for n in range(3)]

    def pads(a):
        return [a[:, r:r + PAD, :].rearrange("b r n -> r b n") for r in (0, PAD + CTX)]

    forward = ExitStack()
    ws = Scope(nc, forward, "G0")
    cost_wave = ws.sb("cost", [LANES, SLOTS, W])
    total = ws.sb("total", [LANES, SLOTS + 1, 1 + W])

    with ExitStack() as stack:
        sc = Scope(nc, stack, "G1")
        wave_filled = sc.sem("wave_filled")
        fill = sc.sb("fill", [PAD, 2, B, S])
        ctx_sq, y_sq = sc.sb("ctx_sq", [P, C, B * CTX]), sc.sb("y_sq", [P, C, T])
        norm = sc.sb("norm", [CTX, B])
        sums, dist2, dist = (sc.sb(n, [CTX, 2, BLK]) for n in ("sums", "dist2", "dist"))
        cost = sc.sb("cost", [CTX, T])
        ps = sc.psum()
        names = "filled ctx_squared y_squared norm_ps norm_ready prod_ps sums_ready dist2_ready dist_ready cost_ready stored"
        s = {n: sc.sem(n) for n in names.split()}
        block = stack.enter_context(nc.Block())

        @block.gpsimd
        def _(pool):
            pool.memset(fill[:, 0], BIG).then_inc(s["filled"], 1)
            pool.memset(fill[:, 1], 0.0).then_inc(s["filled"], 1)
            for c in range(C):
                pool.tensor_tensor(ctx_sq[:, c, :], ctx[:, c, :], ctx[:, c, :], ALU.mult).then_inc(s["ctx_squared"], 1)
            pool.memset(cost_wave[:, :, :], BIG).then_inc(wave_filled, 1)
            pool.memset(total[:, :, :], BIG).then_inc(wave_filled, 1)
            pool.wait_ge(wave_filled, 2)

        @block.scalar
        def _(act):
            for n in range(NBLK):
                act.activation(y_sq[:, :, n * BLK:(n + 1) * BLK], y[:, :, n * BLK:(n + 1) * BLK], ACT.Square)\
                   .then_inc(s["y_squared"], 1)
            for n in range(NBLK):
                act.wait_ge(s["dist_ready"], n + 1)
                act.activation(cost[:, n * BLK:(n + 1) * BLK], dist[:, n % 2, :], ACT.Sqrt).then_inc(s["cost_ready"], 1)

        @block.tensor
        def _(pe):
            pe.wait_ge(s["ctx_squared"], C)
            for b in range(B):
                for c in range(C):
                    mm = pe.matmul(ps[0:CTX, 0, b:b + 1], ctx_sq[:, c, b * CTX:(b + 1) * CTX], consts["ones"][:, 0:1],
                                   start=c == 0, stop=c == C - 1)
            mm.then_inc(s["norm_ps"], 1)
            for n in range(NBLK):
                b = n * BLK // S
                if n >= 2:
                    pe.wait_ge(s["dist2_ready"], n - 1)
                pe.wait_ge(s["y_squared"], n + 1)
                for c in range(C):
                    pe.matmul(ps[0:CTX, 2 + n % 2, :], consts["ones"][:, 0:CTX], y_sq[:, c, n * BLK:(n + 1) * BLK],
                              start=c == 0, stop=c == C - 1)
                for c in range(C):
                    mm = pe.matmul(ps[0:CTX, 4 + n % 2, :], ctx[:, c, b * CTX:(b + 1) * CTX], y[:, c, n * BLK:(n + 1) * BLK],
                                   start=c == 0, stop=c == C - 1)
                mm.then_inc(s["prod_ps"], 1)

        @block.vector
        def _(dve):
            dve.wait_ge(s["norm_ps"], 1)
            dve.tensor_copy(norm[:, :], ps[0:CTX, 0, 0:B]).then_inc(s["norm_ready"], 1)
            dve.wait_ge(s["norm_ready"], 1)
            for n in range(NBLK):
                b = n * BLK // S
                dve.wait_ge(s["prod_ps"], n + 1)
                if n >= 2:
                    dve.wait_ge(s["cost_ready"], n - 1)
                dve.tensor_scalar(sums[:, n % 2, :], ps[0:CTX, 2 + n % 2, :], norm[:, b:b + 1], None, ALU.add)\
                   .then_inc(s["sums_ready"], 1)
                dve.wait_ge(s["sums_ready"], n + 1)
                dve.scalar_tensor_tensor(out=dist2[:, n % 2, :], in0=ps[0:CTX, 4 + n % 2, :], scalar=-2.0,
                                         in1=sums[:, n % 2, :], op0=ALU.mult, op1=ALU.add).then_inc(s["dist2_ready"], 1)
                dve.wait_ge(s["dist2_ready"], n + 1)
                dve.tensor_scalar(dist[:, n % 2, :], dist2[:, n % 2, :], 0.0, None, ALU.max).then_inc(s["dist_ready"], 1)

        @block.sync
        def _(sp):
            sp.wait_ge(s["filled"], 2)
            count = 0
            for n, arrays in enumerate(([cost_dram], move_dram)):
                for a in arrays:
                    for dst in pads(a):
                        sp.dma_start(dst, fill[:, n]).then_inc(s["stored"], 16)
                        count += 16
            sp.wait_ge(s["cost_ready"], NBLK)
            sp.dma_start(straight(cost_dram), cost[:, :].rearrange("r (b n) -> r b n", b=B)).then_inc(s["stored"], 16)
            sp.wait_ge(s["stored"], count + 16)

    with ExitStack() as stack:
        sc = Scope(nc, stack, "G2")
        cost = cost_wave
        above = sc.sb("above", [LANES, W])
        loaded, edge_ready, above_ready, row_ready, stored = (
            sc.sem(n) for n in "loaded edge_ready above_ready row_ready stored".split())
        from_left = [min(q + 1, CK) for q in range(CK)] + list(range(CK, 32))
        block = stack.enter_context(nc.Block())

        @block.sync
        def _(sp):
            for b in range(B):
                sp.dma_start(cost[32 * b:32 * b + CK], skewed(cost_dram, b)).then_inc(loaded, 16)
            sp.dma_start(total[:, 0, :], t["G_start"]).then_inc(loaded, 16)
            sp.wait_ge(row_ready, SLOTS)
            for b in range(B):
                sp.dma_start(skewed(total_dram, b), total[32 * b:32 * b + CK, 1:, 1:]).then_inc(stored, 16)
            sp.wait_ge(stored, 32)

        @block.vector
        def _(dve):
            dve.wait_ge(loaded, 48)
            for n in range(SLOTS):
                if n:
                    dve.wait_ge(row_ready, n)
                dve.stream_shuffle(total[:, n + 1, 0:1], total[:, n, W:W + 1], from_left).then_inc(edge_ready, 1)
                dve.tensor_tensor(above[:, :], total[:, n, 1:], total[:, n, 0:W], ALU.min).then_inc(above_ready, 1)
                dve.wait_ge(edge_ready, n + 1)
                dve.wait_ge(above_ready, n + 1)
                dve.tensor_tensor_scan(total[:, n + 1, 1:], above[:, :], cost[:, n, :], initial=total[:, n + 1, 0:1],
                                       op0=ALU.min, op1=ALU.add).then_inc(row_ready, 1)

    forward.close()
    back = ExitStack()
    bs = Scope(nc, back, "Gb")
    move = bs.sb("move", [LANES, 2, SLOTS + 1, W])
    left_moves = bs.sb("left", [LANES, SLOTS, W])
    path_wave = bs.sb("path", [LANES, SLOTS + 1, W + 1])

    with ExitStack() as stack:
        sc = Scope(nc, stack, "G3")
        here, over = sc.sb("here", [CTX, B, 1 + S]), sc.sb("over", [CTX, B, 1 + S])
        least, not_diag = sc.sb("least", [CTX, B, S]), sc.sb("not_diag", [CTX, B, S])
        up = least
        diag, left = (sc.sb(n, [CTX, B, S + 1]) for n in ("diag", "left"))
        filled, back_filled, loaded, dve_step, stored = (
            sc.sem(n) for n in "filled back_filled loaded dve_step stored".split())
        block = stack.enter_context(nc.Block())

        @block.gpsimd
        def _(pool):
            for a in (here, over):
                pool.memset(a[:, :, 0:1], BIG).then_inc(filled, 1)
            pool.memset(over[0:1, :, 1:], BIG).then_inc(filled, 1)
            for a in (diag, left):
                pool.memset(a[:, :, S:S + 1], 0.0).then_inc(filled, 1)
            for a in (move[:, 0], move[:, 1], left_moves[:, :, :], path_wave[:, :, :]):
                pool.memset(a, 0.0).then_inc(back_filled, 1)
            pool.wait_ge(back_filled, 4)
            pool.memset(move[:, 0, SLOTS, :], 1.0).then_inc(back_filled, 1)
            pool.wait_ge(back_filled, 5)

        @block.sync
        def _(sp):
            sp.dma_start(here[:, :, 1:], straight(total_dram)).then_inc(loaded, 16)
            sp.dma_start(over[1:, :, 1:], straight(total_dram)[0:CTX - 1]).then_inc(loaded, 16)
            sp.wait_ge(dve_step, 6)
            for a, dst in ((up[:, :, 0:S], 0), (diag[:, :, 1:], 1), (left[:, :, 1:], 2)):
                sp.dma_start(straight(move_dram[dst]), a).then_inc(stored, 16)
            sp.wait_ge(stored, 48)

        @block.vector
        def _(dve):
            step = chain(dve, dve_step)
            dve.wait_ge(filled, 5)
            dve.wait_ge(loaded, 32)
            c_up, c_diag, c_left = over[:, :, 1:], over[:, :, 0:S], here[:, :, 0:S]
            step(dve.tensor_tensor(least[:, :, :], c_up, c_left, ALU.min))
            step(dve.tensor_tensor(diag[:, :, 0:S], c_diag, least[:, :, :], ALU.is_le))
            step(dve.tensor_tensor(least[:, :, :], c_up, c_left, ALU.is_le))
            step(dve.tensor_scalar(not_diag[:, :, :], diag[:, :, 0:S], -1.0, 1.0, ALU.mult, ALU.add))
            step(dve.tensor_tensor(up[:, :, 0:S], least[:, :, :], not_diag[:, :, :], ALU.mult))
            step(dve.tensor_tensor(left[:, :, 0:S], not_diag[:, :, :], up[:, :, 0:S], ALU.subtract))

    with ExitStack() as stack:
        sc = Scope(nc, stack, "G4")
        left, path = left_moves, path_wave
        below = sc.sb("below", [LANES, 2, W])
        enter = sc.sb("enter", [LANES, W])
        loaded, edge_ready, below_ready, enter_ready, row_ready, stored = (
            sc.sem(n) for n in "loaded edge_ready below_ready enter_ready row_ready stored".split())
        from_right = [CK] + list(range(CK - 1)) + list(range(CK, 32))
        block = stack.enter_context(nc.Block())

        @block.sync
        def _(sp):
            for b in range(B):
                for a, src in zip((move[:, 0], move[:, 1], left), move_dram):
                    sp.dma_start(a[32 * b:32 * b + CK, 0:SLOTS], skewed(src, b)).then_inc(loaded, 16)
            sp.dma_start(path[:, SLOTS, :], t["G_end"]).then_inc(loaded, 16)
            sp.wait_ge(row_ready, SLOTS)
            for b in range(B):
                sp.dma_start(skewed(path_dram, b), path[32 * b:32 * b + CK, 0:SLOTS, 0:W]).then_inc(stored, 16)
            sp.wait_ge(stored, 32)

        @block.vector
        def _(dve):
            dve.wait_ge(loaded, 16 * (3 * B + 1))
            for i, n in enumerate(reversed(range(SLOTS))):
                if i:
                    dve.wait_ge(row_ready, i)
                dve.stream_shuffle(path[:, n, W:W + 1], path[:, n + 1, 0:1], from_right).then_inc(edge_ready, 1)
                row = path[:, n + 1, 0:W]
                cells = bass.AP(row.tensor, row.offset, [list(row.ap[0]), [1, 2], [1, W]])
                dve.tensor_tensor(below[:, :, :], cells, move[:, :, n + 1, :], ALU.mult).then_inc(below_ready, 1)
                dve.wait_ge(below_ready, i + 1)
                dve.tensor_tensor(enter[:, :], below[:, 0, :], below[:, 1, :], ALU.add).then_inc(enter_ready, 1)
                dve.wait_ge(edge_ready, i + 1)
                dve.wait_ge(enter_ready, i + 1)
                dve.tensor_tensor_scan(path[:, n, W - 1::-1], left[:, n, ::-1], enter[:, ::-1],
                                       initial=path[:, n, W:W + 1], op0=ALU.mult, op1=ALU.add).then_inc(row_ready, 1)

    back.close()

    with ExitStack() as stack:
        sc = Scope(nc, stack, "G5")
        path = sc.sb("path", [CTX, B, S])
        ctx_rows = sc.sb("ctx_rows", [CTX, B, D])
        ps = sc.psum()
        loaded, out_ps, x_added = (sc.sem(n) for n in "loaded out_ps x_added".split())
        block = stack.enter_context(nc.Block())

        @block.sync
        def _(sp):
            sp.dma_start(path[:, :, :], straight(path_dram)).then_inc(loaded, 16)
            sp.dma_start(ctx_rows[:, :, :], t["G_ctx_rows"]).then_inc(loaded, 16)

        @block.tensor
        def _(pe):
            pe.wait_ge(loaded, 32)
            for n in range(NBLK):
                b, blk = divmod(n, S // BLK)
                for c in range(C):
                    mm = pe.matmul(ps[:, C * n + c, :], ctx_rows[:, b, c * P:(c + 1) * P], path[:, b, blk * BLK:(blk + 1) * BLK],
                                   start=True, stop=True)
                mm.then_inc(out_ps, 1)

        @block.vector
        def _(dve):
            for n in range(NBLK):
                dve.wait_ge(out_ps, n + 1)
                part = x[:, :, n * BLK:(n + 1) * BLK]
                dve.tensor_tensor(part, part, ps[:, C * n:C * n + C, :], ALU.add).then_inc(x_added, 1)
            dve.wait_ge(x_added, NBLK)


def slots_stage(nc, consts, x, y, t):
    N, PS = 64, 32
    SL = N * PS
    Q = SL // BLK
    TB = S // P
    G = SL // P
    GE = P // PS
    slots_dram = nc.dram_tensor("slots", [B, P, C, SL], F32).ap()
    made_dram = nc.dram_tensor("made", [B, P, G, D], F32).ap()
    with ExitStack() as outer:
        oc = Scope(nc, outer, "H")
        y_tok = oc.sb("y_tok", [P, TILES, D])
        logits = oc.sb("logits", [P, TILES, SL])

        with ExitStack() as stack:
            sc = Scope(nc, stack, "H0")
            ps = sc.psum()
            turned_ps, turned = sc.sem("turned_ps"), sc.sem("turned")
            with nc.Block() as block:
                @block.tensor
                def _(pe):
                    for n in range(TILES // 2):
                        for k in range(2):
                            for c in range(C):
                                tile = 2 * n + k
                                mm = pe.transpose(ps[:, n, k * D + c * P:k * D + (c + 1) * P],
                                                  y[:, c, tile * P:(tile + 1) * P], consts["ident"][:, :])
                        mm.then_inc(turned_ps, 1)

                @block.vector
                def _(dve):
                    for n in range(TILES // 2):
                        dve.wait_ge(turned_ps, n + 1)
                        dve.tensor_copy(y_tok[:, 2 * n:2 * n + 2, :], ps[:, n, :].rearrange("p (k d) -> p k d", k=2))\
                           .then_inc(turned, 1)

        with ExitStack() as stack:
            sc = Scope(nc, stack, "H1")
            phi = sc.sb("phi", [P, 2, C, BLK])
            diff = sc.sb("diff", [P, 2, BLK])
            dispatch = sc.sb("dispatch", [P, 2, B, BLK])
            staged = sc.sb("staged", [P, B, C, BLK])
            ps = sc.psum()
            names = "logits_ps kept0 kept1 diff_ready dispatch_ready slots_ps staged_ready stored"
            s = {n: sc.sem(n) for n in names.split()}
            phi_loaded = [sc.sem(f"phi_loaded{n}") for n in range(2)]
            LAG = 1
            steps = [(q, m) for q in range(Q) for m in range(TB)]
            block = stack.enter_context(nc.Block())

            @block.sync
            def _(sp):
                for q in range(Q):
                    if q >= 2:
                        sp.wait_ge(s["logits_ps"], TB * (q - 1))
                    sp.dma_start(phi[:, q % 2], t["H_phi"][q]).then_inc(phi_loaded[q % 2], 16)
                    if q >= 1:
                        sp.wait_ge(s["staged_ready"], B * q)
                        for b in range(B):
                            sp.dma_start(slots_dram[b][:, :, (q - 1) * BLK:q * BLK], staged[:, b]).then_inc(s["stored"], 16)
                sp.wait_ge(s["staged_ready"], B * Q)
                for b in range(B):
                    sp.dma_start(slots_dram[b][:, :, (Q - 1) * BLK:Q * BLK], staged[:, b]).then_inc(s["stored"], 16)
                sp.wait_ge(s["stored"], 16 * B * Q)

            @block.tensor
            def _(pe):
                def gather(n):
                    q, m = steps[n]
                    pe.wait_ge(s["dispatch_ready"], B * n + B)
                    if m == 0 and q:
                        pe.wait_ge(s["staged_ready"], B * q)
                    for b in range(B):
                        for c in range(C):
                            mm = pe.matmul(ps[:, 4 + C * b + c, :], y_tok[:, b * TB + m, c * P:(c + 1) * P],
                                           dispatch[:, n % 2, b, :], start=m == 0, stop=m == TB - 1)
                    mm.then_inc(s["slots_ps"], 1)

                for n, (q, m) in enumerate(steps):
                    if m == 0:
                        pe.wait_ge(phi_loaded[q % 2], 16 * (q // 2 + 1))
                    if n >= 2:
                        pe.wait_ge(s["kept0"], n - 1)
                        pe.wait_ge(s["kept1"], n - 1)
                    for b in range(B):
                        for c in range(C):
                            mm = pe.matmul(ps[:, 2 * (n % 2) + b, :], y[:, c, (b * TB + m) * P:(b * TB + m + 1) * P],
                                           phi[:, q % 2, c, :], start=c == 0, stop=c == C - 1)
                    mm.then_inc(s["logits_ps"], 1)
                    if n >= LAG:
                        gather(n - LAG)
                gather(len(steps) - 1)

            @block.scalar
            def _(act):
                for n, (q, m) in enumerate(steps):
                    act.wait_ge(s["logits_ps"], n + 1)
                    act.activation(logits[:, m, q * BLK:(q + 1) * BLK], ps[:, 2 * (n % 2), :], ACT.Copy).then_inc(s["kept0"], 1)
                    act.wait_ge(s["diff_ready"], n + 1)
                    if n >= 2:
                        act.wait_ge(s["slots_ps"], n - 1)
                    for b in range(B):
                        act.activation(dispatch[:, n % 2, b, :], diff[:, n % 2, :], ACT.Sigmoid,
                                       scale=1.0 - 2.0 * b).then_inc(s["dispatch_ready"], 1)

            def stage_out(dve, q, b):
                dve.wait_ge(s["slots_ps"], TB * (q + 1))
                if q:
                    dve.wait_ge(s["stored"], 16 * B * q)
                dve.tensor_copy(staged[:, b], ps[:, 4 + C * b:4 + C * b + C, :]).then_inc(s["staged_ready"], 1)

            @block.vector
            def _(dve):
                for n, (q, m) in enumerate(steps):
                    dve.wait_ge(s["logits_ps"], n + 1)
                    dve.tensor_copy(logits[:, TB + m, q * BLK:(q + 1) * BLK], ps[:, 2 * (n % 2) + 1, :]).then_inc(s["kept1"], 1)
                    if m == 0 and q:
                        for b in range(B):
                            stage_out(dve, q - 1, b)
                for b in range(B):
                    stage_out(dve, Q - 1, b)

            @block.gpsimd
            def _(pool):
                for n, (q, m) in enumerate(steps):
                    pool.wait_ge(s["kept0"], n + 1)
                    pool.wait_ge(s["kept1"], n + 1)
                    if n >= 2:
                        pool.wait_ge(s["dispatch_ready"], B * (n - 1))
                    cols = slice(q * BLK, (q + 1) * BLK)
                    pool.tensor_tensor(diff[:, n % 2, :], logits[:, m, cols], logits[:, TB + m, cols],
                                       ALU.subtract).then_inc(s["diff_ready"], 1)

        assert G == TILES
        slots = [y[:, :, :], y_tok[:, :, :].rearrange("p t d -> p (t d)").rearrange("p (c n) -> p c n", c=C)]
        with ExitStack() as stack:
            sc = Scope(nc, stack, "H2")
            RING = 2
            w = sc.sb("w", [P, RING, GE, C, D])
            bias = sc.sb("bias", [P, 2, D])
            made = sc.sb("made", [P, 2, B, D])
            nmax, total, share = (sc.sb(n, [P, TILES]) for n in ("nmax", "total", "share"))
            ps = sc.psum()
            names = """slots_loaded experts_ps made_ready max_ready exp_ready share_ready combine_ready
                       turned_ps turned_a turned_b"""
            s = {n: sc.sem(n) for n in names.split()}
            w_loaded = [sc.sem(f"w_loaded{n}") for n in range(RING)]
            bias_loaded = [sc.sem(f"bias_loaded{n}") for n in range(2)]
            stored = [sc.sem(f"stored{n}") for n in range(2)]
            block = stack.enter_context(nc.Block())

            @block.sync
            def _(sp):
                for b in range(B):
                    sp.dma_start(slots[b], slots_dram[b]).then_inc(s["slots_loaded"], 16)
                for g in range(G):
                    if g >= RING:
                        sp.wait_ge(s["experts_ps"], g - RING + 1)
                    sp.dma_start(w[:, g % RING], t["H_w"][g]).then_inc(w_loaded[g % RING], 16)

            def store(pool, g):
                pool.wait_ge(s["made_ready"], g + 1)
                pool.dma_start(made_dram[:, :, g, :].rearrange("b p d -> p b d"), made[:, g % 2]).then_inc(stored[g % 2], 16)

            @block.gpsimd
            def _(pool):
                for g in range(G):
                    if g >= 2:
                        pool.wait_ge(s["made_ready"], g - 1)
                    pool.dma_start(bias[:, g % 2, :], t["H_b"][g]).then_inc(bias_loaded[g % 2], 16)
                    if g:
                        store(pool, g - 1)
                store(pool, G - 1)
                for n in range(2):
                    pool.wait_ge(stored[n], 16 * G // 2)

            @block.tensor
            def _(pe):
                pe.wait_ge(s["slots_loaded"], 16 * B)
                for g in range(G):
                    pe.wait_ge(w_loaded[g % RING], 16 * (g // RING + 1))
                    if g >= 2:
                        pe.wait_ge(s["made_ready"], g - 1)
                    for b in range(B):
                        for c in range(C):
                            for i in range(GE):
                                n = GE * g + i
                                mm = pe.matmul(ps[PS * i:PS * i + PS, 2 * (g % 2) + b, 0:D], slots[b][:, c, n * PS:(n + 1) * PS],
                                               w[:, g % RING, i, c, :], start=c == 0, stop=c == C - 1)
                    mm.then_inc(s["experts_ps"], 1)
                    pe.wait_ge(s["combine_ready"], g + 1)
                    if g:
                        pe.wait_ge(s["turned_a"], g)
                        pe.wait_ge(s["turned_b"], g)
                    for k in range(G):
                        mm = pe.transpose(ps[:, 4 + k // 4, (k % 4) * P:(k % 4 + 1) * P], logits[:, g, k * P:(k + 1) * P],
                                          consts["ident"][:, :])
                    mm.then_inc(s["turned_ps"], 1)

            @block.vector
            def _(dve):
                def maximum(n):
                    dve.tensor_reduce(nmax[:, n:n + 1], logits[:, n, :], AX.X, ALU.max, negate=True).then_inc(s["max_ready"], 1)

                def normalise(n):
                    dve.wait_ge(s["exp_ready"], n + 1)
                    dve.reciprocal(share[:, n:n + 1], total[:, n:n + 1]).then_inc(s["share_ready"], 1)
                    dve.wait_ge(s["share_ready"], n + 1)
                    dve.tensor_scalar(logits[:, n, :], logits[:, n, :], share[:, n:n + 1], None, ALU.mult)\
                       .then_inc(s["combine_ready"], 1)

                maximum(0)
                maximum(1)
                normalise(0)
                for g in range(G):
                    if g + 2 < G:
                        maximum(g + 2)
                    if g + 1 < G:
                        normalise(g + 1)
                    dve.wait_ge(s["experts_ps"], g + 1)
                    dve.wait_ge(bias_loaded[g % 2], 16 * (g // 2 + 1))
                    if g >= 2:
                        dve.wait_ge(stored[g % 2], 16 * (g // 2))
                    dve.tensor_tensor(made[:, g % 2], ps[:, 2 * (g % 2):2 * (g % 2) + 2, 0:D],
                                      bias[:, g % 2, :].unsqueeze(1).broadcast_to([P, B, D]), ALU.add).then_inc(s["made_ready"], 1)
                    dve.wait_ge(s["turned_ps"], g + 1)
                    dve.tensor_copy(logits[:, g, SL // 2:], ps[:, 6:8, :].rearrange("p b n -> p (b n)")).then_inc(s["turned_b"], 1)

            @block.scalar
            def _(act):
                def exp(n):
                    act.wait_ge(s["max_ready"], n + 1)
                    act.activation(logits[:, n, :], logits[:, n, :], ACT.Exp, bias=nmax[:, n:n + 1],
                                   accum_out=total[:, n:n + 1]).then_inc(s["exp_ready"], 1)

                exp(0)
                exp(1)
                for g in range(G):
                    if g + 2 < G:
                        exp(g + 2)
                    act.wait_ge(s["turned_ps"], g + 1)
                    act.activation(logits[:, g, 0:SL // 2], ps[:, 4:6, :].rearrange("p b n -> p (b n)"), ACT.Copy)\
                       .then_inc(s["turned_a"], 1)

        outs = [y[:, :, :].rearrange("p c n -> p (c n)").rearrange("p (g d) -> p g d", d=D), y_tok[:, :, :]]
        with ExitStack() as stack:
            sc = Scope(nc, stack, "H3")
            ps = sc.psum()
            out_ps, x_added = sc.sem("out_ps"), sc.sem("x_added")
            made_loaded = [sc.sem(f"made_loaded{b}") for b in range(B)]
            BT = BLK // P
            block = stack.enter_context(nc.Block())

            @block.sync
            def _(sp):
                for b in range(B):
                    sp.dma_start(outs[b], made_dram[b]).then_inc(made_loaded[b], 16)

            @block.tensor
            def _(pe):
                for blk in range(NBLK):
                    b = blk * BLK // S
                    pe.wait_ge(made_loaded[b], 16)
                    for c in range(C):
                        for g in range(G):
                            mm = pe.matmul(ps[:, C * blk + c, :], outs[b][:, g, c * P:(c + 1) * P],
                                           logits[:, BT * blk:BT * blk + BT, g * P:(g + 1) * P], start=g == 0, stop=g == G - 1)
                        mm.then_inc(out_ps, 1)

            @block.vector
            def _(dve):
                for n in range(NBLK * C):
                    blk, c = divmod(n, C)
                    dve.wait_ge(out_ps, n + 1)
                    part = x[:, c, blk * BLK:(blk + 1) * BLK]
                    dve.tensor_tensor(part, part, ps[:, n, :], ALU.add).then_inc(x_added, 1)
                dve.wait_ge(x_added, NBLK * C)

def program(nc, t, out):
    t = dict(t)
    for name in "BDF":
        t["scratch_gates_" + name] = nc.dram_tensor(f"gates_{name}", [E, T], F32).ap()
    with ExitStack() as stack:
        sc = Scope(nc, stack, "g")
        x = sc.sb("x", [P, C, T])
        y = sc.sb("y", [P, C, T])
        ctx = sc.sb("ctx", [P, C, B * CTX])
        names = ["mean", "ident", "ones"]
        consts = {n: sc.sb(n, [P, P]) for n in names}
        consts["eps"] = sc.sb("eps", [P, 1])
        load_stage(nc, "load", [(x[:, :, :], t["x"]), (ctx[:, :, :], t["ctx"]), (consts["eps"][:, :], t["c_eps"])]
                   + [(consts[n][:, :], t["c_" + n]) for n in names])
        with ExitStack() as layer:
            ls = Scope(nc, layer, "A0")
            ctx_n = ls.sb("ctx_n", [P, C, B * CTX])
            lnw = {k: ls.sb(k, [P, C]) for k in ("ln1_w", "ln1_b", "ln2_w", "ln2_b")}
            load_stage(nc, "loadA", [(v[:, :], t["L0_xattn_" + k]) for k, v in lnw.items()])
            norm_stage(nc, "nA1", consts, norm_jobs(x, y))
            norm_stage(nc, "nA2", consts, norm_jobs(y, y, scale=lnw["ln2_w"], shift=lnw["ln2_b"])
                       + [(ctx, ctx_n, 0, B * CTX, lnw["ln1_w"], lnw["ln1_b"])])
            latent_attention(nc, consts, x, y, ctx_n, t["A_wqkv"], t["A_wo"])
        norm_stage(nc, "nB", consts, norm_jobs(x, y))
        moe(nc, "B", "top1", ACT.Gelu, D, consts, x, y, t, [])
        norm_stage(nc, "nC", consts, norm_jobs(x, y))
        context_attention(nc, "C", consts, x, y, ctx, t)
        norm_stage(nc, "nD", consts, norm_jobs(x, y))
        moe(nc, "D", "sinkhorn", ACT.Relu, 2 * D, consts, x, y, t, [y])
        norm_stage(nc, "nE", consts, norm_jobs(x, y))
        context_attention(nc, "E", consts, x, y, ctx, t)
        norm_stage(nc, "nF", consts, norm_jobs(x, y))
        with ExitStack() as layer:
            ls = Scope(nc, layer, "F0")
            r = ls.sb("r", [P, C, T])
            lnw = {k: ls.sb(k, [P, C]) for k in ("ln1_w", "ln2_w")}
            load_stage(nc, "loadF", [(v[:, :], t["F_" + k]) for k, v in lnw.items()])
            norm_stage(nc, "nF1", consts, norm_jobs(y, r, scale=lnw["ln1_w"]), rms=True)
            self_attention(nc, consts, y, r, t)
            norm_stage(nc, "nF2", consts, norm_jobs(y, r, scale=lnw["ln2_w"]), rms=True)
            moe(nc, "F", "top2", ACT.Silu, 2 * D, consts, x, r, t, [y])
        norm_stage(nc, "nG", consts, norm_jobs(x, y))
        align_stage(nc, consts, x, y, ctx, t)
        norm_stage(nc, "nH", consts, norm_jobs(x, y))
        slots_stage(nc, consts, x, y, t)
        with ExitStack() as last:
            stored = Scope(nc, last, "out").sem("stored")
            with nc.Block() as block:
                @block.sync
                def _(sp):
                    sp.dma_start(out, x[:, :, :]).then_inc(stored, 16)
                    sp.wait_ge(stored, 16)


def lay_out(np, i):
    def feat(a):
        return a.T.reshape(-1, P, a.shape[0]).transpose(1, 0, 2)

    def rows(w):
        return w.reshape(-1, P, w.shape[-1]).transpose(1, 0, 2)

    def column(v):
        return v.reshape(-1, P).T

    def everywhere(v):
        return np.broadcast_to(v, (P,) + v.shape)

    def experts(name, w_in, w_out):
        w = np.stack(w_in, axis=1)
        t[name + "_w_in"] = w.reshape(E, len(w_in), C, P, -1).transpose(0, 3, 1, 2, 4)
        t[name + "_w_out"] = w_out.reshape(E, -1, P, D).transpose(0, 2, 1, 3)

    t = {"x": feat(i["x"].reshape(T, D)), "ctx": feat(i["ctx_1024"].reshape(B * CTX, D)),
         "c_mean": np.full((P, P), 1.0 / D, np.float32), "c_ident": np.eye(P, dtype=np.float32),
         "c_ones": np.ones((P, P), np.float32), "c_eps": np.full((P, 1), EPS, np.float32),
         "c_order": everywhere(np.arange(E, 0, -1, dtype=np.float32))}
    for k in ("ln1_w", "ln1_b", "ln2_w", "ln2_b"):
        t["L0_xattn_" + k] = column(i["L0_xattn_" + k])
    wq, wkv = i["L0_xattn_Wq"], i["L0_xattn_Wkv"]
    stacked = np.stack([wq, wkv[:, :1024], wkv[:, 1024:]])
    t["A_wqkv"] = stacked.reshape(3, C, P, 8, P).transpose(3, 2, 0, 1, 4)
    t["A_wo"] = i["L0_xattn_Wo"].reshape(8, P, D)
    experts("B", [i["L0_ffn_W1"]], i["L0_ffn_W2"])
    t["B_router_w"], t["B_router_b"] = rows(i["L0_ffn_Wg"]), everywhere(i["L0_ffn_bg"])
    t["B_b_in"] = i["L0_ffn_b1"].reshape(E, C, P).transpose(0, 2, 1)
    t["B_b_out"] = i["L0_ffn_b2"]
    experts("D", [i["L1_ffn_wg"], i["L1_ffn_wp"]], i["L1_ffn_wo"])
    t["D_router_w"], t["D_router_b"] = rows(i["L1_ffn_router_w"].T), everywhere(i["L1_ffn_router_b"])
    t["D_temperature"] = everywhere(i["L1_ffn_temperature"])
    t["F_ln1_w"], t["F_ln2_w"] = column(i["L2_ffn_ln1_w"]), column(i["L2_ffn_ln2_w"])
    experts("F", [i["L2_ffn_w1"].transpose(0, 2, 1), i["L2_ffn_w3"].transpose(0, 2, 1)], i["L2_ffn_w2"].transpose(0, 2, 1))
    t["F_router_w"] = rows(i["L2_ffn_gate_w"].T)
    t["c_head_mask"] = np.repeat(np.eye(8, dtype=np.float32), 16, axis=0)
    wkv, bkv = i["L1_xattn_Wkv"], i["L1_xattn_bkv"]
    for name, ws in (("C", (i["L1_xattn_Wq"], wkv[:D], wkv[D:], i["L1_xattn_Wo"])),
                     ("E", [i["L2_xattn_" + k] for k in ("wq", "wk", "wv", "wo")])):
        for k, w in zip(("wq", "wk", "wv", "wo"), ws):
            t[f"{name}_{k}"] = rows(w.T)
    for name, bs in (("C", (i["L1_xattn_bq"], bkv[:D], bkv[D:], i["L1_xattn_bo"])),
                     ("E", [i["L2_xattn_" + k] for k in ("bq", "bk", "bv", "bo")])):
        for k, b in zip(("bq", "bk", "bv", "bo"), bs):
            t[f"{name}_{k}"] = column(b)
    hi_hi, lo_hi, hi_lo, aux = 0, 16, 48, 32

    v = np.zeros((4, 4, 32, D), np.float32)
    v[:, :, :16] = i["L2_ffn_wv"].reshape(4, 4, 16, D)
    wo = np.zeros((4, 4, 32, D), np.float32)
    wo[:, :, :16] = i["L2_ffn_wo"].T.reshape(4, 4, 16, D)
    qk = np.concatenate([i["L2_ffn_wq"].reshape(4, 64, D), i["L2_ffn_wk"].reshape(4, 64, D)], 1)
    w_in = np.stack([qk, v.reshape(4, P, D)], 1).transpose(0, 1, 3, 2)
    t["F1_w_in"] = w_in.reshape(4, 2, C, P, P).transpose(0, 3, 1, 2, 4)
    t["F1_w_out"] = wo.reshape(4, P, D)
    place = np.zeros((P, 4, 2, P), np.float32)
    for o in range(4):
        pair, is_k = o % 2, o // 2
        for head in range(2):
            for d in range(16):
                feature, row = 64 * is_k + 16 * (2 * pair + head) + d, 64 * head + d
                place[feature, o, 0, row + hi_hi] = 1
                place[feature, o, 1 if is_k else 0, row + lo_hi] = 1
                place[feature, o, 0 if is_k else 1, row + hi_lo] = 1
    t["F1_place"] = place.reshape(P, -1)
    k_one = np.zeros((2, 64, 1), np.float32)
    k_one[:, aux] = 1
    t["F1_k_one"] = k_one.reshape(P, 1)
    t["F1_ones_at"] = everywhere(np.tile(np.repeat(np.array([0, 1], np.float32), 16), 4))
    den = np.zeros((4, 32, 4, 32), np.float32)
    for hd in range(4):
        den[hd, 16, hd, :] = 1
    t["F1_den_to"] = den.reshape(P, P)
    start = np.full((2, 32, 65), 1.0e30, np.float32)
    start[:, 15, 0] = 0
    end = np.zeros((2, 32, 65), np.float32)
    end[:, 0, 63] = 1
    t["G_start"], t["G_end"] = start.reshape(64, 65), end.reshape(64, 65)
    t["G_ctx_rows"] = i["ctx_1024"].transpose(1, 0, 2)
    t["H_phi"] = rows(i["L3_ffn_phi"].reshape(D, 2048)).reshape(P, C, 4, BLK).transpose(2, 0, 1, 3)
    t["H_w"] = i["L3_ffn_W"].reshape(16, 4, C, P, D).transpose(0, 3, 1, 2, 4)
    t["H_b"] = np.repeat(i["L3_ffn_b"], 32, axis=0).reshape(16, P, D)
    return {k: np.ascontiguousarray(v) for k, v in t.items()}


def kernel(**inputs):
    import numpy as np
    import concourse.bacc as bacc
    from concourse.bass_utils import run_bass_kernel_spmd as run

    nc = bacc.Bacc("TRN2", target_bir_lowering=False, num_devices=1)
    arrays = lay_out(np, {k: np.asarray(v) for k, v in inputs.items()})
    aps = {k: nc.dram_tensor(f"in_{k}", v.shape, mybir.dt.from_np(v.dtype), kind="ExternalInput").ap()
           for k, v in arrays.items()}
    out = nc.dram_tensor("out", [P, C, T], F32, kind="ExternalOutput").ap()
    program(nc, aps, out)
    got = run(nc, [{f"in_{k}": v for k, v in arrays.items()}], core_ids=[0]).results[0]["out"]
    return got.transpose(1, 0, 2).reshape(D, T).T.reshape(B, S, D)
```
